# Optimizing a Trainium2 kernel written in Bass

```python
import numpy as np
import jax
import jax.numpy as jnp

def _softmax(x, axis=-1):
    return jax.nn.softmax(x, axis=axis)

def _gelu(x):
    return jax.nn.gelu(x, approximate=True)

def _silu(x):
    return jax.nn.silu(x)

def _sigmoid(x):
    return jax.nn.sigmoid(x)

def _layernorm(x, axis=-1, eps=1e-05):
    m = jnp.mean(x, axis=axis, keepdims=True)
    v = jnp.var(x, axis=axis, keepdims=True)
    return (x - m) / jnp.sqrt(v + eps)

def _scatter_add(tgt, idx, src, axis=0):
    return tgt.at[idx].add(src)

def _segment_sum(src, seg, n):
    return jax.ops.segment_sum(src, seg, n)
kernel_name = 'mk_prb_d2_jaxref_r4_d1597b'

def setup_inputs(seed: int=0):
    np.random.seed(seed)
    _w = jnp.asarray

    def _L0_attn_setup():
        import jax, jax.numpy as jnp
        import numpy as np
        H, EXP, N, CONV = (256, 2, 16, 4)
        INNER = H * EXP
        DTR = max(H // 16, 1)
        BATCH, SEQ = (2, 256)

        def _forward(x, norm_w, norm_b, in_w, in_b, conv_w, conv_b, bc_w, bc_b, dtr_w, dtr_b, dt_w, dt_b, out_w, out_b):
            B, L, _ = x.shape
            mu = x.mean(-1, keepdims=True)
            var = ((x - mu) ** 2).mean(-1, keepdims=True)
            normed = (x - mu) * jax.lax.rsqrt(var + 1e-05) * norm_w + norm_b
            xz = normed @ in_w + in_b
            xb, z = (xz[..., :INNER], xz[..., INNER:])
            xp = jnp.pad(xb, ((0, 0), (CONV - 1, 0), (0, 0)))
            xc = sum((xp[:, k:k + L, :] * conv_w[:, k] for k in range(CONV))) + conv_b
            xa = jax.nn.silu(xc)
            bc = xa @ bc_w + bc_b
            Bm, Cm = (bc[..., :N], bc[..., N:])
            dt = jax.nn.softplus((xa @ dtr_w + dtr_b) @ dt_w + dt_b)
            dt = jnp.clip(dt, 0.001, 0.1)
            a_diag = -(jnp.arange(N, dtype=jnp.float32) + 1.0)
            a_bar = jnp.exp(dt[..., None] * a_diag)
            dt_mean = dt.mean(axis=2, keepdims=True)[..., None]
            bx = dt_mean * Bm[:, :, None, :] * xa[..., None]

            def step(h, ts):
                a_t, bx_t, c_t = ts
                h = a_t * h + bx_t
                y = jnp.einsum('bdn,bn->bd', h, c_t)
                return (h, y)
            h0 = jnp.zeros((B, INNER, N), x.dtype)
            _, ys = jax.lax.scan(step, h0, (a_bar.transpose(1, 0, 2, 3), bx.transpose(1, 0, 2, 3), Cm.transpose(1, 0, 2)))
            ssm_out = ys.transpose(1, 0, 2)
            gated = ssm_out * jax.nn.silu(z)
            return gated @ out_w + out_b
        key = jax.random.key(seed)
        ks = jax.random.split(key, 16)
        g = lambda k, shape, s=0.02: jax.random.normal(k, shape, dtype=jnp.float32) * s
        return {'x': jax.random.normal(ks[0], (BATCH, SEQ, H), dtype=jnp.float32), 'norm_w': jnp.ones((H,), jnp.float32), 'norm_b': jnp.zeros((H,), jnp.float32), 'in_w': g(ks[1], (H, 2 * INNER)), 'in_b': jnp.zeros((2 * INNER,), jnp.float32), 'conv_w': g(ks[2], (INNER, CONV), 0.1), 'conv_b': jnp.zeros((INNER,), jnp.float32), 'bc_w': g(ks[3], (INNER, 2 * N)), 'bc_b': jnp.zeros((2 * N,), jnp.float32), 'dtr_w': g(ks[4], (INNER, DTR)), 'dtr_b': jnp.zeros((DTR,), jnp.float32), 'dt_w': g(ks[5], (DTR, INNER)), 'dt_b': jnp.zeros((INNER,), jnp.float32), 'out_w': g(ks[6], (INNER, H)), 'out_b': jnp.zeros((H,), jnp.float32)}
    _L0_attn_in = _L0_attn_setup()

    def _L0_ffn_setup():
        import jax, jax.numpy as jnp
        import numpy as np
        DIM = 256
        DEPTH = 2
        HEADS = 8
        DIM_HEAD = 64
        WINDOW = 128
        INNER = HEADS * DIM_HEAD
        HID = int(DIM * 4 * 2 / 3)
        B, N = (2, 2048)
        QK_SCALE = 8.0

        def shift_token(t):
            t1, t2 = jnp.split(t, 2, axis=-1)
            t2 = jnp.pad(t2, ((0, 0), (1, 0), (0, 0)))[:, :-1]
            return jnp.concatenate([t1, t2], axis=-1)

        def l2norm(t):
            return t / jnp.clip(jnp.linalg.norm(t, axis=-1, keepdims=True), 1e-12)

        def rotate_half(x):
            x1, x2 = jnp.split(x, 2, axis=-1)
            return jnp.concatenate([-x2, x1], axis=-1)

        def rotary_xpos(q, k):
            n = q.shape[-2]
            half_idx = jnp.arange(0, DIM_HEAD, 2, dtype=jnp.float32)
            inv_freq = 1.0 / 10000.0 ** (half_idx / DIM_HEAD)
            t = jnp.arange(n, dtype=jnp.float32)
            freqs = t[:, None] * inv_freq[None, :]
            freqs = jnp.concatenate([freqs, freqs], axis=-1)
            base = (half_idx + 0.4 * DIM_HEAD) / (1.4 * DIM_HEAD)
            power = (t - n // 2) / float(WINDOW // 2)
            scale = base[None, :] ** power[:, None]
            scale = jnp.concatenate([scale, scale], axis=-1)
            cos, sin = (jnp.cos(freqs), jnp.sin(freqs))
            q = q * cos * scale + rotate_half(q) * sin * scale
            k = k * cos / scale + rotate_half(k) * sin / scale
            return (q, k)

        def local_attention(q, k, v):
            b, h, n, d = q.shape
            w = n // WINDOW
            bq = q.reshape(b, h, w, WINDOW, d) * QK_SCALE
            bk = k.reshape(b, h, w, WINDOW, d)
            bv = v.reshape(b, h, w, WINDOW, d)

            def look_around(t):
                p = jnp.pad(t, ((0, 0), (0, 0), (1, 0), (0, 0), (0, 0)))
                return jnp.concatenate([p[:, :, :w], p[:, :, 1:]], axis=3)
            bk, bv = (look_around(bk), look_around(bv))
            bt = jnp.arange(n).reshape(w, WINDOW)
            btp = jnp.pad(bt, ((1, 0), (0, 0)), constant_values=-1)
            btk = jnp.concatenate([btp[:w], btp[1:]], axis=1)
            sim = jnp.einsum('bhwid,bhwjd->bhwij', bq, bk)
            i = bt[:, :, None]
            j = btk[:, None, :]
            mask = (i < j) | (i > j + WINDOW) | (j == -1)
            sim = jnp.where(mask, -jnp.finfo(sim.dtype).max, sim)
            attn = jax.nn.softmax(sim, axis=-1)
            out = jnp.einsum('bhwij,bhwjd->bhwid', attn, bv)
            return out.reshape(b, h, n, d)

        def _layer(x, wqkv, qs, ksc, wo, lg, lb, w1, b1, w2, b2):
            b, n, _ = x.shape
            h = shift_token(x)
            qkv = h @ wqkv
            q, k, v = jnp.split(qkv, 3, axis=-1)
            to_heads = lambda t: t.reshape(b, n, HEADS, DIM_HEAD).transpose(0, 2, 1, 3)
            q, k, v = (to_heads(q), to_heads(k), to_heads(v))
            q = l2norm(q) * qs
            k = l2norm(k) * ksc
            q, k = rotary_xpos(q, k)
            o = local_attention(q, k, v)
            o = o.transpose(0, 2, 1, 3).reshape(b, n, INNER)
            x = x + o @ wo
            h = shift_token(x)
            mu = h.mean(-1, keepdims=True)
            var = h.var(-1, keepdims=True)
            h = (h - mu) / jnp.sqrt(var + 1e-05) * lg + lb
            h = h @ w1 + b1
            a, g = jnp.split(h, 2, axis=-1)
            h = a * jax.nn.gelu(g, approximate=False)
            x = x + h @ w2 + b2
            return x
        key = jax.random.key(seed)
        ks = jax.random.split(key, 6)
        return {'x': jax.random.normal(ks[0], (B, N, DIM), jnp.float32), 'wqkv': jax.random.normal(ks[1], (DEPTH, DIM, 3 * INNER), jnp.float32) * 0.02, 'q_scale': jnp.ones((DEPTH, DIM_HEAD), jnp.float32), 'k_scale': jnp.ones((DEPTH, DIM_HEAD), jnp.float32), 'wo': jax.random.normal(ks[2], (DEPTH, INNER, DIM), jnp.float32) * 0.02, 'ln_g': jnp.ones((DEPTH, DIM), jnp.float32), 'ln_b': jnp.zeros((DEPTH, DIM), jnp.float32), 'w1': jax.random.normal(ks[3], (DEPTH, DIM, 2 * HID), jnp.float32) * 0.02, 'b1': jnp.zeros((DEPTH, 2 * HID), jnp.float32), 'w2': jax.random.normal(ks[4], (DEPTH, HID, DIM), jnp.float32) * 0.02, 'b2': jnp.zeros((DEPTH, DIM), jnp.float32)}
    _L0_ffn_in = _L0_ffn_setup()

    def _L1_attn_setup():
        import jax, jax.numpy as jnp
        import numpy as np
        B, S, HID = (2, 512, 256)
        H, D = (16, 64)
        KD = H * D
        RMS_EPS = 1e-05
        L2_EPS = 1e-12

        def _l2norm(t):
            n = jnp.sqrt(jnp.sum(t * t, axis=-1, keepdims=True))
            return t / jnp.clip(n, L2_EPS)
        key = jax.random.key(seed)
        ks = jax.random.split(key, 9)
        w = lambda k, shape: jax.random.normal(k, shape, jnp.float32) * 0.02
        return {'x': jax.random.normal(ks[0], (B, S, HID), jnp.float32), 'Wq': w(ks[1], (HID, KD)), 'Wk': w(ks[2], (HID, KD)), 'Wv': w(ks[3], (HID, KD)), 'Wf': w(ks[4], (HID, KD)), 'Wb': w(ks[5], (HID, H)), 'A_log': jnp.log(jnp.full((H,), 8.0, jnp.float32)), 'dt_bias': jnp.zeros((KD,), jnp.float32), 'Wg': w(ks[6], (HID, KD)), 'bg': jnp.zeros((KD,), jnp.float32), 'Wo': w(ks[7], (KD, HID)), 'norm_w': jnp.ones((D,), jnp.float32)}
    _L1_attn_in = _L1_attn_setup()

    def _L1_ffn_setup():
        import jax, jax.numpy as jnp
        import numpy as np
        TAU = 10.0
        EPS = 1e-06
        TOP_K = 8

        def _layernorm(x, g, b):
            mu = jnp.mean(x, axis=-1, keepdims=True)
            var = jnp.var(x, axis=-1, keepdims=True)
            return (x - mu) * jax.lax.rsqrt(var + 1e-05) * g + b

        def _unit_rows(W):
            n = jnp.linalg.norm(W, axis=1, keepdims=True)
            return W / jnp.maximum(n, EPS)
        key = jax.random.key(seed)
        ks = jax.random.split(key, 5)
        D, NB, H = (256, 128, 1024)
        B, S = (4, 512)
        x = jax.random.normal(ks[0], (B, S, D), dtype=jnp.float32)
        W1 = jax.random.normal(ks[1], (H, D), dtype=jnp.float32) * (1.0 / np.sqrt(D))
        W2 = jax.random.normal(ks[2], (D, H), dtype=jnp.float32) * (1.0 / np.sqrt(H))
        ln_g = jnp.ones((D,), jnp.float32)
        ln_b = jnp.zeros((D,), jnp.float32)
        router_W = jax.random.normal(ks[3], (NB, D), dtype=jnp.float32) * 0.01
        router_b = jnp.zeros((NB,), jnp.float32)
        raw_U = jax.random.normal(ks[4], (NB, D), dtype=jnp.float32) * 0.02
        raw_V = jax.random.normal(jax.random.fold_in(key, 7), (NB, D), dtype=jnp.float32) * 0.02
        gamma = jnp.ones((1, 1, D), jnp.float32) * 0.1
        return {'x': x, 'W1': W1, 'W2': W2, 'ln_g': ln_g, 'ln_b': ln_b, 'router_W': router_W, 'router_b': router_b, 'raw_U': raw_U, 'raw_V': raw_V, 'gamma': gamma}
    _L1_ffn_in = _L1_ffn_setup()
    _d = {'L0_attn_x': _L0_attn_in['x'], 'L0_attn_norm_w': _L0_attn_in['norm_w'], 'L0_attn_norm_b': _L0_attn_in['norm_b'], 'L0_attn_in_w': _L0_attn_in['in_w'], 'L0_attn_in_b': _L0_attn_in['in_b'], 'L0_attn_conv_w': _L0_attn_in['conv_w'], 'L0_attn_conv_b': _L0_attn_in['conv_b'], 'L0_attn_bc_w': _L0_attn_in['bc_w'], 'L0_attn_bc_b': _L0_attn_in['bc_b'], 'L0_attn_dtr_w': _L0_attn_in['dtr_w'], 'L0_attn_dtr_b': _L0_attn_in['dtr_b'], 'L0_attn_dt_w': _L0_attn_in['dt_w'], 'L0_attn_dt_b': _L0_attn_in['dt_b'], 'L0_attn_out_w': _L0_attn_in['out_w'], 'L0_attn_out_b': _L0_attn_in['out_b'], 'L0_ffn_wqkv': _L0_ffn_in['wqkv'], 'L0_ffn_q_scale': _L0_ffn_in['q_scale'], 'L0_ffn_k_scale': _L0_ffn_in['k_scale'], 'L0_ffn_wo': _L0_ffn_in['wo'], 'L0_ffn_ln_g': _L0_ffn_in['ln_g'], 'L0_ffn_ln_b': _L0_ffn_in['ln_b'], 'L0_ffn_w1': _L0_ffn_in['w1'], 'L0_ffn_b1': _L0_ffn_in['b1'], 'L0_ffn_w2': _L0_ffn_in['w2'], 'L0_ffn_b2': _L0_ffn_in['b2'], 'L1_attn_Wq': _L1_attn_in['Wq'], 'L1_attn_Wk': _L1_attn_in['Wk'], 'L1_attn_Wv': _L1_attn_in['Wv'], 'L1_attn_Wf': _L1_attn_in['Wf'], 'L1_attn_Wb': _L1_attn_in['Wb'], 'L1_attn_A_log': _L1_attn_in['A_log'], 'L1_attn_dt_bias': _L1_attn_in['dt_bias'], 'L1_attn_Wg': _L1_attn_in['Wg'], 'L1_attn_bg': _L1_attn_in['bg'], 'L1_attn_Wo': _L1_attn_in['Wo'], 'L1_attn_norm_w': _L1_attn_in['norm_w'], 'L1_ffn_W1': _L1_ffn_in['W1'], 'L1_ffn_W2': _L1_ffn_in['W2'], 'L1_ffn_ln_g': _L1_ffn_in['ln_g'], 'L1_ffn_ln_b': _L1_ffn_in['ln_b'], 'L1_ffn_router_W': _L1_ffn_in['router_W'], 'L1_ffn_router_b': _L1_ffn_in['router_b'], 'L1_ffn_raw_U': _L1_ffn_in['raw_U'], 'L1_ffn_raw_V': _L1_ffn_in['raw_V'], 'L1_ffn_gamma': _L1_ffn_in['gamma']}
    _x0 = _d['L0_attn_x']
    _d['L0_attn_x'] = jax.random.normal(jax.random.fold_in(jax.random.key(seed), 1), (8, 512, 256), dtype=_x0.dtype)
    del _x0
    return _d

def reference(L0_attn_x, L0_attn_norm_w, L0_attn_norm_b, L0_attn_in_w, L0_attn_in_b, L0_attn_conv_w, L0_attn_conv_b, L0_attn_bc_w, L0_attn_bc_b, L0_attn_dtr_w, L0_attn_dtr_b, L0_attn_dt_w, L0_attn_dt_b, L0_attn_out_w, L0_attn_out_b, L0_ffn_wqkv, L0_ffn_q_scale, L0_ffn_k_scale, L0_ffn_wo, L0_ffn_ln_g, L0_ffn_ln_b, L0_ffn_w1, L0_ffn_b1, L0_ffn_w2, L0_ffn_b2, L1_attn_Wq, L1_attn_Wk, L1_attn_Wv, L1_attn_Wf, L1_attn_Wb, L1_attn_A_log, L1_attn_dt_bias, L1_attn_Wg, L1_attn_bg, L1_attn_Wo, L1_attn_norm_w, L1_ffn_W1, L1_ffn_W2, L1_ffn_ln_g, L1_ffn_ln_b, L1_ffn_router_W, L1_ffn_router_b, L1_ffn_raw_U, L1_ffn_raw_V, L1_ffn_gamma):

    def _L0_attn_ref(x, norm_w, norm_b, in_w, in_b, conv_w, conv_b, bc_w, bc_b, dtr_w, dtr_b, dt_w, dt_b, out_w, out_b):
        import jax, jax.numpy as jnp
        import numpy as np
        H, EXP, N, CONV = (256, 2, 16, 4)
        INNER = H * EXP
        DTR = max(H // 16, 1)
        BATCH, SEQ = (2, 256)

        def _forward(x, norm_w, norm_b, in_w, in_b, conv_w, conv_b, bc_w, bc_b, dtr_w, dtr_b, dt_w, dt_b, out_w, out_b):
            B, L, _ = x.shape
            mu = x.mean(-1, keepdims=True)
            var = ((x - mu) ** 2).mean(-1, keepdims=True)
            normed = (x - mu) * jax.lax.rsqrt(var + 1e-05) * norm_w + norm_b
            xz = normed @ in_w + in_b
            xb, z = (xz[..., :INNER], xz[..., INNER:])
            xp = jnp.pad(xb, ((0, 0), (CONV - 1, 0), (0, 0)))
            xc = sum((xp[:, k:k + L, :] * conv_w[:, k] for k in range(CONV))) + conv_b
            xa = jax.nn.silu(xc)
            bc = xa @ bc_w + bc_b
            Bm, Cm = (bc[..., :N], bc[..., N:])
            dt = jax.nn.softplus((xa @ dtr_w + dtr_b) @ dt_w + dt_b)
            dt = jnp.clip(dt, 0.001, 0.1)
            a_diag = -(jnp.arange(N, dtype=jnp.float32) + 1.0)
            a_bar = jnp.exp(dt[..., None] * a_diag)
            dt_mean = dt.mean(axis=2, keepdims=True)[..., None]
            bx = dt_mean * Bm[:, :, None, :] * xa[..., None]

            def step(h, ts):
                a_t, bx_t, c_t = ts
                h = a_t * h + bx_t
                y = jnp.einsum('bdn,bn->bd', h, c_t)
                return (h, y)
            h0 = jnp.zeros((B, INNER, N), x.dtype)
            _, ys = jax.lax.scan(step, h0, (a_bar.transpose(1, 0, 2, 3), bx.transpose(1, 0, 2, 3), Cm.transpose(1, 0, 2)))
            ssm_out = ys.transpose(1, 0, 2)
            gated = ssm_out * jax.nn.silu(z)
            return gated @ out_w + out_b
        return _forward(x, norm_w, norm_b, in_w, in_b, conv_w, conv_b, bc_w, bc_b, dtr_w, dtr_b, dt_w, dt_b, out_w, out_b)

    def _L0_ffn_ref(x, wqkv, q_scale, k_scale, wo, ln_g, ln_b, w1, b1, w2, b2):
        import jax, jax.numpy as jnp
        import numpy as np
        DIM = 256
        DEPTH = 2
        HEADS = 8
        DIM_HEAD = 64
        WINDOW = 128
        INNER = HEADS * DIM_HEAD
        HID = int(DIM * 4 * 2 / 3)
        B, N = (2, 2048)
        QK_SCALE = 8.0

        def shift_token(t):
            t1, t2 = jnp.split(t, 2, axis=-1)
            t2 = jnp.pad(t2, ((0, 0), (1, 0), (0, 0)))[:, :-1]
            return jnp.concatenate([t1, t2], axis=-1)

        def l2norm(t):
            return t / jnp.clip(jnp.linalg.norm(t, axis=-1, keepdims=True), 1e-12)

        def rotate_half(x):
            x1, x2 = jnp.split(x, 2, axis=-1)
            return jnp.concatenate([-x2, x1], axis=-1)

        def rotary_xpos(q, k):
            n = q.shape[-2]
            half_idx = jnp.arange(0, DIM_HEAD, 2, dtype=jnp.float32)
            inv_freq = 1.0 / 10000.0 ** (half_idx / DIM_HEAD)
            t = jnp.arange(n, dtype=jnp.float32)
            freqs = t[:, None] * inv_freq[None, :]
            freqs = jnp.concatenate([freqs, freqs], axis=-1)
            base = (half_idx + 0.4 * DIM_HEAD) / (1.4 * DIM_HEAD)
            power = (t - n // 2) / float(WINDOW // 2)
            scale = base[None, :] ** power[:, None]
            scale = jnp.concatenate([scale, scale], axis=-1)
            cos, sin = (jnp.cos(freqs), jnp.sin(freqs))
            q = q * cos * scale + rotate_half(q) * sin * scale
            k = k * cos / scale + rotate_half(k) * sin / scale
            return (q, k)

        def local_attention(q, k, v):
            b, h, n, d = q.shape
            w = n // WINDOW
            bq = q.reshape(b, h, w, WINDOW, d) * QK_SCALE
            bk = k.reshape(b, h, w, WINDOW, d)
            bv = v.reshape(b, h, w, WINDOW, d)

            def look_around(t):
                p = jnp.pad(t, ((0, 0), (0, 0), (1, 0), (0, 0), (0, 0)))
                return jnp.concatenate([p[:, :, :w], p[:, :, 1:]], axis=3)
            bk, bv = (look_around(bk), look_around(bv))
            bt = jnp.arange(n).reshape(w, WINDOW)
            btp = jnp.pad(bt, ((1, 0), (0, 0)), constant_values=-1)
            btk = jnp.concatenate([btp[:w], btp[1:]], axis=1)
            sim = jnp.einsum('bhwid,bhwjd->bhwij', bq, bk)
            i = bt[:, :, None]
            j = btk[:, None, :]
            mask = (i < j) | (i > j + WINDOW) | (j == -1)
            sim = jnp.where(mask, -jnp.finfo(sim.dtype).max, sim)
            attn = jax.nn.softmax(sim, axis=-1)
            out = jnp.einsum('bhwij,bhwjd->bhwid', attn, bv)
            return out.reshape(b, h, n, d)

        def _layer(x, wqkv, qs, ksc, wo, lg, lb, w1, b1, w2, b2):
            b, n, _ = x.shape
            h = shift_token(x)
            qkv = h @ wqkv
            q, k, v = jnp.split(qkv, 3, axis=-1)
            to_heads = lambda t: t.reshape(b, n, HEADS, DIM_HEAD).transpose(0, 2, 1, 3)
            q, k, v = (to_heads(q), to_heads(k), to_heads(v))
            q = l2norm(q) * qs
            k = l2norm(k) * ksc
            q, k = rotary_xpos(q, k)
            o = local_attention(q, k, v)
            o = o.transpose(0, 2, 1, 3).reshape(b, n, INNER)
            x = x + o @ wo
            h = shift_token(x)
            mu = h.mean(-1, keepdims=True)
            var = h.var(-1, keepdims=True)
            h = (h - mu) / jnp.sqrt(var + 1e-05) * lg + lb
            h = h @ w1 + b1
            a, g = jnp.split(h, 2, axis=-1)
            h = a * jax.nn.gelu(g, approximate=False)
            x = x + h @ w2 + b2
            return x
        for l in range(DEPTH):
            x = _layer(x, wqkv[l], q_scale[l], k_scale[l], wo[l], ln_g[l], ln_b[l], w1[l], b1[l], w2[l], b2[l])
        return x

    def _L1_attn_ref(x, Wq, Wk, Wv, Wf, Wb, A_log, dt_bias, Wg, bg, Wo, norm_w):
        import jax, jax.numpy as jnp
        import numpy as np
        B, S, HID = (2, 512, 256)
        H, D = (16, 64)
        KD = H * D
        RMS_EPS = 1e-05
        L2_EPS = 1e-12

        def _l2norm(t):
            n = jnp.sqrt(jnp.sum(t * t, axis=-1, keepdims=True))
            return t / jnp.clip(n, L2_EPS)
        b, s, _ = x.shape
        h = A_log.shape[0]
        d = norm_w.shape[0]
        q = jax.nn.silu(x @ Wq).reshape(b, s, h, d)
        k = jax.nn.silu(x @ Wk).reshape(b, s, h, d)
        v = jax.nn.silu(x @ Wv).reshape(b, s, h, d)
        g = (x @ Wf).reshape(b, s, h, d)
        beta = jax.nn.sigmoid(x @ Wb)
        q = _l2norm(q)
        k = _l2norm(k)
        g = jax.nn.sigmoid(g - dt_bias.reshape(h, d))
        A = jnp.exp(-jnp.exp(A_log))
        qs = jnp.moveaxis(q, 1, 0)
        kss = jnp.moveaxis(k, 1, 0)
        vs = jnp.moveaxis(v, 1, 0)
        gs = jnp.moveaxis(g, 1, 0)
        bs = jnp.moveaxis(beta, 1, 0)
        state0 = jnp.zeros((b, h, d, d), x.dtype)

        def step(state, inp):
            q_t, k_t, v_t, g_t, b_t = inp
            o_t = jnp.einsum('bhd,bhde->bhe', q_t, state) * g_t
            state = A[None, :, None, None] * state + b_t[..., None, None] * (k_t[..., :, None] * v_t[..., None, :])
            return (state, o_t)
        _, o = jax.lax.scan(step, state0, (qs, kss, vs, gs, bs))
        o = jnp.moveaxis(o, 0, 1)
        o = o * jax.lax.rsqrt(jnp.mean(o * o, axis=-1, keepdims=True) + RMS_EPS) * norm_w
        gate = jax.nn.sigmoid(x @ Wg + bg).reshape(b, s, h, d)
        o = (o * gate).reshape(b, s, h * d)
        return o @ Wo

    def _L1_ffn_ref(x, W1, W2, ln_g, ln_b, router_W, router_b, raw_U, raw_V, gamma):
        import jax, jax.numpy as jnp
        import numpy as np
        TAU = 10.0
        EPS = 1e-06
        TOP_K = 8

        def _layernorm(x, g, b):
            mu = jnp.mean(x, axis=-1, keepdims=True)
            var = jnp.var(x, axis=-1, keepdims=True)
            return (x - mu) * jax.lax.rsqrt(var + 1e-05) * g + b

        def _unit_rows(W):
            n = jnp.linalg.norm(W, axis=1, keepdims=True)
            return W / jnp.maximum(n, EPS)
        B, S, D = x.shape
        x_flat = x.reshape(-1, D)
        r_raw = _layernorm(x_flat, ln_g, ln_b) @ router_W.T + router_b
        r = jnp.clip(r_raw, -TAU, TAU)
        alpha = jax.nn.softplus(r)
        phi, idx = jax.lax.top_k(alpha, TOP_K)
        S_sum = jnp.sum(phi, axis=-1, keepdims=True)
        Z = phi / (S_sum + EPS) * jnp.tanh(S_sum)
        U_sel = _unit_rows(raw_U)[idx]
        V_sel = _unit_rows(raw_V)[idx]
        h_lat = jnp.einsum('nd,nkd->nk', x_flat, U_sel)
        dyn = jnp.einsum('nk,nkd->nd', h_lat * Z, V_sel).reshape(B, S, D) * gamma
        static = (jax.nn.gelu(x_flat @ W1.T, approximate=False) @ W2.T).reshape(B, S, D)
        return static + dyn
    x = L0_attn_x
    xn = _layernorm(x, axis=-1)
    x = x + _L0_attn_ref(xn, L0_attn_norm_w, L0_attn_norm_b, L0_attn_in_w, L0_attn_in_b, L0_attn_conv_w, L0_attn_conv_b, L0_attn_bc_w, L0_attn_bc_b, L0_attn_dtr_w, L0_attn_dtr_b, L0_attn_dt_w, L0_attn_dt_b, L0_attn_out_w, L0_attn_out_b) + _L0_ffn_ref(xn, L0_ffn_wqkv, L0_ffn_q_scale, L0_ffn_k_scale, L0_ffn_wo, L0_ffn_ln_g, L0_ffn_ln_b, L0_ffn_w1, L0_ffn_b1, L0_ffn_w2, L0_ffn_b2)
    xn = _layernorm(x, axis=-1)
    x = x + _L1_attn_ref(xn, L1_attn_Wq, L1_attn_Wk, L1_attn_Wv, L1_attn_Wf, L1_attn_Wb, L1_attn_A_log, L1_attn_dt_bias, L1_attn_Wg, L1_attn_bg, L1_attn_Wo, L1_attn_norm_w) + _L1_ffn_ref(xn, L1_ffn_W1, L1_ffn_W2, L1_ffn_ln_g, L1_ffn_ln_b, L1_ffn_router_W, L1_ffn_router_b, L1_ffn_raw_U, L1_ffn_raw_V, L1_ffn_gamma)
    return x

_drawn_inputs = setup_inputs


def setup_inputs(seed=0):
    import zlib

    import numpy as np

    out = dict(_drawn_inputs(seed))
    spreads = {'L0_attn_norm_w': (1.0, 0.2),
     'L0_attn_norm_b': (0.0, 0.1),
     'L0_attn_in_b': (0.0, 0.1),
     'L0_attn_conv_b': (0.0, 0.1),
     'L0_attn_bc_b': (0.0, 0.1),
     'L0_attn_dtr_b': (0.0, 0.1),
     'L0_attn_dt_b': (0.0, 0.1),
     'L0_attn_out_b': (0.0, 0.1),
     'L0_ffn_q_scale': (1.0, 0.2),
     'L0_ffn_k_scale': (1.0, 0.2),
     'L0_ffn_ln_g': (1.0, 0.2),
     'L0_ffn_ln_b': (0.0, 0.1),
     'L0_ffn_b1': (0.0, 0.1),
     'L0_ffn_b2': (0.0, 0.1),
     'L1_attn_A_log': (2.079441547393799, 0.2),
     'L1_attn_dt_bias': (0.0, 0.1),
     'L1_attn_bg': (0.0, 0.1),
     'L1_attn_norm_w': (1.0, 0.2),
     'L1_ffn_ln_g': (1.0, 0.2),
     'L1_ffn_ln_b': (0.0, 0.1),
     'L1_ffn_router_b': (0.0, 0.1),
     'L1_ffn_gamma': (0.10000000149011612, 0.2)}
    factors = {}
    for name, (base, spread) in spreads.items():
        noise = np.random.default_rng([zlib.crc32(name.encode()), seed]).standard_normal(out[name].shape)
        drawn = base * np.exp(spread * noise) if base else spread * noise
        out[name] = jnp.asarray(drawn.astype(out[name].dtype))
    for name, factor in factors.items():
        out[name] = (out[name] * factor).astype(out[name].dtype)
    return out
```

```python
from contextlib import ExitStack

import numpy as np
import concourse.bass as bass
from concourse import mybir

F32 = mybir.dt.float32
BF16 = mybir.dt.bfloat16
ACT = mybir.ActivationFunctionType
ALU = mybir.AluOpType
AX = mybir.AxisListType.X

P = 128
B, L, H = 8, 512, 256
NT = L // P
HC = H // P
LN_EPS = 1e-5
PART_ROWS = 65

INNER, NS, CONV, DTR = 512, 16, 4, 16
IC = INNER // P
DEPTH, NH, DH, WIN = 2, 8, 64, 128
FI = NH * DH
FC = FI // P
HID = int(H * 4 * 2 / 3)
UC = -(-HID // P)
LAST = HID - (UC - 1) * P
QK_SCALE = 8.0
LH, LD = 16, 64
KD = LH * LD
KC = KD // P
NB, FF, TOPK, TAU, UNIT_EPS = 128, 1024, 8, 10.0, 1e-6
FFC = FF // P


def shape_constants():
    half = np.arange(0, DH, 2, dtype=np.float32)
    inv = (1.0 / 10000.0 ** (half / DH)).astype(np.float32)
    t = np.arange(L, dtype=np.float32)
    freqs = t[:, None] * inv[None, :]
    freqs = np.concatenate([freqs, freqs], -1)
    base = (half + np.float32(0.4 * DH)) / np.float32(1.4 * DH)
    power = (t - L // 2) / np.float32(WIN // 2)
    scale = base[None, :] ** power[:, None]
    scale = np.concatenate([scale, scale], -1)
    sign = np.where(np.arange(DH) < DH // 2, -1.0, 1.0).astype(np.float32)
    cos, sin = np.cos(freqs), np.sin(freqs) * sign
    rope = np.stack([cos * scale * QK_SCALE, sin * scale * QK_SCALE, cos / scale, sin / scale])
    rope = rope.reshape(4, NT, P, DH).transpose(2, 0, 1, 3)
    i = np.arange(P)
    far = -3.0e38
    window = np.stack([np.where(i[None, :] >= i[:, None], 0.0, far), np.where(i[None, :] <= i[:, None], 0.0, far)], 1)
    after = (i[None, :] > i[:, None]).astype(np.float32)
    gap = np.maximum(i[None, :] - 1 - i[:, None], 0)
    steps = np.broadcast_to(i[None, :], (P, P))
    tail = (P - 1 - i)[:, None]
    heads = (i[:, None] // LD == np.arange(2)[None, :])
    parts = [np.eye(P), rope, window, after, gap, steps, tail, heads]
    return np.concatenate([p.reshape(P, -1) for p in parts], 1).astype(np.float32)


CONST_AT = {}
_at = 0
for _name, _n in (("ident", P), ("rope", 4 * NT * DH), ("window", 2 * P), ("after", P), ("gap", P), ("steps", P),
                  ("tail", 1), ("heads", 2)):
    CONST_AT[_name] = (_at, _n)
    _at += _n


class Banks:

    def __init__(self, products, banks, filled, emptied):
        self.banks, self.filled_sem, self.emptied_sem = banks, filled, emptied
        self.place, self.by, self.nth, count = {}, [], [], {}
        for i, (key, engine) in enumerate(products):
            assert key not in self.place, key
            self.place[key] = i
            count[engine] = count.get(engine, 0) + 1
            self.by.append(engine)
            self.nth.append(count[engine])

    def bank(self, key):
        return self.banks[self.place[key] % len(self.banks)]

    def claim(self, pe, key):
        before = self.place[key] - len(self.banks)
        if before >= 0:
            pe.wait_ge(self.emptied_sem[self.by[before]], self.nth[before])
        return self.bank(key)

    def filled(self, eng, key):
        eng.wait_ge(self.filled_sem, self.place[key] + 1)
        return self.bank(key)

    def emptied(self, eng, key):
        i = self.place[key]
        eng.wait_ge(self.emptied_sem[self.by[i]], self.nth[i])


class Chain:

    def __init__(self, eng, sem):
        self.eng, self.sem, self.count = eng, sem, 0

    def __call__(self, instruction):
        self.count += 1
        instruction.then_inc(self.sem, 1)
        self.eng.wait_ge(self.sem, self.count)


def split3(ap, n):
    return ap.rearrange("p (a b) -> p a b", a=n)


def spread(column, shape):
    return column.unsqueeze(2).to_broadcast(shape)


def end_of_turn(eng, arrived, go):
    eng.drain().then_inc(arrived, 1)
    eng.wait_ge(go, 1)
    eng.sem_clear(go)


ATT = [(l, t) for l in range(DEPTH) for t in range(NT)]
PAIRS = FC
STEPS = [(n, c) for n in range(NS) for c in range(IC)]


SEGMENTS = {}
_chunk = 0
for _key, _rows in [((0, 1), 1), ((0, 2), 2), ((0, 3), 1), ((0, "ffn"), 2), ((1, 0), 2), ((1, 1), 1), ((1, 2), 2),
                    ((1, 3), 1), ((1, "ffn"), 2), ("tail", 2)]:
    SEGMENTS[_key] = (_chunk, _rows * IC // 2)
    _chunk += _rows * IC // 2
assert _chunk * 2 == NS * IC


def chunks(segment, place, places=4):
    first, n = SEGMENTS.get(segment, (0, 0))
    per = -(-n // places)
    skip = places - -(-n // per) if n else places
    if place < skip:
        return range(0)
    at = (place - skip) * per
    return range(first + at, first + min(n, at + per))


def segment_rows(segment):
    first, n = SEGMENTS.get(segment, (0, 0))
    return range(first * 2 // IC, (first + n) * 2 // IC)


def score_heads(p):
    return [4 * (p // 2) + 2 * i + p % 2 for i in range(2)]


def block_products():
    out = []
    for l in range(DEPTH):
        out += [(("hT", l, c), "act") for c in range(HC)]
        for t in range(NT):
            out += [(("q", l, t), "dve"), (("k", l, t), "dve"), (("v", l, t), "act"),
                    (("qT", l, t), "act"), (("kT", l, t), "act")]
            out += [(("s", l, t, p), "dve") for p in range(PAIRS)]
            out += [(("pT", l, t, p), "act") for p in range(PAIRS)]
            out += [(("o", l, t), "dve"), (("oT", l, t), "act"), (("wo", l, t), "dve")]
        out += [(("nT", l, c), "act") for c in range(HC)]
        for f in range(UC):
            out += [(("gate", l, f), "act"), (("up", l, f), "dve")]
        out += [(("down", l, t), "dve") for t in range(NT)]
    return out


def ssm_products():
    out = [(("zT", c), "act") for c in range(HC)]
    out += [(("xb", f), "act") for f in range(IC)]
    out += [(("B",), "act"), (("C",), "act"), (("R",), "act")]
    out += [(("dt", c), "dve") for c in range(IC)] + [(("mean",), "dve")]
    for n in range(NS):
        out += [(("Brow", n), "act"), (("Crow", n), "dve")]
    out += [(("z", f), "act") for f in range(IC)] + [(("ssm", t), "dve") for t in range(NT)]
    return out


def stage_one(nc, w, mid, consts):
    with ExitStack() as ctx:
        def sb(name, shape, dt=F32):
            return ctx.enter_context(nc.sbuf_tensor("one_" + name, shape, dt))

        turn_sems = []

        def sem(name, per_turn=True):
            s = ctx.enter_context(nc.semaphore("one_" + name))
            if per_turn:
                turn_sems.append(s)
            return s

        ps = ctx.enter_context(nc.psum_tensor("one_ps", [P, 8, 512], F32))

        ident = sb("ident", [P, P])[:]
        window = sb("window", [P, 2 * P])
        in_w = sb("in_w", [P, HC, 2 * INNER])
        out_w = sb("out_w", [P, IC, H])
        bc_w = sb("bc_w", [P, IC, 2 * NS])
        dtr_w = sb("dtr_w", [P, IC, DTR])
        dt_w = sb("dt_w", [DTR, INNER])
        out_b = sb("out_b", [1, H])
        ones = sb("ones", [1, P])
        wqkv = sb("wqkv", [P, DEPTH, HC, 3 * FI])
        wo = sb("wo", [P, DEPTH, FC, H])
        w1 = sb("w1", [P, DEPTH, HC, 2 * HID])
        w2 = sb("w2", [P, DEPTH, UC, H])
        col = sb("col", [P, 64])
        cols, at = {}, 0
        for name, n in (("norm_w", HC), ("norm_b", HC), ("in_b", 2 * IC), ("conv_b", IC), ("dt_b", IC),
                        ("ln_g", DEPTH * HC), ("ln_b", DEPTH * HC), ("b1", DEPTH * 2 * UC)):
            cols[name] = col[:, at:at + n]
            at += n
        conv_w = sb("conv_w", [P, IC, CONV])
        small_b = sb("small_b", [NS, 3])
        scales = sb("scales", [P, 2, DEPTH, DH])
        rope = sb("rope", [P, DEPTH, 4, NT, DH])
        mean_w = sb("mean_w", [P, NS])
        neghalf = sb("neghalf", [P, 8])
        one = sb("one", [P, 1])
        zeros = sb("zeros", [1, P])
        zero_row = zeros[0:1, :]

        xf = sb("xf", [P, NT, H])
        xs = sb("xs", [P, NT, H])
        hT = sb("hT", [P, HC, L + 1])
        qk = sb("qk", [P, 2, FI])
        vv = sb("vv", [P, 2, FI])
        qT = sb("qT", [P, PAIRS, P])
        kT = sb("kT", [P, 2, PAIRS, P])
        sm = sb("sm", [P, 2, 2, 2 * P])
        hid = sb("hid", [P, UC * L])
        pT = hid[:, 0:NH * 2 * P].rearrange("p (h k q) -> p h k q", h=NH, k=2)
        u = hid[:, :].rearrange("p (f t) -> p f t", f=UC)
        rope_table = hid[:, 0:4 * NT * DH]
        scratch = sb("scratch", [P, 2, L])
        sq, turned, gl, zs = scratch[:, 0, :], scratch[:, 1, :], scratch, scratch
        orow = sb("orow", [P, FI])
        oT = sb("oT", [P, FC, P])
        stat = sb("stat", [P, NT, 6])
        mv = sb("mv", [P, NT, 2])
        var = sb("var", [P, NT])
        rstd = sb("rstd", [P, NT])
        ssq = sb("ssq", [P, 2, NH])
        rnorm = sb("rnorm", [P, 2, NH])
        nmax = sb("nmax", [P, 2, 2])
        rsum = sb("rsum", [P, 2, NH])
        rinv = sb("rinv", [P, NH])

        zT = sb("zT", [P, HC, L])
        xb = sb("xb", [P, IC, L + CONV - 1])
        y = sb("y", [P, IC, L])
        xa = sb("xa", [P, IC, L])
        dt = sb("dt", [P, IC, L])
        bcr = sb("bcr", [NS, 3, L])
        rounded = bcr[:, 2, :].bitcast(BF16).rearrange("p (i t) -> p i t", i=2)
        left = scratch[0:NS]
        bc3 = sb("bc3", [64 + NS, 2, L], BF16)
        pick3 = sb("pick3", [64 + NS, NS], BF16)
        brow = sb("brow", [P, 2, L])
        decay = sb("decay", [P, 4, L])
        st = sb("st", [P, 4, L])

        wload = sem("wload", False)
        setup = sem("setup", False)
        setup_chain = sem("setup_chain", False)
        arrived = sem("arrived")
        go = {e: sem("go_" + e, False) for e in ("pe", "act", "dve", "pool")}

        FB = Banks(block_products(), [ps[:, i, :] for i in range(4)], sem("blk_filled"),
                   {"act": sem("blk_act_emptied"), "dve": sem("blk_dve_emptied")})
        MB = Banks(ssm_products(), [ps[:, 4 + i, :] for i in range(4)], sem("ssm_filled"),
                   {"act": sem("ssm_act_emptied"), "dve": sem("ssm_dve_emptied")})

        x_loaded = sem("x_loaded")
        stored = sem("stored")
        shifted = sem("shifted")
        x_again = sem("x_again")
        dve_chain = sem("dve_chain")
        pool_chain = sem("pool_chain")
        var_ready = sem("var_ready")
        rstd_ready = sem("rstd_ready")
        xn_ready = sem("xn_ready")
        zn_ready = sem("zn_ready")
        sq_ready = sem("sq_ready")
        ssq_ready = sem("ssq_ready")
        rnorm_ready = sem("rnorm_ready")
        qk_ready = sem("qk_ready")
        smax_ready = sem("smax_ready")
        p_ready = sem("p_ready")
        n_ready = sem("n_ready")
        out_ready = sem("out_ready")
        conv_ready = sem("conv_ready")
        xa_ready = sem("xa_ready")
        pre_ready = sem("pre_ready")
        e_ready = sem("e_ready")
        sp_ready = sem("sp_ready")
        dt_ready = sem("dt_ready")
        bc_split = sem("bc_split")
        decay_ready = sem("decay_ready")
        bx_ready = sem("bx_ready")
        scanned = sem("scanned")
        hc_ready = sem("hc_ready")
        y_added = sem("y_added")
        zs_ready = sem("zs_ready")
        gated_ready = sem("gated_ready")

        def const(name):
            a, n = CONST_AT[name]
            return consts[:, a:a + n]

        weight_loads = [
            (ident, const("ident")), (window[:], const("window")), (rope_table, const("rope")), (in_w[:], w["L0_attn_in_w"].rearrange("(c p) n -> p c n", p=P)),
            (out_w[:], w["L0_attn_out_w"].rearrange("(c p) n -> p c n", p=P)),
            (bc_w[:], w["L0_attn_bc_w"].rearrange("(c p) n -> p c n", p=P)),
            (dtr_w[:], w["L0_attn_dtr_w"].rearrange("(c p) n -> p c n", p=P)),
            (dt_w[:], w["L0_attn_dt_w"]), (out_b[:], w["L0_attn_out_b"].unsqueeze(0)),
            (conv_w[:], w["L0_attn_conv_w"].rearrange("(c p) k -> p c k", p=P)),
            (small_b[:, 0:1], w["L0_attn_bc_b"][0:NS].unsqueeze(1)),
            (small_b[:, 1:2], w["L0_attn_bc_b"][NS:2 * NS].unsqueeze(1)),
            (small_b[:, 2:3], w["L0_attn_dtr_b"].unsqueeze(1)),
            (scales[:, 0, :, :], w["L0_ffn_q_scale"].partition_broadcast(P)),
            (scales[:, 1, :, :], w["L0_ffn_k_scale"].partition_broadcast(P)),
        ]
        for name in ("norm_w", "norm_b", "in_b", "conv_b", "dt_b"):
            weight_loads.append((cols[name], w["L0_attn_" + name].rearrange("(c p) -> p c", p=P)))
        for l in range(DEPTH):
            weight_loads += [
                (wqkv[:, l], w["L0_ffn_wqkv"][l].rearrange("(c p) n -> p c n", p=P)),
                (wo[:, l], w["L0_ffn_wo"][l].rearrange("(c p) n -> p c n", p=P)),
                (w1[:, l], w["L0_ffn_w1"][l].rearrange("(c p) n -> p c n", p=P)),
                (w2[:, l, 0:UC - 1], w["L0_ffn_w2"][l, 0:(UC - 1) * P].rearrange("(c p) n -> p c n", p=P)),
                (w2[0:LAST, l, UC - 1], w["L0_ffn_w2"][l, (UC - 1) * P:HID]),
                (w2[LAST:LAST + 1, l, UC - 1], w["L0_ffn_b2"][l:l + 1]),
                (cols["ln_g"][:, l * HC:(l + 1) * HC], w["L0_ffn_ln_g"][l].rearrange("(c p) -> p c", p=P)),
                (cols["ln_b"][:, l * HC:(l + 1) * HC], w["L0_ffn_ln_b"][l].rearrange("(c p) -> p c", p=P)),
            ]
            for part in range(2):
                at, b1 = (2 * l + part) * UC, w["L0_ffn_b1"][l, part * HID:(part + 1) * HID]
                weight_loads += [
                    (cols["b1"][:, at:at + UC - 1], b1[0:(UC - 1) * P].rearrange("(c p) -> p c", p=P)),
                    (cols["b1"][0:LAST, at + UC - 1:at + UC], b1[(UC - 1) * P:HID].unsqueeze(1)),
                ]

        x_rows = w["L0_attn_x"].rearrange("b (t p) h -> b p t h", p=P)
        mid_rows = mid.rearrange("b (t p) h -> b p t h", p=P)
        block = ctx.enter_context(nc.Block())

        @block.sync
        def _(sp):
            with nc.allow_non_contiguous_dma(reason="per-feature vectors as columns, once"):
                for dst, src in weight_loads:
                    sp.dma_start(dst, src).then_inc(wload, 16)
            with sp.Fori(0, B) as b:
                sp.dma_start(xs[:], x_rows[bass.ds(b, 1)].squeeze(0)).then_inc(x_loaded, 16)
                for l in range(DEPTH):
                    FB.emptied(sp, ("wo", l, NT - 1))
                    if l == 0:
                        MB.filled(sp, ("zT", HC - 1))
                    sp.dma_start(xs[:, :, 0:P], xf[:, :, 0:P]).then_inc(shifted, 16)
                    sp.dma_start(xs[1:P, :, P:H], xf[0:P - 1, :, P:H]).then_inc(shifted, 16)
                    sp.dma_start(xs[0:1, 1:NT, P:H], xf[P - 1:P, 0:NT - 1, P:H]).then_inc(shifted, 16)
                    sp.dma_start(xs[0:1, 0, P:H], zero_row).then_inc(shifted, 16)
                FB.filled(sp, ("nT", DEPTH - 1, HC - 1))
                sp.dma_start(xs[:], x_rows[bass.ds(b, 1)].squeeze(0)).then_inc(x_again, 16)
                sp.wait_ge(out_ready, NT)
                sp.dma_start(mid_rows[bass.ds(b, 1)].squeeze(0), xf[:]).then_inc(stored, 16)
                sp.wait_ge(stored, 16)
                sp.wait_ge(arrived, 4)
                for s in turn_sems:
                    sp.sem_clear(s)
                for e in go:
                    sp.sem_inc(go[e], 1)


        @block.tensor
        def _(pe):
            def mm(out, lhsT, rhs, first, last):
                return pe.matmul(out, lhsT, rhs, start=first, stop=last)

            def close(product, banks):
                product.then_inc(banks.filled_sem, 1)

            def turn(banks, key, source, n):
                bank = banks.claim(pe, key)
                for i in range(n):
                    last = pe.transpose(bank[:, i * P:(i + 1) * P], source(i), ident)
                close(last, banks)

            def ssm_inputs():
                pe.wait_ge(zn_ready, NT)
                for c in range(HC):
                    turn(MB, ("zT", c), lambda t: xs[:, t, c * P:(c + 1) * P], NT)
                ssm_project("xb", 0)

            def ssm_project(name, first_chunk):
                MB.emptied(pe, ("zT", HC - 1))
                for f in range(IC):
                    bank = MB.claim(pe, (name, f))
                    at = (first_chunk + f) * P
                    for c in range(HC):
                        last = mm(bank, in_w[:, c, at:at + P], zT[:, c, :], c == 0, c == HC - 1)
                    close(last, MB)

            def ssm_rates():
                pe.wait_ge(xa_ready, IC)
                for key, wt in ((("B",), bc_w[:, :, 0:NS]), (("C",), bc_w[:, :, NS:2 * NS]), (("R",), dtr_w[:])):
                    bank = MB.claim(pe, key)
                    for c in range(IC):
                        last = mm(bank[0:NS, :], wt[:, c, :], xa[:, c, :], c == 0, c == IC - 1)
                    close(last, MB)
                MB.emptied(pe, ("R",))
                for c in range(IC):
                    bank = MB.claim(pe, ("dt", c))
                    close(mm(bank, dt_w[:, c * P:(c + 1) * P], bcr[:, 2, :], True, True), MB)
                bank = MB.claim(pe, ("mean",))
                pe.wait_ge(dt_ready, IC)
                for c in range(IC):
                    last = mm(bank[0:NS, :], mean_w[:], dt[:, c, :], c == 0, c == IC - 1)
                close(last, MB)

            def ssm_row(n):
                if n == 0:
                    pe.wait_ge(bc_split, 1)
                pick = pick3[:, n:n + 1].to_broadcast([64 + NS, P])
                for i, name in enumerate(("Brow", "Crow")):
                    bank = MB.claim(pe, (name, n))
                    close(mm(bank, pick, bc3[:, i, :], True, True), MB)

            def features(l):
                if l == 0:
                    pe.wait_ge(xn_ready, NT)
                else:
                    FB.emptied(pe, ("down", l - 1, NT - 1))
                for c in range(HC):
                    turn(FB, ("hT", l, c), lambda t: xf[:, t, c * P:(c + 1) * P], NT)

            def project(l, t):
                FB.emptied(pe, ("hT", l, HC - 1))
                for i, name in enumerate("qkv"):
                    bank = FB.claim(pe, (name, l, t))
                    for c in range(HC):
                        last = mm(bank, hT[:, c, t * P:(t + 1) * P], wqkv[:, l, c, i * FI:(i + 1) * FI],
                                  c == 0, c == HC - 1)
                    close(last, FB)

            def turn_qk(l, t):
                g = l * NT + t
                for i, name in enumerate(("qT", "kT")):
                    pe.wait_ge(qk_ready, 2 * g + i + 1)
                    turn(FB, (name, l, t), lambda p: qk[:, i, p * P:(p + 1) * P], PAIRS)

            def scores(l, t):
                g = l * NT + t
                FB.emptied(pe, ("kT", l, t))
                for p in range(PAIRS):
                    bank = split3(FB.claim(pe, ("s", l, t, p)), 2)
                    for h, head in enumerate(score_heads(p)):
                        rows = slice(head % 2 * DH, (head % 2 + 1) * DH)
                        for k in range(0 if t else 1, 2):
                            last = mm(bank[:, h, k * P:(k + 1) * P], qT[rows, head // 2, :],
                                      kT[rows, (g + k - 1) % 2, head // 2, :], True, True)
                    close(last, FB)

            def turn_p(l, t):
                g = l * NT + t
                for p in range(PAIRS):
                    bank = FB.claim(pe, ("pT", l, t, p)).rearrange("p (h k q) -> p h k q", h=2, k=2)
                    pe.wait_ge(p_ready, g * PAIRS + p + 1)
                    for h in range(2):
                        for k in range(0 if t else 1, 2):
                            last = pe.transpose(bank[:, h, k, :], sm[:, p % 2, h, k * P:(k + 1) * P], ident)
                    close(last, FB)

            def attend(l, t):
                g = l * NT + t
                bank = FB.claim(pe, ("o", l, t))
                FB.emptied(pe, ("pT", l, t, PAIRS - 1))
                for h in range(NH):
                    for k in range(0 if t else 1, 2):
                        last = mm(bank[:, h * DH:(h + 1) * DH], pT[:, h, k, :],
                                  vv[:, (g + k - 1) % 2, h * DH:(h + 1) * DH], k == 0 or t == 0, k == 1)
                close(last, FB)

            def attend_out(l, t):
                FB.emptied(pe, ("o", l, t))
                turn(FB, ("oT", l, t), lambda c: orow[:, c * P:(c + 1) * P], FC)
                bank = FB.claim(pe, ("wo", l, t))
                FB.emptied(pe, ("oT", l, t))
                for c in range(FC):
                    last = mm(bank[:, 0:H], oT[:, c, :], wo[:, l, c, :], c == 0, c == FC - 1)
                close(last, FB)

            def ffn_in(l):
                pe.wait_ge(n_ready, (l + 1) * NT)
                for c in range(HC):
                    turn(FB, ("nT", l, c), lambda t: xs[:, t, c * P:(c + 1) * P], NT)

            def ffn_hidden(l, f):
                if f == 0:
                    FB.emptied(pe, ("nT", l, HC - 1))
                m = P if f < UC - 1 else LAST
                for name, at in (("gate", HID), ("up", 0)):
                    bank = FB.claim(pe, (name, l, f))
                    for c in range(HC):
                        last = mm(bank[0:m, :], w1[:, l, c, at + f * P:at + f * P + m], hT[:, c, c:c + L],
                                  c == 0, c == HC - 1)
                    close(last, FB)

            def ffn_down(l):
                FB.emptied(pe, ("up", l, UC - 1))
                for t in range(NT):
                    bank = FB.claim(pe, ("down", l, t))
                    for f in range(UC):
                        m = P if f < UC - 1 else LAST + 1
                        last = mm(bank[:, 0:H], u[0:m, f, t * P:(t + 1) * P], w2[0:m, l, f, :],
                                  f == 0, f == UC - 1)
                    close(last, FB)

            def ssm_out():
                pe.wait_ge(gated_ready, IC)
                for t in range(NT):
                    bank = MB.claim(pe, ("ssm", t))[:, 0:H]
                    for c in range(IC):
                        mm(bank, y[:, c, t * P:(t + 1) * P], out_w[:, c, :], c == 0, False)
                    close(mm(bank, ones[:], out_b[:], False, True), MB)

            pe.wait_ge(wload, 16 * len(weight_loads))
            pe.wait_ge(setup, 1)
            with pe.Fori(0, B):
                rows = iter(range(NS))
                features(0)
                project(0, 0)
                ssm_inputs()
                ssm_rates()
                for l in range(DEPTH):
                    if l:
                        features(l)
                        project(l, 0)
                    for t in range(NT):
                        turn_qk(l, t)
                        scores(l, t)
                        turn_p(l, t)
                        attend(l, t)
                        attend_out(l, t)
                        if t + 1 < NT:
                            project(l, t + 1)
                        ssm_row(next(rows))
                        if t % 2:
                            ssm_row(next(rows))
                    ffn_in(l)
                    for f in range(UC):
                        ffn_hidden(l, f)
                        if f in (2, 5):
                            ssm_row(next(rows))
                    ffn_down(l)
                assert next(rows, None) is None
                ssm_project("z", IC)
                ssm_out()
                end_of_turn(pe, arrived, go["pe"])


        @block.scalar
        def _(act):
            def run(out, src, func, **kw):
                return nc.scalar.activation(out, src, func, **kw)

            def ssm_prepare():
                for c in range(HC):
                    run(zT[:, c, :], MB.filled(act, ("zT", c)), ACT.Identity, scale=cols["norm_w"][:, c:c + 1],
                        bias=cols["norm_b"][:, c:c + 1]).then_inc(MB.emptied_sem["act"], 1)
                for f in range(IC):
                    run(xb[:, f, CONV - 1:], MB.filled(act, ("xb", f)), ACT.Identity,
                        bias=cols["in_b"][:, f:f + 1]).then_inc(MB.emptied_sem["act"], 1)
                for f in range(IC):
                    act.wait_ge(conv_ready, (CONV - 1) * IC + f + 1)
                    run(xa[:, f, :], y[:, f, :], ACT.Silu).then_inc(xa_ready, 1)
                for i, name in enumerate("BCR"):
                    run(bcr[:, i, :], MB.filled(act, (name,))[0:NS, :], ACT.Identity,
                        bias=small_b[:, i:i + 1]).then_inc(MB.emptied_sem["act"], 1)
                for c in range(IC):
                    MB.emptied(act, ("dt", c))
                    run(dt[:, c, :], dt[:, c, :], ACT.Exp).then_inc(e_ready, 1)
                for c in range(IC):
                    act.wait_ge(e_ready, c + 1)
                    run(dt[:, c, :], dt[:, c, :], ACT.Ln, bias=one[:]).then_inc(sp_ready, 1)

            def take_rows(segment):
                for n in segment_rows(segment):
                    src = MB.filled(act, ("Brow", n))
                    if n >= 2:
                        act.wait_ge(bx_ready, IC * (n - 1))
                    run(brow[:, n % 2, :], src, ACT.Copy).then_inc(MB.emptied_sem["act"], 1)

            def decays(chunk_range):
                for j in chunk_range:
                    for i in (2 * j, 2 * j + 1):
                        n, c = STEPS[i]
                        if i == 0:
                            act.wait_ge(dt_ready, IC)
                        if i >= 4:
                            act.wait_ge(scanned, i - 3)
                        run(decay[:, i % 4, :], dt[:, c, :], ACT.Exp, scale=-(n + 1.0)).then_inc(decay_ready, 1)

            def features(l):
                for c in range(HC):
                    run(hT[:, c, c:c + L], FB.filled(act, ("hT", l, c)), ACT.Copy)\
                        .then_inc(FB.emptied_sem["act"], 1)

            def squares(l, t):
                g = l * NT + t
                for i, name in enumerate("qk"):
                    bank = FB.filled(act, (name, l, t))
                    if 2 * g + i >= 1:
                        act.wait_ge(ssq_ready, 2 * g + i)
                    run(sq, bank, ACT.Square).then_inc(sq_ready, 1)
                bank = FB.filled(act, ("v", l, t))
                run(vv[:, g % 2, :], bank, ACT.Copy).then_inc(FB.emptied_sem["act"], 1)

            def attention(l, t):
                g = l * NT + t
                lo = 0 if t else P
                for key, dst in ((("qT", l, t), qT[:]), (("kT", l, t), kT[:, g % 2])):
                    run(dst, split3(FB.filled(act, key), PAIRS), ACT.Copy).then_inc(FB.emptied_sem["act"], 1)
                decays(chunks((l, t), 0))

                def exps(p):
                    act.wait_ge(smax_ready, g * PAIRS + p + 1)
                    for h, head in enumerate(score_heads(p)):
                        s = sm[:, p % 2, h, lo:2 * P]
                        last = run(s, s, ACT.Exp, bias=nmax[:, p % 2, h:h + 1],
                                   accum_out=rsum[:, g % 2, head:head + 1])
                    last.then_inc(p_ready, 1)

                def take(p):
                    src = FB.filled(act, ("pT", l, t, p)).rearrange("p (h k q) -> p h k q", h=2, k=2)
                    k = 0 if t else 1
                    first, last = score_heads(p)
                    run(pT[:, first:last + 1:2, k:2, :], src[:, :, k:2, :], ACT.Copy)\
                        .then_inc(FB.emptied_sem["act"], 1)

                exps(0)
                exps(1)
                decays(chunks((l, t), 1))
                take(0)
                exps(2)
                take(1)
                exps(3)
                decays(chunks((l, t), 2))
                take(2)
                take(3)
                decays(chunks((l, t), 3))
                run(oT[:], split3(FB.filled(act, ("oT", l, t)), FC), ACT.Copy).then_inc(FB.emptied_sem["act"], 1)

            def ffn(l):
                take_rows((l, "ffn"))
                decays(chunks((l, "ffn"), 0, 2))
                for c in range(HC):
                    at = l * HC + c
                    run(hT[:, c, c:c + L], FB.filled(act, ("nT", l, c)), ACT.Identity,
                        scale=cols["ln_g"][:, at:at + 1], bias=cols["ln_b"][:, at:at + 1])\
                        .then_inc(FB.emptied_sem["act"], 1)
                for f in range(UC):
                    m = P if f < UC - 1 else LAST
                    at = (2 * l + 1) * UC + f
                    src = FB.filled(act, ("gate", l, f))
                    if f >= 2:
                        FB.emptied(act, ("up", l, f - 2))
                    run(gl[0:m, f % 2, :], src[0:m, :], ACT.Gelu, bias=cols["b1"][0:m, at:at + 1])\
                        .then_inc(FB.emptied_sem["act"], 1)
                    if f == 2:
                        decays(chunks((l, "ffn"), 1, 2))

            act.wait_ge(wload, 16 * len(weight_loads))
            act.wait_ge(setup, 1)
            with act.Fori(0, B):
                features(0)
                squares(0, 0)
                ssm_prepare()
                for l in range(DEPTH):
                    if l:
                        features(l)
                        squares(l, 0)
                    for t in range(NT):
                        take_rows((l, t))
                        attention(l, t)
                        if t + 1 < NT:
                            squares(l, t + 1)
                    ffn(l)
                take_rows("tail")
                for place in range(4):
                    decays(chunks("tail", place))
                for f in range(IC):
                    src = MB.filled(act, ("z", f))
                    if f >= 2:
                        act.wait_ge(gated_ready, f - 1)
                    run(zs[:, f % 2, :], src, ACT.Silu, bias=cols["in_b"][:, IC + f:IC + f + 1])\
                        .then_inc(MB.emptied_sem["act"], 1)
                end_of_turn(act, arrived, go["act"])

        @block.vector
        def _(dve):
            chain = Chain(dve, dve_chain)
            norms = [0]

            def tt(out, a, b, op):
                return nc.vector.tensor_tensor(out, a, b, op)

            def norm(src, dst, signal):
                for t in range(NT):
                    last = nc.vector.bn_stats(stat[:, t, :], src[:, t, :])
                chain(last)
                for t in range(NT):
                    last = nc.vector.bn_aggr(mv[:, t, :], stat[:, t, :])
                chain(last)
                nc.vector.tensor_scalar(var[:], mv[:, :, 1], LN_EPS, None, ALU.add).then_inc(var_ready, 1)
                norms[0] += 1
                dve.wait_ge(rstd_ready, norms[0])
                for t in range(NT):
                    nc.vector.tensor_scalar(dst[:, t, :], src[:, t, :], mv[:, t, 0:1], rstd[:, t:t + 1],
                                            ALU.subtract, ALU.mult).then_inc(signal, 1)

            def ssm_prepare():
                for k in range(CONV):
                    for f in range(IC):
                        if k == 0:
                            MB.emptied(dve, ("xb", f))
                            ins = nc.vector.tensor_scalar(y[:, f, :], xb[:, f, 0:L], conv_w[:, f, 0:1],
                                                          cols["conv_b"][:, f:f + 1], ALU.mult, ALU.add)
                        else:
                            dve.wait_ge(conv_ready, (k - 1) * IC + f + 1)
                            ins = nc.vector.scalar_tensor_tensor(
                                out=y[:, f, :], in0=xb[:, f, k:k + L], scalar=conv_w[:, f, k:k + 1],
                                in1=y[:, f, :], op0=ALU.mult, op1=ALU.add)
                        ins.then_inc(conv_ready, 1)
                for c in range(IC):
                    nc.vector.tensor_scalar(dt[:, c, :], MB.filled(dve, ("dt", c)), cols["dt_b"][:, c:c + 1],
                                            20.0, ALU.add, ALU.min).then_inc(MB.emptied_sem["dve"], 1)
                for c in range(IC):
                    dve.wait_ge(sp_ready, c + 1)
                    nc.vector.tensor_scalar(dt[:, c, :], dt[:, c, :], 0.001, 0.1, ALU.max, ALU.min)\
                        .then_inc(dt_ready, 1)
                MB.emptied(dve, ("B",))
                tt(bcr[:, 0, :], bcr[:, 0, :], MB.filled(dve, ("mean",))[0:NS, :], ALU.mult)\
                    .then_inc(MB.emptied_sem["dve"], 1)
                MB.emptied(dve, ("mean",))
                rows = bcr[:, 0:2, :]
                chain(nc.vector.tensor_copy(bc3[0:NS], rows))
                chain(tt(left, rows, bc3[0:NS], ALU.subtract))
                chain(nc.vector.tensor_copy(rounded, left))
                nc.vector.tensor_copy(bc3[32:32 + NS], rounded)
                tt(bc3[64:64 + NS], left, rounded, ALU.subtract).then_inc(bc_split, 1)

            def scans(chunk_range):
                for j in chunk_range:
                    pair = (2 * j, 2 * j + 1)
                    for i in pair:
                        dve.wait_ge(decay_ready, i + 1)
                        dve.wait_ge(bx_ready, i + 1)
                        s = st[:, i % 4, :]
                        nc.vector.tensor_tensor_scan(s, decay[:, i % 4, :], s, 0.0, ALU.mult, ALU.add)\
                            .then_inc(scanned, 1)
                    for i in pair:
                        n, c = STEPS[i]
                        crow = MB.filled(dve, ("Crow", n))
                        dve.wait_ge(scanned, i + 1)
                        dst = y[:, c, :] if n == 0 else st[:, i % 4, :]
                        ins = tt(dst, st[:, i % 4, :], crow, ALU.mult)
                        ins.then_inc(MB.emptied_sem["dve"] if c == IC - 1 else hc_ready, 1)

            def rotate(l, t):
                g = l * NT + t
                for i, name in enumerate("qk"):
                    bank = FB.filled(dve, (name, l, t))
                    if g:
                        FB.filled(dve, (name + "T",) + ATT[g - 1])
                    heads = bank.rearrange("p (h d) -> p h d", h=NH)
                    swapped = bank.rearrange("p (h s d) -> p h s d", h=NH, s=2)[:, :, ::-1, :]
                    cos = rope[:, l, 2 * i, t, :].unsqueeze(1).to_broadcast([P, NH, DH])
                    sin = split3(rope[:, l, 2 * i + 1, t, :], 2).unsqueeze(1).to_broadcast([P, NH, 2, DH // 2])
                    rows = qk[:, i, :].rearrange("p (h d) -> p h d", h=NH)
                    dve.wait_ge(sq_ready, 2 * g + i + 1)
                    tt(rows, heads, cos, ALU.mult)
                    tt(turned.rearrange("p (h s d) -> p h s d", h=NH, s=2), swapped, sin, ALU.mult)\
                        .then_inc(FB.emptied_sem["dve"], 1)
                    nc.vector.reduce_sum(ssq[:, i, :], sq.rearrange("p (h d) -> p h d", h=NH), AX)\
                        .then_inc(ssq_ready, 1)
                    FB.emptied(dve, (name, l, t))
                    chain(tt(qk[:, i, :], qk[:, i, :], turned, ALU.add))
                for i in range(2):
                    rows = qk[:, i, :].rearrange("p (h d) -> p h d", h=NH)
                    dve.wait_ge(rnorm_ready, 2 * g + i + 1)
                    tt(rows, rows, spread(rnorm[:, i, :], [P, NH, DH]), ALU.mult).then_inc(qk_ready, 1)

            def attention(l, t):
                g = l * NT + t
                lo = 0 if t else P
                scans(chunks((l, t), 0))
                for p in range(PAIRS):
                    bank = split3(FB.filled(dve, ("s", l, t, p)), 2)
                    if p >= 2:
                        FB.filled(dve, ("pT", l, t, p - 2))
                    elif g:
                        FB.filled(dve, ("pT",) + ATT[g - 1] + (p + 2,))
                    s = sm[:, p % 2, :, lo:2 * P]
                    tt(s, bank[:, :, lo:2 * P], window[:, lo:2 * P].unsqueeze(1)
                       .to_broadcast([P, 2, 2 * P - lo]), ALU.add).then_inc(FB.emptied_sem["dve"], 1)
                    FB.emptied(dve, ("s", l, t, p))
                    nc.vector.tensor_reduce(nmax[:, p % 2, :], s, AX, ALU.max, negate=True).then_inc(smax_ready, 1)
                    if p % 2:
                        scans(chunks((l, t), 1 + p // 2))
                dve.wait_ge(p_ready, (g + 1) * PAIRS)
                chain(nc.vector.reciprocal(rinv[:], rsum[:, g % 2, :]))
                bank = FB.filled(dve, ("o", l, t))
                if g:
                    FB.filled(dve, ("oT",) + ATT[g - 1])
                tt(orow[:].rearrange("p (h d) -> p h d", h=NH), bank.rearrange("p (h d) -> p h d", h=NH),
                   spread(rinv[:], [P, NH, DH]), ALU.mult).then_inc(FB.emptied_sem["dve"], 1)
                scans(chunks((l, t), 3))
                add_rows(("wo", l, t), t)

            def add_rows(key, t):
                tt(xf[:, t, :], xf[:, t, :], FB.filled(dve, key)[:, 0:H], ALU.add)\
                    .then_inc(FB.emptied_sem["dve"], 1)

            def ffn(l):
                scans(chunks((l, "ffn"), 0, 2))
                dve.wait_ge(shifted, 16 * 4 * (l + 1))
                norm(xs, xs, n_ready)
                for f in range(UC):
                    m = P if f < UC - 1 else LAST
                    at = 2 * l * UC + f
                    bank = FB.filled(dve, ("up", l, f))
                    FB.emptied(dve, ("gate", l, f))
                    nc.vector.scalar_tensor_tensor(
                        out=u[0:m, f, :], in0=bank[0:m, :], scalar=cols["b1"][0:m, at:at + 1],
                        in1=gl[0:m, f % 2, :], op0=ALU.add, op1=ALU.mult).then_inc(FB.emptied_sem["dve"], 1)
                    if f == 2:
                        scans(chunks((l, "ffn"), 1, 2))
                for t in range(NT):
                    add_rows(("down", l, t), t)

            dve.memset(xb[:], 0.0)
            dve.memset(hT[:], 0.0)
            dve.memset(hid[32:64, (UC - 1) * L:UC * L], 1.0)
            dve.memset(zeros[:], 0.0)
            prepare = Chain(dve, setup_chain)
            prepare(dve.memset(bc3[:], 0.0))
            prepare(dve.memset(pick3[:], 0.0))
            dve.memset(ones[:], 1.0)
            dve.memset(one[:], 1.0)
            dve.memset(neghalf[:], -0.5)
            dve.memset(mean_w[:], 1.0 / INNER)
            dve.wait_ge(wload, 16 * len(weight_loads))
            for i in range(3):
                nc.vector.tensor_copy(pick3[32 * i:32 * i + NS, :], ident[0:NS, 0:NS])
            table = rope_table.rearrange("p (k t d) -> p k t d", k=4, t=NT)
            for l in range(DEPTH):
                for i in range(2):
                    s = scales[:, i, l, :]
                    flip = split3(s, 2)[:, ::-1, :]
                    tt(rope[:, l, 2 * i], table[:, 2 * i], s.unsqueeze(1).to_broadcast([P, NT, DH]), ALU.mult)
                    for t in range(NT):
                        ins = tt(split3(rope[:, l, 2 * i + 1, t], 2), split3(table[:, 2 * i + 1, t], 2), flip,
                                 ALU.mult)
            ins.then_inc(setup, 1)
            dve.wait_ge(setup, 1)
            with dve.Fori(0, B):
                chain.count = norms[0] = 0
                dve.wait_ge(x_loaded, 16)
                norm(xs, xf, xn_ready)
                dve.wait_ge(xn_ready, NT)
                norm(xf, xs, zn_ready)
                rotate(0, 0)
                ssm_prepare()
                for l in range(DEPTH):
                    for t in range(NT):
                        if (l, t) != (0, 0):
                            rotate(l, t)
                        attention(l, t)
                    ffn(l)
                for place in range(4):
                    scans(chunks("tail", place))
                for t in range(NT):
                    MB.filled(dve, ("ssm", t))
                    FB.emptied(dve, ("down", DEPTH - 1, t))
                    tt(xf[:, t, :], xf[:, t, :], MB.bank(("ssm", t))[:, 0:H], ALU.add)\
                        .then_inc(MB.emptied_sem["dve"], 1)
                dve.wait_ge(x_again, 16)
                for t in range(NT):
                    MB.emptied(dve, ("ssm", t))
                    tt(xf[:, t, :], xf[:, t, :], xs[:, t, :], ALU.add).then_inc(out_ready, 1)
                end_of_turn(dve, arrived, go["dve"])

        @block.gpsimd
        def _(pool):
            norms, tiles = [0], [0]

            def inverse_roots():
                norms[0] += 1
                pool.wait_ge(var_ready, norms[0])
                nc.gpsimd.tensor_tensor(rstd[:], var[:], neghalf[:, 0:NT], ALU.pow).then_inc(rstd_ready, 1)

            def inverse_norms(g):
                for i in range(2):
                    pool.wait_ge(ssq_ready, 2 * g + i + 1)
                    nc.gpsimd.tensor_scalar(ssq[:, i, :], ssq[:, i, :], 1e-24, None, ALU.max)\
                        .then_inc(pool_chain, 1)
                    pool.wait_ge(pool_chain, 2 * g + i + 1)
                    nc.gpsimd.tensor_tensor(rnorm[:, i, :], ssq[:, i, :], neghalf[:], ALU.pow)\
                        .then_inc(rnorm_ready, 1)

            def inputs(j):
                for i in (2 * j, 2 * j + 1):
                    n, c = STEPS[i]
                    MB.emptied(pool, ("Brow", n))
                    if i >= 4 + IC:
                        pool.wait_ge(y_added, i - 4 - IC + 1)
                    nc.gpsimd.tensor_tensor(st[:, i % 4, :], brow[:, n % 2, :], xa[:, c, :], ALU.mult)\
                        .then_inc(bx_ready, 1)

            def product_ready(i):
                n, c = STEPS[i]
                if c == IC - 1:
                    MB.emptied(pool, ("Crow", n))
                else:
                    pool.wait_ge(hc_ready, n * (IC - 1) + c + 1)

            def sums(j):
                for i in (2 * j, 2 * j + 1):
                    n, c = STEPS[i]
                    product_ready(i)
                    if n == 0:
                        continue
                    if n >= 2:
                        pool.wait_ge(y_added, i - 2 * IC + 1)
                    nc.gpsimd.tensor_tensor(y[:, c, :], y[:, c, :], st[:, i % 4, :], ALU.add).then_inc(y_added, 1)

            def segment(key, between=None, halfway=None):
                first, n = SEGMENTS.get(key, (0, 0))
                if n:
                    inputs(first)
                if between:
                    between()
                for j in range(first, first + n):
                    if j + 1 < first + n:
                        inputs(j + 1)
                    sums(j)
                    if halfway and j == first + n // 2 - 1:
                        halfway()

            pool.wait_ge(setup, 1)
            with pool.Fori(0, B):
                norms[0] = 0
                inverse_roots()
                inverse_roots()
                for l in range(DEPTH):
                    for t in range(NT):
                        segment((l, t), lambda: inverse_norms(l * NT + t))
                    segment((l, "ffn"), halfway=inverse_roots)
                segment("tail")
                pool.wait_ge(y_added, (NS - 1) * IC)
                for f in range(IC):
                    MB.emptied(pool, ("z", f))
                    nc.gpsimd.tensor_tensor(y[:, f, :], y[:, f, :], zs[:, f % 2, :], ALU.mult)\
                        .then_inc(gated_ready, 1)
                end_of_turn(pool, arrived, go["pool"])


QUAD = 4
HALF = KD // 2


def score_quad(j):
    return [2 * (QUAD * (j // 2) + i) + j % 2 for i in range(QUAD)]


def mixer_products():
    out = [(("xT", c), "act") for c in range(HC)] + [(("nT", c), "act") for c in range(HC)]
    out += [(("r",), "dve")] + [(("q", f), "act") for f in range(KC)]
    out += [(("beta",), "act"), (("hl",), "dve"), (("nq",), "dve")]
    out += [(("h", f), "act") for f in range(FFC)] + [(("hzT",), "act")]

    def keys_values(t):
        return [((name, t, i), "act") for name in "kv" for i in range(2)]

    def finish(t):
        return [(("oT", t, i), "act") for i in range(2)] + [(("y", t), "dve")]

    out += keys_values(0)
    for t in range(NT):
        out += [(("kT", t, i), "act") for i in range(2)]
        out += [(("s", t, j), "dve") for j in range(LH // QUAD)]
        out += [((name, t, i), "act") for name in "fg" for i in range(2)]
        out += keys_values(t + 1) if t + 1 < NT else []
        out += finish(t - 1) if t else []
        out += [(("o", t, i), "dve") for i in range(2)]
        out += [(("u", t, i), "dve") for i in range(2)] if t + 1 < NT else []
    return out + finish(NT - 1)


def stage_two(nc, w, mid, result, consts):
    with ExitStack() as ctx:
        def sb(name, shape, dt=F32):
            return ctx.enter_context(nc.sbuf_tensor("two_" + name, shape, dt))

        turn_sems = []

        def sem(name, per_turn=True):
            s = ctx.enter_context(nc.semaphore("two_" + name))
            if per_turn:
                turn_sems.append(s)
            return s

        ps = ctx.enter_context(nc.psum_tensor("two_ps", [P, 8, 512], F32))

        first = CONST_AT["after"][0]
        cst = sb("cst", [P, _at - first])
        ident_sb = sb("ident", [P, P])

        def const(name):
            a, n = CONST_AT[name]
            return cst[:, a - first:a - first + n]

        ident = ident_sb[:]
        wk, wv, wf, wg, wq = [sb("w" + n, [P, HC, KD]) for n in "kvfgq"]
        wb = sb("wb", [P, HC, LH])
        wo = sb("wo", [P, KC, H])
        w1t = sb("w1t", [P, HC, FF])
        w2t = sb("w2t", [P, FFC, H])
        router = sb("router", [P, HC, NB])
        ubasis = sb("ubasis", [P, H])
        uT = sb("uT", [P, HC, NB])
        vbasis = sb("vbasis", [P, H])
        gamma = sb("gamma", [P, H])
        bias3 = sb("bias3", [PART_ROWS, 2 * KD + NB], BF16)
        ones = sb("ones", [PART_ROWS, P], BF16)
        one = sb("one", [P, 1])
        neghalf = sb("neghalf", [P, NT * LH])
        col = sb("col", [P, 2 * HC + 1])
        rate = sb("rate", [P, LH + LH // 2])
        decay_s = sb("decay_s", [P, LH, P])
        decay_q = sb("decay_q", [P, LH // 2, P])
        decay_k = sb("decay_k", [P, LH])
        decay_all = sb("decay_all", [P, LH // 2])
        unit = sb("unit", [P, 4])

        xi = sb("xi", [P, NT, H])
        xn = sb("xn", [P, NT, H])
        zn = sb("zn", [P, NT, H])
        xT = sb("xT", [P, HC, L])
        squares = xn[:, 0, :]
        nT = sb("nT", [P, HC, L])
        qT = sb("qT", [P, KC, L])
        big = sb("big", [P, KC, L])
        rows = big[0:1].rearrange("p c t -> p (c t)")[:, 0:2 * KD + NB]
        rounded = xn[0:1].rearrange("p t h -> p (t h)").bitcast(BF16)[:, 0:HALF]
        beta = sb("beta", [P, NT, LH])
        qnorm = sb("qnorm", [P, NT, LH])
        r = sb("r", [P, NT, NB])
        rest = zn[:, :, 0:NB]
        alpha = zn[:, :, NB:2 * NB]
        top = sb("top", [P, NT, TOPK])
        mass = sb("mass", [P, 4, NT])
        hzT = nT[:, 0, :]
        k = sb("k", [P, 2, KD])
        v = sb("v", [P, 2, KD])
        vt = sb("vt", [P, KD])
        sqs = sb("sqs", [P, KD])
        kn = sb("kn", [P, LH])
        on = sb("on", [P, LH])
        kT = sb("kT", [P, KC, P])
        qd = sb("qd", [P, KC, P])
        sm = sb("sm", [P, LH, P])
        g = sb("g", [P, KD])
        gate = sb("gate", [P, KD])
        state = sb("state", [P, LH // 2, LD])
        o = sb("o", [P, KD])
        oT = sb("oT", [P, KC, P])
        stat = sb("stat", [P, NT, 6])
        mv = sb("mv", [P, NT, 2])
        var = sb("var", [P, NT])
        rstd = sb("rstd", [P, NT])

        wload = sem("wload", False)
        memset_done = sem("memset_done", False)
        prep = {e: sem("prep_" + e, False) for e in ("act", "dve", "pool", "pe")}
        setup_chain = sem("setup_chain", False)
        arrived = sem("arrived")
        go = {e: sem("go_" + e, False) for e in ("pe", "act", "dve", "pool")}
        BK = Banks(mixer_products(), [ps[:, i, :] for i in range(8)], sem("filled"),
                   {"act": sem("act_emptied"), "dve": sem("dve_emptied")})

        x_loaded = sem("x_loaded")
        stored = sem("stored")
        dve_chain = sem("dve_chain")
        pool_chain = sem("pool_chain")
        var_ready = sem("var_ready")
        rstd_ready = sem("rstd_ready")
        xn_ready = sem("xn_ready")
        zn_ready = sem("zn_ready")
        qsq_ready = sem("qsq_ready")
        qnorm_ready = sem("qnorm_ready")
        rc_ready = sem("rc_ready")
        er_ready = sem("er_ready")
        alpha_ready = sem("alpha_ready")
        mass_ready = sem("mass_ready")
        tanh_ready = sem("tanh_ready")
        hz_ready = sem("hz_ready")
        ksq_ready = sem("ksq_ready")
        ksum_ready = sem("ksum_ready")
        kn_ready = sem("kn_ready")
        v_ready = sem("v_ready")
        vt_ready = sem("vt_ready")
        qd_ready = sem("qd_ready")
        gq_ready = sem("gq_ready")
        osq_ready = sem("osq_ready")
        osum_ready = sem("osum_ready")
        on_ready = sem("on_ready")
        gated = sem("gated")
        o_ready = sem("o_ready")

        def wide(name):
            return w[name].rearrange("(c p) n -> p c n", p=P)

        weight_loads = [(cst[:], consts[:, first:_at]), (ident, consts[:, 0:P])]
        for dst, name in ((wk, "Wk"), (wv, "Wv"), (wf, "Wf"), (wg, "Wg"), (wq, "Wq"), (wb, "Wb"), (wo, "Wo")):
            weight_loads.append((dst[:], wide("L1_attn_" + name)))
        weight_loads += [(w1t[:], wide("W1_turned")), (w2t[:], wide("W2_turned")), (router[:], wide("router_turned")),
                         (ubasis[:], w["L1_ffn_raw_U"]), (vbasis[:], w["L1_ffn_raw_V"]),
                         (gamma[:], w["L1_ffn_gamma"].rearrange("a b h -> (a b h)").partition_broadcast(P)),
                         (rows[:, 0:KD], w["L1_attn_dt_bias"].unsqueeze(0)),
                         (rows[:, KD:2 * KD], w["L1_attn_bg"].unsqueeze(0)),
                         (rows[:, 2 * KD:], w["L1_ffn_router_b"].unsqueeze(0)),
                         (col[:, 0:HC], w["L1_ffn_ln_g"].rearrange("(c p) -> p c", p=P)),
                         (col[:, HC:2 * HC], w["L1_ffn_ln_b"].rearrange("(c p) -> p c", p=P)),
                         (rate[:, 0:LH], w["L1_attn_A_log"].partition_broadcast(P))]
        for half in range(2):
            part = slice(half * LD, (half + 1) * LD)
            weight_loads += [(col[part, 2 * HC:], w["L1_attn_norm_w"].unsqueeze(1)),
                             (rate[part, LH:], w["L1_attn_A_log"].rearrange("(j s) -> s j", s=2)[half]
                              .partition_broadcast(LD))]
        LOADED = 16 * len(weight_loads)
        mid_rows = mid.rearrange("b (t p) h -> b p t h", p=P)
        out_rows = result.rearrange("b (t p) h -> b p t h", p=P)
        block = ctx.enter_context(nc.Block())

        @block.sync
        def _(sp):
            with nc.allow_non_contiguous_dma(reason="per-feature vectors as columns, once"):
                for dst, src in weight_loads:
                    sp.dma_start(dst, src).then_inc(wload, 16)
            with sp.Fori(0, B) as b:
                sp.dma_start(xi[:], mid_rows[bass.ds(b, 1)].squeeze(0)).then_inc(x_loaded, 16)
                for t in range(NT):
                    BK.emptied(sp, ("y", t))
                    sp.dma_start(out_rows[bass.ds(b, 1)].squeeze(0)[:, t, :], xi[:, t, :]).then_inc(stored, 16)
                sp.wait_ge(stored, 16 * NT)
                sp.wait_ge(arrived, 4)
                for s in turn_sems:
                    sp.sem_clear(s)
                for e in go:
                    sp.sem_inc(go[e], 1)

        @block.tensor
        def _(pe):
            def mm(out, lhsT, rhs, first, last):
                return pe.matmul(out, lhsT, rhs, start=first, stop=last)

            def close(product):
                product.then_inc(BK.filled_sem, 1)

            def turn(key, source, n):
                bank = BK.claim(pe, key)
                for i in range(n):
                    last = pe.transpose(bank[:, i * P:(i + 1) * P], source(i), ident)
                close(last)

            def columns(name, weights, src, n):
                for f in range(n):
                    bank = BK.claim(pe, (name, f))
                    for c in range(HC):
                        last = mm(bank, weights[:, c, f * P:(f + 1) * P], src[:, c, :], c == 0, c == HC - 1)
                    close(last)

            def token_rows(key, t, weights, bias=None):
                bank = BK.claim(pe, key)
                for c in range(HC):
                    last = mm(bank, xT[:, c, t * P:(t + 1) * P], weights[:, c, :], c == 0,
                              c == HC - 1 and bias is None)
                if bias is not None:
                    last = mm(bank, ones[:], bias, False, True)
                close(last)

            def routing():
                BK.emptied(pe, ("nT", HC - 1))
                bank = BK.claim(pe, ("r",))
                for t in range(NT):
                    at = slice(t * P, (t + 1) * P)
                    for c in range(HC):
                        mm(bank[:, at], nT[:, c, at], router[:, c, :], c == 0, False)
                    last = mm(bank[:, at], ones[:], bias3[:, 2 * KD:], False, True)
                close(last)

            def small_products():
                bank = BK.claim(pe, ("beta",))
                for t in range(NT):
                    for c in range(HC):
                        last = mm(bank[:, t * LH:(t + 1) * LH], xT[:, c, t * P:(t + 1) * P], wb[:, c, :],
                                  c == 0, c == HC - 1)
                close(last)
                bank = BK.claim(pe, ("hl",))
                for t in range(NT):
                    at = slice(t * P, (t + 1) * P)
                    for c in range(HC):
                        last = mm(bank[:, at], xT[:, c, at], uT[:, c, :], c == 0, c == HC - 1)
                close(last)
                bank = BK.claim(pe, ("nq",))
                pe.wait_ge(qsq_ready, KC)
                for t in range(NT):
                    for j in range(KC):
                        at = t * LH + 2 * j
                        last = mm(bank[:, at:at + 2], big[:, j, t * P:(t + 1) * P], const("heads"), True, True)
                close(last)

            def keys_values(t):
                for name, weights in (("k", wk), ("v", wv)):
                    for i in range(2):
                        token_rows((name, t, i), t, weights[:, :, i * HALF:(i + 1) * HALF])

            def finish(t):
                pe.wait_ge(o_ready, t + 1)
                for i in range(2):
                    turn(("oT", t, i), lambda c: o[:, (4 * i + c) * P:(4 * i + c + 1) * P], 4)
                bank = BK.claim(pe, ("y", t))[:, 0:H]
                at = slice(t * P, (t + 1) * P)
                BK.emptied(pe, ("oT", t, 1))
                for f in range(FFC):
                    mm(bank, big[:, f, at], w2t[:, f, :], f == 0, False)
                for c in range(KC):
                    mm(bank, oT[:, c, :], wo[:, c, :], False, False)
                close(mm(bank, hzT[:, at], vbasis[:], False, True))

            pe.wait_ge(prep["dve"], 3)
            for c in range(HC):
                last = pe.transpose(ps[:, 0, c * P:(c + 1) * P], ubasis[:, c * P:(c + 1) * P], ident)
            last.then_inc(prep["pe"], 1)
            pe.wait_ge(prep["dve"], 4)
            pe.wait_ge(prep["pool"], 2)
            with pe.Fori(0, B):
                pe.wait_ge(xn_ready, NT)
                for c in range(HC):
                    turn(("xT", c), lambda t: xn[:, t, c * P:(c + 1) * P], NT)
                pe.wait_ge(zn_ready, NT)
                for c in range(HC):
                    turn(("nT", c), lambda t: zn[:, t, c * P:(c + 1) * P], NT)
                BK.emptied(pe, ("xT", HC - 1))
                routing()
                columns("q", wq, xT, KC)
                small_products()
                columns("h", w1t, xT, FFC)
                pe.wait_ge(hz_ready, 1)
                turn(("hzT",), lambda t: rest[:, t, :], NT)
                keys_values(0)
                BK.emptied(pe, ("hzT",))
                for t in range(NT):
                    at = slice(t * P, (t + 1) * P)
                    BK.emptied(pe, ("k", t, 1))
                    for i in range(2):
                        turn(("kT", t, i), lambda c: k[:, t % 2, (4 * i + c) * P:(4 * i + c + 1) * P], 4)
                    BK.emptied(pe, ("kT", t, 1))
                    for j in range(LH // QUAD):
                        bank = BK.claim(pe, ("s", t, j))
                        for i, h in enumerate(score_quad(j)):
                            part = slice(h % 2 * LD, (h % 2 + 1) * LD)
                            last = mm(bank[:, i * P:(i + 1) * P], kT[part, h // 2, :], qT[part, h // 2, at],
                                      True, True)
                        close(last)
                    for name, weights, b0 in (("f", wf, 0), ("g", wg, KD)):
                        for i in range(2):
                            token_rows((name, t, i), t, weights[:, :, i * HALF:(i + 1) * HALF],
                                       bias3[:, b0 + i * HALF:b0 + (i + 1) * HALF])
                    if t + 1 < NT:
                        keys_values(t + 1)
                    if t:
                        finish(t - 1)
                    pe.wait_ge(v_ready, t + 1)
                    BK.emptied(pe, ("s", t, LH // QUAD - 1))
                    if t:
                        pe.wait_ge(qd_ready, t)
                        BK.emptied(pe, ("u", t - 1, 1))
                    for i in range(2):
                        bank = BK.claim(pe, ("o", t, i))
                        part = slice(i * LD, (i + 1) * LD)
                        for j in range(LH // 2):
                            out, h = bank[:, j * LD:(j + 1) * LD], 2 * j + i
                            if t:
                                mm(out, qd[part, j, :], state[part, j, :], True, False)
                            last = mm(out, sm[:, h, :], v[:, t % 2, h * LD:(h + 1) * LD], t == 0, True)
                        close(last)
                    if t + 1 < NT:
                        pe.wait_ge(vt_ready, t + 1)
                        for i in range(2):
                            bank = BK.claim(pe, ("u", t, i))
                            for j in range(4):
                                pair = slice((4 * i + j) * P, (4 * i + j + 1) * P)
                                last = mm(bank[:, j * P:(j + 1) * P], k[:, t % 2, pair], vt[:, pair], True, True)
                            close(last)
                finish(NT - 1)
                end_of_turn(pe, arrived, go["pe"])

        @block.scalar
        def _(act):
            def run(out, src, func, **kw):
                return nc.scalar.activation(out, src, func, **kw)

            def take(dst, key, func, **kw):
                src = BK.filled(act, key)
                if len(dst.shape) == 3:
                    src = src[:, 0:dst.shape[1] * dst.shape[2]].rearrange("p (a b) -> p a b", a=dst.shape[1])
                run(dst, src, func, **kw).then_inc(BK.emptied_sem["act"], 1)

            def keys_values(t):
                if t >= 2:
                    BK.filled(act, ("u", t - 2, 1))
                for name, dst in (("k", k), ("v", v)):
                    for i in range(2):
                        take(dst[:, t % 2, i * HALF:(i + 1) * HALF], (name, t, i), ACT.Silu)

            def finish(t):
                if t:
                    BK.filled(act, ("y", t - 1))
                for i in range(2):
                    take(oT[:, 4 * i:4 * i + 4, :], ("oT", t, i), ACT.Copy)

            act.wait_ge(wload, LOADED)
            act.wait_ge(memset_done, 1)
            run(squares, ubasis[:], ACT.Square, accum_out=unit[:, 0:1]).then_inc(prep["act"], 1)
            act.wait_ge(prep["act"], 1)
            run(squares, vbasis[:], ACT.Square, accum_out=unit[:, 1:2]).then_inc(prep["act"], 1)
            run(rate[:], rate[:], ACT.Exp).then_inc(prep["act"], 1)
            act.wait_ge(prep["dve"], 1)
            for h in range(LH):
                run(decay_s[:, h, :], const("gap"), ACT.Exp, scale=rate[:, h:h + 1])
            for j in range(LH // 2):
                run(decay_q[:, j, :], const("steps"), ACT.Exp, scale=rate[:, LH + j:LH + j + 1])
            run(decay_k[:], rate[:, 0:LH], ACT.Exp, scale=const("tail"))
            run(decay_all[:], rate[:, LH:], ACT.Exp, scale=float(P)).then_inc(prep["act"], 1)
            act.wait_ge(prep["dve"], 4)
            act.wait_ge(prep["pool"], 2)
            with act.Fori(0, B):
                for c in range(HC):
                    take(xT[:, c, :], ("xT", c), ACT.Copy)
                for c in range(HC):
                    take(nT[:, c, :], ("nT", c), ACT.Identity, scale=col[:, c:c + 1], bias=col[:, HC + c:HC + c + 1])
                for f in range(KC):
                    take(qT[:, f, :], ("q", f), ACT.Silu)
                take(beta[:], ("beta",), ACT.Sigmoid)
                act.wait_ge(rc_ready, 1)
                run(alpha, r[:], ACT.Exp).then_inc(er_ready, 1)
                act.wait_ge(er_ready, 1)
                run(alpha, alpha, ACT.Ln, bias=one[:]).then_inc(alpha_ready, 1)
                act.wait_ge(mass_ready, 1)
                run(mass[:, 1, :], mass[:, 0, :], ACT.Tanh).then_inc(tanh_ready, 1)
                for f in range(FFC):
                    take(big[:, f, :], ("h", f), ACT.Gelu)
                take(hzT, ("hzT",), ACT.Copy)
                keys_values(0)
                for t in range(NT):
                    if t:
                        BK.filled(act, ("s", t - 1, LH // QUAD - 1))
                    for i in range(2):
                        take(kT[:, 4 * i:4 * i + 4, :], ("kT", t, i), ACT.Copy)
                    if t:
                        BK.emptied(act, ("o", t - 1, 1))
                    for i in range(2):
                        take(g[:, i * HALF:(i + 1) * HALF], ("f", t, i), ACT.Sigmoid)
                    if t:
                        act.wait_ge(gated, t)
                    for i in range(2):
                        take(gate[:, i * HALF:(i + 1) * HALF], ("g", t, i), ACT.Sigmoid)
                    if t + 1 < NT:
                        keys_values(t + 1)
                    if t:
                        finish(t - 1)
                finish(NT - 1)
                end_of_turn(act, arrived, go["act"])

        @block.vector
        def _(dve):
            chain = Chain(dve, dve_chain)
            norms = [0]

            def tt(out, a, b, op):
                return nc.vector.tensor_tensor(out, a, b, op)

            def by_head(ap):
                return ap.rearrange("p (h d) -> p h d", d=LD)

            def norm(src, dst, signal):
                for t in range(NT):
                    last = nc.vector.bn_stats(stat[:, t, :], src[:, t, :])
                chain(last)
                for t in range(NT):
                    last = nc.vector.bn_aggr(mv[:, t, :], stat[:, t, :])
                chain(last)
                nc.vector.tensor_scalar(var[:], mv[:, :, 1], LN_EPS, None, ALU.add).then_inc(var_ready, 1)
                norms[0] += 1
                dve.wait_ge(rstd_ready, norms[0])
                for t in range(NT):
                    nc.vector.tensor_scalar(dst[:, t, :], src[:, t, :], mv[:, t, 0:1], rstd[:, t:t + 1],
                                            ALU.subtract, ALU.mult).then_inc(signal, 1)

            def route():
                nc.vector.tensor_scalar(r[:], split3(BK.filled(dve, ("r",)), NT), -TAU, TAU, ALU.max, ALU.min)\
                    .then_inc(BK.emptied_sem["dve"], 1)
                BK.emptied(dve, ("r",))
                for t in range(NT):
                    last = nc.vector.max(top[:, t, :], r[:, t, :])
                last.then_inc(rc_ready, 1)
                dve.wait_ge(rc_ready, 1)
                for t in range(NT):
                    last = nc.vector.match_replace(rest[:, t, :], top[:, t, :], r[:, t, :], -1e30)
                chain(last)
                chain(tt(rest, r[:], rest, ALU.not_equal))
                dve.wait_ge(alpha_ready, 1)
                chain(tt(alpha, alpha, rest, ALU.mult))
                nc.vector.reduce_sum(mass[:, 0, :], alpha, AX).then_inc(mass_ready, 1)
                dve.wait_ge(mass_ready, 1)
                chain(nc.vector.tensor_scalar(mass[:, 2, :], mass[:, 0, :], UNIT_EPS, None, ALU.add))
                chain(nc.vector.reciprocal(mass[:, 3, :], mass[:, 2, :]))
                tt(rest, split3(BK.filled(dve, ("hl",)), NT), alpha, ALU.mult)\
                    .then_inc(BK.emptied_sem["dve"], 1)
                dve.wait_ge(tanh_ready, 1)
                chain(tt(mass[:, 3, :], mass[:, 3, :], mass[:, 1, :], ALU.mult))
                BK.emptied(dve, ("hl",))
                tt(rest, rest, spread(mass[:, 3, :], [P, NT, NB]), ALU.mult).then_inc(hz_ready, 1)

            def add_result(t):
                tt(xi[:, t, :], xi[:, t, :], BK.filled(dve, ("y", t))[:, 0:H], ALU.add)\
                    .then_inc(BK.emptied_sem["dve"], 1)

            def output_sums(t):
                dve.wait_ge(osq_ready, t + 1)
                nc.vector.reduce_sum(on[:], by_head(sqs[:]), AX).then_inc(osum_ready, 1)

            def output_norm(t):
                dve.wait_ge(gated, t + 1)
                dve.wait_ge(on_ready, t + 1)
                tt(by_head(o[:]), by_head(o[:]), spread(on[:], [P, LH, LD]), ALU.mult).then_inc(o_ready, 1)

            dve.memset(one[:], 1.0)
            dve.memset(ones[:], 1.0)
            prepare = Chain(dve, setup_chain)
            prepare(dve.memset(bias3[:], 0.0))
            dve.memset(neghalf[:], -0.5).then_inc(memset_done, 1)
            dve.wait_ge(wload, LOADED)
            dve.wait_ge(prep["act"], 3)
            nc.vector.tensor_scalar(rate[:], rate[:], -1.0, -1e30, ALU.mult, ALU.max).then_inc(prep["dve"], 1)
            nc.vector.tensor_scalar(unit[:, 2:4], unit[:, 0:2], UNIT_EPS * UNIT_EPS, None, ALU.max)\
                .then_inc(prep["dve"], 1)
            prepare(nc.vector.tensor_scalar(rows[:, 0:KD], rows[:, 0:KD], -1.0, None, ALU.mult))
            for at in range(0, 2 * KD + NB, HALF):
                cut = slice(at, min(at + HALF, 2 * KD + NB))
                piece = rounded[:, 0:cut.stop - cut.start]
                for i in range(3):
                    prepare(nc.vector.tensor_copy(piece, rows[:, cut]))
                    prepare(nc.vector.tensor_copy(bias3[32 * i:32 * i + 1, cut], piece))
                    prepare(tt(rows[:, cut], rows[:, cut], piece, ALU.subtract))
            nc.vector.tensor_scalar(wo[:], wo[:], col[:, 2 * HC:2 * HC + 1], None, ALU.mult)
            dve.wait_ge(prep["pool"], 1)
            nc.vector.scalar_tensor_tensor(out=vbasis[:], in0=vbasis[:], scalar=unit[:, 1:2], in1=gamma[:],
                                           op0=ALU.mult, op1=ALU.mult)
            nc.vector.tensor_scalar(ubasis[:], ubasis[:], unit[:, 0:1], None, ALU.mult).then_inc(prep["dve"], 1)
            dve.wait_ge(prep["pe"], 1)
            nc.vector.tensor_copy(uT[:], ps[:, 0, 0:HC * NB].rearrange("p (c n) -> p c n", c=HC))\
                .then_inc(prep["dve"], 1)
            dve.wait_ge(prep["dve"], 4)
            dve.wait_ge(prep["pool"], 2)
            with dve.Fori(0, B):
                chain.count = norms[0] = 0
                dve.wait_ge(x_loaded, 16)
                norm(xi, xn, xn_ready)
                dve.wait_ge(xn_ready, NT)
                norm(xn, zn, zn_ready)
                route()
                nc.vector.tensor_scalar(qnorm[:].rearrange("p t h -> p (t h)"), BK.filled(dve, ("nq",))[:, 0:NT * LH],
                                        1e-24, None, ALU.max).then_inc(BK.emptied_sem["dve"], 1)
                for t in range(NT):
                    if t:
                        output_sums(t - 1)
                    dve.wait_ge(ksq_ready, t + 1)
                    if t:
                        dve.wait_ge(vt_ready, t)
                    nc.vector.reduce_sum(kn[:], by_head(sqs[:]), AX).then_inc(ksum_ready, 1)
                    for j in range(LH // QUAD):
                        bank = split3(BK.filled(dve, ("s", t, j)), QUAD)
                        if t:
                            BK.filled(dve, ("o", t - 1, 1))
                        first, last = score_quad(j)[0], score_quad(j)[-1]
                        tt(sm[:, first:last + 1:2, :], bank, decay_s[:, first:last + 1:2, :], ALU.mult)\
                            .then_inc(BK.emptied_sem["dve"], 1)
                    if t:
                        output_norm(t - 1)
                    dve.wait_ge(kn_ready, t + 1)
                    BK.emptied(dve, ("v", t, 1))
                    rows_v = by_head(v[:, t % 2, :])
                    tt(rows_v, rows_v, spread(kn[:], [P, LH, LD]), ALU.mult).then_inc(v_ready, 1)
                    if t:
                        add_result(t - 1)
                        BK.filled(dve, ("oT", t - 1, 1))
                    dve.wait_ge(gq_ready, t + 1)
                    for i in range(2):
                        out = by_head(o[:])[:, i:LH:2, :]
                        tt(out, by_head(BK.filled(dve, ("o", t, i))), by_head(g[:])[:, i:LH:2, :], ALU.mult)\
                            .then_inc(BK.emptied_sem["dve"], 1)
                    if t + 1 < NT:
                        if t:
                            chain(tt(state[:], state[:], spread(decay_all[:], [P, LH // 2, LD]), ALU.mult))
                        for i in range(2):
                            bank = split3(BK.filled(dve, ("u", t, i)), 4)
                            for half in range(2):
                                part = slice(half * LD, (half + 1) * LD)
                                dst, src = state[part, 4 * i:4 * i + 4, :], bank[part, :, half * LD:(half + 1) * LD]
                                if t:
                                    ins = tt(dst, dst, src, ALU.add)
                                else:
                                    ins = nc.vector.tensor_copy(dst, src)
                            ins.then_inc(BK.emptied_sem["dve"], 1)
                output_sums(NT - 1)
                output_norm(NT - 1)
                add_result(NT - 1)
                end_of_turn(dve, arrived, go["dve"])

        @block.gpsimd
        def _(pool):
            steps = Chain(pool, pool_chain)
            norms = [0]

            def tt(out, a, b, op):
                return nc.gpsimd.tensor_tensor(out, a, b, op)

            def by_head(ap):
                return ap.rearrange("p (h d) -> p h d", d=LD)

            def inverse_roots():
                norms[0] += 1
                pool.wait_ge(var_ready, norms[0])
                tt(rstd[:], var[:], neghalf[:, 0:NT], ALU.pow).then_inc(rstd_ready, 1)

            def output_squares(t):
                BK.emptied(pool, ("o", t, 1))
                tt(sqs[:], o[:], o[:], ALU.mult).then_inc(osq_ready, 1)

            def output_gates(t):
                pool.wait_ge(osq_ready, t + 1)
                BK.emptied(pool, ("g", t, 1))
                tt(o[:], o[:], gate[:], ALU.mult).then_inc(gated, 1)
                pool.wait_ge(osum_ready, t + 1)
                steps(nc.gpsimd.tensor_scalar(on[:], on[:], 1.0 / LD, 1e-5, ALU.mult, ALU.add))
                tt(on[:], on[:], neghalf[:, 0:LH], ALU.pow).then_inc(on_ready, 1)

            pool.wait_ge(prep["dve"], 2)
            tt(unit[:, 0:2], unit[:, 2:4], neghalf[:, 0:2], ALU.pow).then_inc(prep["pool"], 1)
            pool.wait_ge(prep["act"], 4)
            tt(decay_s[:], decay_s[:], const("after").unsqueeze(1).to_broadcast([P, LH, P]), ALU.mult)\
                .then_inc(prep["pool"], 1)
            pool.wait_ge(prep["pool"], 2)
            with pool.Fori(0, B):
                steps.count = norms[0] = 0
                inverse_roots()
                inverse_roots()
                for f in range(KC):
                    BK.emptied(pool, ("q", f))
                    tt(big[:, f, :], qT[:, f, :], qT[:, f, :], ALU.mult).then_inc(qsq_ready, 1)
                BK.emptied(pool, ("nq",))
                flat = qnorm[:].rearrange("p t h -> p (t h)")
                tt(flat, flat, neghalf[:], ALU.pow).then_inc(qnorm_ready, 1)
                pool.wait_ge(qnorm_ready, 1)
                for t in range(NT):
                    if t:
                        output_squares(t - 1)
                        output_gates(t - 1)
                    BK.emptied(pool, ("k", t, 1))
                    tt(sqs[:], k[:, t % 2, :], k[:, t % 2, :], ALU.mult).then_inc(ksq_ready, 1)
                    if t:
                        BK.filled(pool, ("o", t - 1, 1))
                        tt(qd[:], qT[:, :, t * P:(t + 1) * P], decay_q[:], ALU.mult).then_inc(qd_ready, 1)
                    pool.wait_ge(ksum_ready, t + 1)
                    steps(nc.gpsimd.tensor_scalar(kn[:], kn[:], 1e-24, None, ALU.max))
                    steps(tt(kn[:], kn[:], neghalf[:, 0:LH], ALU.pow))
                    tt(kn[:], kn[:], beta[:, t, :], ALU.mult).then_inc(kn_ready, 1)
                    BK.emptied(pool, ("f", t, 1))
                    tt(by_head(g[:]), by_head(g[:]), spread(qnorm[:, t, :], [P, LH, LD]), ALU.mult)\
                        .then_inc(gq_ready, 1)
                    if t + 1 < NT:
                        pool.wait_ge(v_ready, t + 1)
                        if t:
                            BK.filled(pool, ("u", t - 1, 1))
                        tt(by_head(vt[:]), by_head(v[:, t % 2, :]), spread(decay_k[:], [P, LH, LD]), ALU.mult)\
                            .then_inc(vt_ready, 1)
                output_squares(NT - 1)
                output_gates(NT - 1)
                end_of_turn(pool, arrived, go["pool"])


def kernel(**inputs):
    import concourse.bacc as bacc
    from concourse.bass_utils import run_bass_kernel_spmd

    nc = bacc.Bacc("TRN2", target_bir_lowering=False, num_devices=1)
    arrays, aps = {}, {}

    def given(name, value):
        a = np.ascontiguousarray(value)
        arrays[f"in_{name}"] = a
        aps[name] = nc.dram_tensor(f"in_{name}", a.shape, mybir.dt.from_np(a.dtype), kind="ExternalInput").ap()

    turned = {"L1_ffn_W1": "W1_turned", "L1_ffn_W2": "W2_turned", "L1_ffn_router_W": "router_turned"}
    for name, value in inputs.items():
        if name in turned:
            given(turned[name], np.asarray(value).T)
        else:
            given(name, value)
    given("shape_constants", shape_constants())
    mid = nc.dram_tensor("mid", (B, L, H), F32, kind="Internal").ap()
    result = nc.dram_tensor("result", (B, L, H), F32, kind="ExternalOutput").ap()
    stage_one(nc, aps, mid, aps["shape_constants"])
    stage_two(nc, aps, mid, result, aps["shape_constants"])
    r = run_bass_kernel_spmd(nc, [arrays], core_ids=[0])
    return r.results[0]["result"]
```

```python
from contextlib import ExitStack

import numpy as np
import concourse.bass as bass
from concourse import mybir

F32 = mybir.dt.float32
BF16 = mybir.dt.bfloat16
ACT = mybir.ActivationFunctionType
ALU = mybir.AluOpType
AX = mybir.AxisListType.X

P = 128
B, L, H = 8, 512, 256
NT = L // P
HC = H // P
LN_EPS = 1e-5
PART_ROWS = 65

INNER, NS, CONV, DTR = 512, 16, 4, 16
IC = INNER // P
DEPTH, NH, DH, WIN = 2, 8, 64, 128
FI = NH * DH
FC = FI // P
HID = int(H * 4 * 2 / 3)
UC = -(-HID // P)
LAST = HID - (UC - 1) * P
QK_SCALE = 8.0
LH, LD = 16, 64
KD = LH * LD
KC = KD // P
NB, FF, TOPK, TAU, UNIT_EPS = 128, 1024, 8, 10.0, 1e-6
FFC = FF // P


def shape_constants():
    half = np.arange(0, DH, 2, dtype=np.float32)
    inv = (1.0 / 10000.0 ** (half / DH)).astype(np.float32)
    t = np.arange(L, dtype=np.float32)
    freqs = t[:, None] * inv[None, :]
    freqs = np.concatenate([freqs, freqs], -1)
    base = (half + np.float32(0.4 * DH)) / np.float32(1.4 * DH)
    power = (t - L // 2) / np.float32(WIN // 2)
    scale = base[None, :] ** power[:, None]
    scale = np.concatenate([scale, scale], -1)
    sign = np.where(np.arange(DH) < DH // 2, -1.0, 1.0).astype(np.float32)
    cos, sin = np.cos(freqs), np.sin(freqs) * sign
    rope = np.stack([cos * scale * QK_SCALE, sin * scale * QK_SCALE, cos / scale, sin / scale])
    rope = rope.reshape(4, NT, P, DH).transpose(2, 0, 1, 3)
    i = np.arange(P)
    far = -3.0e38
    window = np.stack([np.where(i[None, :] >= i[:, None], 0.0, far), np.where(i[None, :] <= i[:, None], 0.0, far)], 1)
    after = (i[None, :] > i[:, None]).astype(np.float32)
    gap = np.maximum(i[None, :] - 1 - i[:, None], 0)
    steps = np.broadcast_to(i[None, :], (P, P))
    tail = (P - 1 - i)[:, None]
    heads = (i[:, None] // LD == np.arange(2)[None, :])
    parts = [np.eye(P), rope, window, after, gap, steps, tail, heads]
    return np.concatenate([p.reshape(P, -1) for p in parts], 1).astype(np.float32)


CONST_AT = {}
_at = 0
for _name, _n in (("ident", P), ("rope", 4 * NT * DH), ("window", 2 * P), ("after", P), ("gap", P), ("steps", P),
                  ("tail", 1), ("heads", 2)):
    CONST_AT[_name] = (_at, _n)
    _at += _n


class Banks:

    def __init__(self, products, banks, filled, emptied):
        self.banks, self.filled_sem, self.emptied_sem = banks, filled, emptied
        self.place, self.by, self.nth, count = {}, [], [], {}
        for i, (key, engine) in enumerate(products):
            assert key not in self.place, key
            self.place[key] = i
            count[engine] = count.get(engine, 0) + 1
            self.by.append(engine)
            self.nth.append(count[engine])

    def bank(self, key):
        return self.banks[self.place[key] % len(self.banks)]

    def claim(self, pe, key):
        before = self.place[key] - len(self.banks)
        if before >= 0:
            pe.wait_ge(self.emptied_sem[self.by[before]], self.nth[before])
        return self.bank(key)

    def filled(self, eng, key):
        eng.wait_ge(self.filled_sem, self.place[key] + 1)
        return self.bank(key)

    def emptied(self, eng, key):
        i = self.place[key]
        eng.wait_ge(self.emptied_sem[self.by[i]], self.nth[i])


class Chain:

    def __init__(self, eng, sem):
        self.eng, self.sem, self.count = eng, sem, 0

    def __call__(self, instruction):
        self.count += 1
        instruction.then_inc(self.sem, 1)
        self.eng.wait_ge(self.sem, self.count)


def split3(ap, n):
    return ap.rearrange("p (a b) -> p a b", a=n)


def spread(column, shape):
    return column.unsqueeze(2).to_broadcast(shape)


def end_of_turn(eng, arrived, go):
    eng.drain().then_inc(arrived, 1)
    eng.wait_ge(go, 1)
    eng.sem_clear(go)


ATT = [(l, t) for l in range(DEPTH) for t in range(NT)]
PAIRS = FC
STEPS = [(n, c) for n in range(NS) for c in range(IC)]
PLACES = [(0, t, i) for t in range(1, NT) for i in range(2)] + ["ffn", "layer"] \
    + [(1, t, i) for t in range(NT) for i in range(2)]
ROW_AT = {place: n for n, place in enumerate(PLACES)}
assert len(PLACES) == NS


def score_heads(p):
    return [4 * (p // 2) + 2 * i + p % 2 for i in range(2)]


def block_products():
    out = [(("hT", 0, t), "act") for t in range(NT)]
    out += [(("q", 0, 0), "dve"), (("k", 0, 0), "dve"), (("v", 0, 0), "act")]
    for l in range(DEPTH):
        out += [(("qT", l, 0), "act"), (("kT", l, 0), "act")]
        for t in range(NT):
            ahead = t + 1 < NT
            out += [(("s", l, t, p), "dve") for p in range(PAIRS)]
            out += [(("q", l, t + 1), "dve"), (("k", l, t + 1), "dve")] if ahead else []
            out += [(("pT", l, t, p), "act") for p in range(PAIRS)] + [(("o", l, t), "dve")]
            out += [(("v", l, t + 1), "act")] if ahead else []
            out += [(("oT", l, t), "act")]
            out += [(("qT", l, t + 1), "act"), (("kT", l, t + 1), "act")] if ahead else []
            out += [(("wo", l, t), "dve")]
        out += [(("nT", l, t), "act") for t in range(NT)]
        for f in range(UC):
            out += [(("gate", l, f), "act"), (("up", l, f), "dve")]
        if l + 1 < DEPTH:
            n = l + 1
            out += [(("down", l, 0), "dve"), (("down", l, 1), "dve"), (("hT", n, 0), "act"), (("down", l, 2), "dve"),
                    (("q", n, 0), "dve"), (("k", n, 0), "dve"), (("down", l, 3), "dve"), (("v", n, 0), "act"),
                    (("hT", n, 1), "act"), (("hT", n, 2), "act"), (("hT", n, 3), "act")]
        else:
            out += [(("down", l, t), "dve") for t in range(NT)]
    return out


def ssm_products():
    out = [(("zT", c), "act") for c in range(HC)]
    out += [(("xb", f), "act") for f in range(IC)] + [(("z", f), "act") for f in range(IC)]
    out += [(("B",), "act"), (("C",), "act"), (("R",), "act")]
    out += [(("dt", c), "dve") for c in range(IC)] + [(("mean",), "dve")]
    for n in range(NS):
        out += [(("Brow", n), "act"), (("Crow", n), "dve")]
    return out + [(("ssm", i), "dve") for i in range(NT // 2)]


def stage_one(nc, w, mid, consts):
    with ExitStack() as ctx:
        def sb(name, shape, dt=F32):
            return ctx.enter_context(nc.sbuf_tensor("one_" + name, shape, dt))

        turn_sems = []

        def sem(name, per_turn=True):
            s = ctx.enter_context(nc.semaphore("one_" + name))
            if per_turn:
                turn_sems.append(s)
            return s

        ps = ctx.enter_context(nc.psum_tensor("one_ps", [P, 8, 512], F32))

        ident = sb("ident", [P, P])[:]
        window = sb("window", [P, 2 * P])
        in_w = sb("in_w", [P, HC, 2 * INNER])
        out_w = sb("out_w", [P, IC, H])
        bc_w = sb("bc_w", [P, IC, 2 * NS])
        dtr_w = sb("dtr_w", [P, IC, DTR])
        dt_w = sb("dt_w", [DTR, INNER])
        out_b = sb("out_b", [1, H])
        ones = sb("ones", [1, P])
        wqkv = sb("wqkv", [P, DEPTH, HC, 3 * FI])
        wo = sb("wo", [P, DEPTH, FC, H])
        w1 = sb("w1", [P, DEPTH, HC, 2 * HID])
        w2 = sb("w2", [P, DEPTH, UC, H])
        col = sb("col", [P, 64])
        cols, at = {}, 0
        for name, n in (("norm_w", HC), ("norm_b", HC), ("in_b", 2 * IC), ("conv_b", IC), ("dt_b", IC),
                        ("ln_g", DEPTH * HC), ("ln_b", DEPTH * HC), ("b1", DEPTH * 2 * UC)):
            cols[name] = col[:, at:at + n]
            at += n
        conv_w = sb("conv_w", [P, IC, CONV])
        small_b = sb("small_b", [NS, 3])
        scales = sb("scales", [P, 2, DEPTH, DH])
        rope = sb("rope", [P, DEPTH, 4, NT, DH])
        mean_w = sb("mean_w", [P, NS])
        neghalf = sb("neghalf", [P, 8])
        one = sb("one", [P, 1])
        zeros = sb("zeros", [1, P])
        zero_row = zeros[0:1, :]

        xf = sb("xf", [P, NT, H])
        xs = sb("xs", [P, NT, H])
        hT = sb("hT", [P, HC * (L + 1)])
        hT_write = hT[:, :].rearrange("p (c t) -> p c t", c=HC)[:, :, 0:L]
        qk = sb("qk", [P, 2, FI])
        vv = sb("vv", [P, 2, FI])
        qT = sb("qT", [P, PAIRS, P])
        kT = sb("kT", [P, 2, PAIRS, P])
        sm = sb("sm", [P, PAIRS, 2, 2 * P])
        hid = sb("hid", [P, UC * L])
        pT = hid[:, 0:NH * 2 * P].rearrange("p (h k q) -> p h k q", h=NH, k=2)
        u = hid[:, :].rearrange("p (f t) -> p f t", f=UC)
        rope_table = hid[:, 0:4 * NT * DH]
        scratch = sb("scratch", [P, 2, L])
        sq, turned, gl = scratch[:, 0, :], scratch[:, 1, :], scratch
        orow = sb("orow", [P, FI])
        oT = sb("oT", [P, FC, P])
        stat = sb("stat", [P, NT, 6])
        mv = sb("mv", [P, NT, 2])
        var = sb("var", [P, NT])
        rstd = sb("rstd", [P, NT])
        ssq = sb("ssq", [P, 2, NH])
        rnorm = sb("rnorm", [P, 2, NH])
        nmax = sb("nmax", [P, PAIRS, 2])
        rsum = sb("rsum", [P, 2, NH])
        rinv = sb("rinv", [P, NH])

        xb = sb("xb", [P, IC, L + CONV - 1])
        y = sb("y", [P, IC, L])
        xa = sb("xa", [P, IC, L])
        dt = sb("dt", [P, IC, L])
        bcr = sb("bcr", [NS, 3, L])
        rounded = bcr[:, 2, :].bitcast(BF16).rearrange("p (i t) -> p i t", i=2)
        left = scratch[0:NS]
        bc3 = sb("bc3", [64 + NS, 2, L], BF16)
        pick3 = sb("pick3", [64 + NS, NS], BF16)
        brow = sb("brow", [P, 2, L])
        decay = sb("decay", [P, 4, L])
        zT = decay[:, 0:HC, :]
        st = sb("st", [P, 4, L])

        wload = sem("wload", False)
        setup = sem("setup", False)
        setup_chain = sem("setup_chain", False)
        arrived = sem("arrived")
        go = {e: sem("go_" + e, False) for e in ("pe", "act", "dve", "pool")}

        FB = Banks(block_products(), [ps[:, i, :] for i in range(5)], sem("blk_filled"),
                   {"act": sem("blk_act_emptied"), "dve": sem("blk_dve_emptied")})
        MB = Banks(ssm_products(), [ps[:, 5 + i, :] for i in range(3)], sem("ssm_filled"),
                   {"act": sem("ssm_act_emptied"), "dve": sem("ssm_dve_emptied")})

        x_loaded = sem("x_loaded")
        stored = sem("stored")
        shifted = [[sem(f"shifted_{l}_{t}") for t in range(NT)] for l in range(DEPTH)]
        x_again = sem("x_again")
        dve_chain = sem("dve_chain")
        pool_chain = sem("pool_chain")
        var_ready = sem("var_ready")
        rstd_ready = sem("rstd_ready")
        xn_ready = sem("xn_ready")
        zn_ready = sem("zn_ready")
        sq_ready = sem("sq_ready")
        ssq_ready = sem("ssq_ready")
        rnorm_ready = sem("rnorm_ready")
        qk_ready = sem("qk_ready")
        smax_ready = sem("smax_ready")
        p_ready = sem("p_ready")
        n_ready = sem("n_ready")
        conv_ready = sem("conv_ready")
        xa_ready = sem("xa_ready")
        pre_ready = sem("pre_ready")
        e_ready = sem("e_ready")
        sp_ready = sem("sp_ready")
        dt_ready = sem("dt_ready")
        bc_split = sem("bc_split")
        decay_ready = sem("decay_ready")
        bx_ready = sem("bx_ready")
        scanned = sem("scanned")
        hc_ready = sem("hc_ready")
        y_added = sem("y_added")
        gated_ready = sem("gated_ready")

        def const(name):
            a, n = CONST_AT[name]
            return consts[:, a:a + n]

        weight_loads = [
            (ident, const("ident")), (window[:], const("window")), (rope_table, const("rope")), (in_w[:], w["L0_attn_in_w"].rearrange("(c p) n -> p c n", p=P)),
            (out_w[:], w["L0_attn_out_w"].rearrange("(c p) n -> p c n", p=P)),
            (bc_w[:], w["L0_attn_bc_w"].rearrange("(c p) n -> p c n", p=P)),
            (dtr_w[:], w["L0_attn_dtr_w"].rearrange("(c p) n -> p c n", p=P)),
            (dt_w[:], w["L0_attn_dt_w"]), (out_b[:], w["L0_attn_out_b"].unsqueeze(0)),
            (conv_w[:], w["L0_attn_conv_w"].rearrange("(c p) k -> p c k", p=P)),
            (small_b[:, 0:1], w["L0_attn_bc_b"][0:NS].unsqueeze(1)),
            (small_b[:, 1:2], w["L0_attn_bc_b"][NS:2 * NS].unsqueeze(1)),
            (small_b[:, 2:3], w["L0_attn_dtr_b"].unsqueeze(1)),
            (scales[:, 0, :, :], w["L0_ffn_q_scale"].partition_broadcast(P)),
            (scales[:, 1, :, :], w["L0_ffn_k_scale"].partition_broadcast(P)),
        ]
        for name in ("norm_w", "norm_b", "in_b", "conv_b", "dt_b"):
            weight_loads.append((cols[name], w["L0_attn_" + name].rearrange("(c p) -> p c", p=P)))
        for l in range(DEPTH):
            weight_loads += [
                (wqkv[:, l], w["L0_ffn_wqkv"][l].rearrange("(c p) n -> p c n", p=P)),
                (wo[:, l], w["L0_ffn_wo"][l].rearrange("(c p) n -> p c n", p=P)),
                (w1[:, l], w["L0_ffn_w1"][l].rearrange("(c p) n -> p c n", p=P)),
                (w2[:, l, 0:UC - 1], w["L0_ffn_w2"][l, 0:(UC - 1) * P].rearrange("(c p) n -> p c n", p=P)),
                (w2[0:LAST, l, UC - 1], w["L0_ffn_w2"][l, (UC - 1) * P:HID]),
                (w2[LAST:LAST + 1, l, UC - 1], w["L0_ffn_b2"][l:l + 1]),
                (cols["ln_g"][:, l * HC:(l + 1) * HC], w["L0_ffn_ln_g"][l].rearrange("(c p) -> p c", p=P)),
                (cols["ln_b"][:, l * HC:(l + 1) * HC], w["L0_ffn_ln_b"][l].rearrange("(c p) -> p c", p=P)),
            ]
            for part in range(2):
                at, b1 = (2 * l + part) * UC, w["L0_ffn_b1"][l, part * HID:(part + 1) * HID]
                weight_loads += [
                    (cols["b1"][:, at:at + UC - 1], b1[0:(UC - 1) * P].rearrange("(c p) -> p c", p=P)),
                    (cols["b1"][0:LAST, at + UC - 1:at + UC], b1[(UC - 1) * P:HID].unsqueeze(1)),
                ]

        x_rows = w["L0_attn_x"].rearrange("b (t p) h -> b p t h", p=P)
        mid_rows = mid.rearrange("b (t p) h -> b p t h", p=P)
        block = ctx.enter_context(nc.Block())

        @block.sync
        def _(sp):
            with nc.allow_non_contiguous_dma(reason="per-feature vectors as columns, once"):
                for dst, src in weight_loads:
                    sp.dma_start(dst, src).then_inc(wload, 16)
            with sp.Fori(0, B) as b:
                sp.dma_start(xs[:], x_rows[bass.ds(b, 1)].squeeze(0)).then_inc(x_loaded, 16)
                for l in range(DEPTH):
                    for t in range(NT):
                        FB.emptied(sp, ("wo", l, t))
                        if l == 0 and t == 0:
                            MB.filled(sp, ("zT", HC - 1))
                        sp.dma_start(xs[:, t, 0:P], xf[:, t, 0:P]).then_inc(shifted[l][t], 16)
                        sp.dma_start(xs[1:P, t, P:H], xf[0:P - 1, t, P:H]).then_inc(shifted[l][t], 16)
                        before = xf[P - 1:P, t - 1, P:H] if t else zero_row
                        sp.dma_start(xs[0:1, t, P:H], before).then_inc(shifted[l][t], 16)
                FB.filled(sp, ("nT", DEPTH - 1, NT - 1))
                sp.dma_start(xs[:], x_rows[bass.ds(b, 1)].squeeze(0)).then_inc(x_again, 16)
                for t in range(NT):
                    FB.emptied(sp, ("down", DEPTH - 1, t))
                    sp.dma_start(mid_rows[bass.ds(b, 1)].squeeze(0)[:, t, :], xf[:, t, :]).then_inc(stored, 16)
                sp.wait_ge(stored, 16 * NT)
                sp.wait_ge(arrived, 4)
                for s in turn_sems:
                    sp.sem_clear(s)
                for e in go:
                    sp.sem_inc(go[e], 1)


        @block.tensor
        def _(pe):
            def mm(out, lhsT, rhs, first, last):
                return pe.matmul(out, lhsT, rhs, start=first, stop=last)

            def close(product, banks):
                product.then_inc(banks.filled_sem, 1)

            def turn(banks, key, source, n):
                bank = banks.claim(pe, key)
                for i in range(n):
                    last = pe.transpose(bank[:, i * P:(i + 1) * P], source(i), ident)
                close(last, banks)

            def ssm_inputs():
                pe.wait_ge(zn_ready, NT)
                for c in range(HC):
                    turn(MB, ("zT", c), lambda t: xs[:, t, c * P:(c + 1) * P], NT)
                MB.emptied(pe, ("zT", HC - 1))
                ssm_project("xb", 0)

            def ssm_project(name, first_chunk):
                for f in range(IC):
                    bank = MB.claim(pe, (name, f))
                    at = (first_chunk + f) * P
                    for c in range(HC):
                        last = mm(bank, in_w[:, c, at:at + P], zT[:, c, :], c == 0, c == HC - 1)
                    close(last, MB)

            def ssm_rows():
                pe.wait_ge(xa_ready, IC)
                for key, wt in ((("B",), bc_w[:, :, 0:NS]), (("C",), bc_w[:, :, NS:2 * NS]), (("R",), dtr_w[:])):
                    bank = MB.claim(pe, key)
                    for c in range(IC):
                        last = mm(bank[0:NS, :], wt[:, c, :], xa[:, c, :], c == 0, c == IC - 1)
                    close(last, MB)

            def ssm_rates():
                MB.emptied(pe, ("R",))
                for c in range(IC):
                    bank = MB.claim(pe, ("dt", c))
                    close(mm(bank, dt_w[:, c * P:(c + 1) * P], bcr[:, 2, :], True, True), MB)

            def ssm_mean():
                bank = MB.claim(pe, ("mean",))
                pe.wait_ge(dt_ready, IC)
                for c in range(IC):
                    last = mm(bank[0:NS, :], mean_w[:], dt[:, c, :], c == 0, c == IC - 1)
                close(last, MB)

            def ssm_row(place):
                if place not in ROW_AT:
                    return
                n = ROW_AT[place]
                if n == 0:
                    pe.wait_ge(bc_split, 1)
                pick = pick3[:, n:n + 1].to_broadcast([64 + NS, P])
                for i, name in enumerate(("Brow", "Crow")):
                    bank = MB.claim(pe, (name, n))
                    close(mm(bank, pick, bc3[:, i, :], True, True), MB)

            def features(l, t):
                if l == 0:
                    pe.wait_ge(xn_ready, t + 1)
                else:
                    FB.emptied(pe, ("down", l - 1, t))
                turn(FB, ("hT", l, t), lambda c: xf[:, t, c * P:(c + 1) * P], HC)

            def project(l, t, names):
                FB.emptied(pe, ("hT", l, t))
                for name in names:
                    i = "qkv".index(name)
                    bank = FB.claim(pe, (name, l, t))
                    for c in range(HC):
                        last = mm(bank, hT[:, c * L + t * P:c * L + (t + 1) * P], wqkv[:, l, c, i * FI:(i + 1) * FI],
                                  c == 0, c == HC - 1)
                    close(last, FB)

            def turn_qk(l, t):
                g = l * NT + t
                for i, name in enumerate(("qT", "kT")):
                    pe.wait_ge(qk_ready, 2 * g + i + 1)
                    turn(FB, (name, l, t), lambda p: qk[:, i, p * P:(p + 1) * P], PAIRS)

            def scores(l, t):
                g = l * NT + t
                FB.emptied(pe, ("kT", l, t))
                if t == 0:
                    FB.emptied(pe, ("qT", l, t))
                for p in range(0, PAIRS, 2):
                    banks = [split3(FB.claim(pe, ("s", l, t, p + i)), 2) for i in range(2)]
                    for h in range(2):
                        for k in range(0 if t else 1, 2):
                            for i in range(2):
                                head = score_heads(p + i)[h]
                                rows = slice(i * DH, (i + 1) * DH)
                                last = mm(banks[i][:, h, k * P:(k + 1) * P], qT[rows, head // 2, :],
                                          kT[rows, (g + k - 1) % 2, head // 2, :], True, True)
                                if h == 1 and k == 1:
                                    close(last, FB)

            def turn_p(l, t):
                g = l * NT + t
                for p in range(PAIRS):
                    bank = FB.claim(pe, ("pT", l, t, p)).rearrange("p (h k q) -> p h k q", h=2, k=2)
                    pe.wait_ge(p_ready, g * PAIRS + p + 1)
                    for h in range(2):
                        for k in range(0 if t else 1, 2):
                            last = pe.transpose(bank[:, h, k, :], sm[:, p, h, k * P:(k + 1) * P], ident)
                    close(last, FB)

            def attend(l, t):
                g = l * NT + t
                bank = FB.claim(pe, ("o", l, t))
                FB.emptied(pe, ("pT", l, t, PAIRS - 1))
                for h in range(NH):
                    for k in range(0 if t else 1, 2):
                        last = mm(bank[:, h * DH:(h + 1) * DH], pT[:, h, k, :],
                                  vv[:, (g + k - 1) % 2, h * DH:(h + 1) * DH], k == 0 or t == 0, k == 1)
                close(last, FB)

            def turn_o(l, t):
                FB.emptied(pe, ("o", l, t))
                turn(FB, ("oT", l, t), lambda c: orow[:, c * P:(c + 1) * P], FC)

            def attend_out(l, t):
                bank = FB.claim(pe, ("wo", l, t))
                FB.emptied(pe, ("oT", l, t))
                for c in range(FC):
                    last = mm(bank[:, 0:H], oT[:, c, :], wo[:, l, c, :], c == 0, c == FC - 1)
                close(last, FB)

            def ffn_in(l, t):
                pe.wait_ge(n_ready, l * NT + t + 1)
                turn(FB, ("nT", l, t), lambda c: xs[:, t, c * P:(c + 1) * P], HC)

            def ffn_hidden(l, f):
                if f == 0:
                    FB.emptied(pe, ("nT", l, NT - 1))
                m = P if f < UC - 1 else LAST
                for name, at in (("gate", HID), ("up", 0)):
                    bank = FB.claim(pe, (name, l, f))
                    for c in range(HC):
                        last = mm(bank[0:m, :], w1[:, l, c, at + f * P:at + f * P + m], hT_write[:, c, :],
                                  c == 0, c == HC - 1)
                    close(last, FB)

            def ffn_down(l, t):
                FB.emptied(pe, ("up", l, UC - 1))
                bank = FB.claim(pe, ("down", l, t))
                for f in range(UC):
                    m = P if f < UC - 1 else LAST + 1
                    last = mm(bank[:, 0:H], u[0:m, f, t * P:(t + 1) * P], w2[0:m, l, f, :], f == 0, f == UC - 1)
                close(last, FB)

            def ssm_out():
                pe.wait_ge(gated_ready, IC)
                for i in range(NT // 2):
                    bank = MB.claim(pe, ("ssm", i))
                    for t in (2 * i, 2 * i + 1):
                        out = bank[:, (t % 2) * H:(t % 2 + 1) * H]
                        for c in range(IC):
                            mm(out, y[:, c, t * P:(t + 1) * P], out_w[:, c, :], c == 0, False)
                        last = mm(out, ones[:], out_b[:], False, True)
                    close(last, MB)

            pe.wait_ge(wload, 16 * len(weight_loads))
            pe.wait_ge(setup, 1)
            with pe.Fori(0, B):
                for t in range(NT):
                    features(0, t)
                project(0, 0, "qkv")
                ssm_inputs()
                for l in range(DEPTH):
                    turn_qk(l, 0)
                    for t in range(NT):
                        scores(l, t)
                        ssm_row((l, t, 0))
                        if t + 1 < NT:
                            project(l, t + 1, "qk")
                        if (l, t) == (0, 0):
                            ssm_project("z", IC)
                        turn_p(l, t)
                        if (l, t) == (0, 0):
                            ssm_rows()
                        ssm_row((l, t, 1))
                        attend(l, t)
                        if t + 1 < NT:
                            project(l, t + 1, "v")
                        turn_o(l, t)
                        if (l, t) == (0, 0):
                            ssm_rates()
                        if t + 1 < NT:
                            turn_qk(l, t + 1)
                        attend_out(l, t)
                        if (l, t) == (0, 0):
                            ssm_mean()
                    for t in range(NT - 1):
                        ffn_in(l, t)
                    if l == 0:
                        ssm_row("ffn")
                    else:
                        ssm_out()
                    ffn_in(l, NT - 1)
                    for f in range(UC):
                        ffn_hidden(l, f)
                    if l + 1 < DEPTH:
                        n = l + 1
                        ffn_down(l, 0)
                        ffn_down(l, 1)
                        features(n, 0)
                        ffn_down(l, 2)
                        project(n, 0, "qk")
                        ffn_down(l, 3)
                        project(n, 0, "v")
                        for t in range(1, NT):
                            features(n, t)
                        ssm_row("layer")
                    else:
                        for t in range(NT):
                            ffn_down(l, t)
                end_of_turn(pe, arrived, go["pe"])


        @block.scalar
        def _(act):
            def run(out, src, func, **kw):
                return nc.scalar.activation(out, src, func, **kw)

            def free(instruction, banks):
                instruction.then_inc(banks.emptied_sem["act"], 1)

            def ssm_inputs():
                for c in range(HC):
                    free(run(zT[:, c, :], MB.filled(act, ("zT", c)), ACT.Identity,
                             scale=cols["norm_w"][:, c:c + 1], bias=cols["norm_b"][:, c:c + 1]), MB)
                for f in range(IC):
                    free(run(xb[:, f, CONV - 1:], MB.filled(act, ("xb", f)), ACT.Identity,
                             bias=cols["in_b"][:, f:f + 1]), MB)

            def ssm_silus():
                for f in range(IC):
                    act.wait_ge(conv_ready, (CONV - 1) * IC + f + 1)
                    run(xa[:, f, :], y[:, f, :], ACT.Silu).then_inc(xa_ready, 1)
                for f in range(IC):
                    free(run(xb[:, f, CONV - 1:], MB.filled(act, ("z", f)), ACT.Silu,
                             bias=cols["in_b"][:, IC + f:IC + f + 1]), MB)

            def ssm_rows():
                for i, name in enumerate("BCR"):
                    free(run(bcr[:, i, :], MB.filled(act, (name,))[0:NS, :], ACT.Identity,
                             bias=small_b[:, i:i + 1]), MB)

            def ssm_rates():
                for c in range(IC):
                    MB.emptied(act, ("dt", c))
                    run(dt[:, c, :], dt[:, c, :], ACT.Exp).then_inc(e_ready, 1)
                for c in range(IC):
                    act.wait_ge(e_ready, c + 1)
                    run(dt[:, c, :], dt[:, c, :], ACT.Ln, bias=one[:]).then_inc(sp_ready, 1)

            def take_row(place):
                if place not in ROW_AT:
                    return
                n = ROW_AT[place]
                src = MB.filled(act, ("Brow", n))
                if n >= 2:
                    act.wait_ge(bx_ready, IC * (n - 1))
                free(run(brow[:, n % 2, :], src, ACT.Copy), MB)

            def decays(place, half=None):
                if place not in ROW_AT:
                    return
                n = ROW_AT[place]
                for c in range(IC) if half is None else range(2 * half, 2 * half + 2):
                    i = n * IC + c
                    if i == 0:
                        act.wait_ge(dt_ready, IC)
                    if i >= 4:
                        act.wait_ge(scanned, i - 3)
                    run(decay[:, i % 4, :], dt[:, c, :], ACT.Exp, scale=-(n + 1.0)).then_inc(decay_ready, 1)

            def features(l, t):
                src = FB.filled(act, ("hT", l, t))[:, 0:HC * P]
                free(run(hT_write[:, :, t * P:(t + 1) * P], split3(src, HC), ACT.Copy), FB)

            def square(l, t, i):
                g = l * NT + t
                bank = FB.filled(act, ("qk"[i], l, t))
                if 2 * g + i >= 1:
                    act.wait_ge(ssq_ready, 2 * g + i)
                if t == 0 and l and i == 0:
                    FB.emptied(act, ("up", l - 1, UC - 1))
                run(sq, bank, ACT.Square).then_inc(sq_ready, 1)

            def values(l, t):
                free(run(vv[:, (l * NT + t) % 2, :], FB.filled(act, ("v", l, t)), ACT.Copy), FB)

            def turned_qk(l, t):
                for key, dst in ((("qT", l, t), qT[:]), (("kT", l, t), kT[:, (l * NT + t) % 2])):
                    free(run(dst, split3(FB.filled(act, key), PAIRS), ACT.Copy), FB)

            def attention(l, t):
                g = l * NT + t
                lo = 0 if t else P

                def exps(p):
                    act.wait_ge(smax_ready, g * PAIRS + p + 1)
                    for h, head in enumerate(score_heads(p)):
                        s = sm[:, p, h, lo:2 * P]
                        last = run(s, s, ACT.Exp, bias=nmax[:, p, h:h + 1],
                                   accum_out=rsum[:, g % 2, head:head + 1])
                    last.then_inc(p_ready, 1)

                def take(p):
                    src = FB.filled(act, ("pT", l, t, p)).rearrange("p (h k q) -> p h k q", h=2, k=2)
                    k = 0 if t else 1
                    first, last = score_heads(p)
                    free(run(pT[:, first:last + 1:2, k:2, :], src[:, :, k:2, :], ACT.Copy), FB)

                decays((l, t, 0))
                for p in range(PAIRS):
                    exps(p)
                    if p == 1:
                        take_row((l, t, 0))
                if t + 1 < NT:
                    square(l, t + 1, 0)
                take(0)
                take(1)
                if t + 1 < NT:
                    square(l, t + 1, 1)
                take(2)
                take(3)
                if (l, t) == (0, 0):
                    ssm_rows()
                take_row((l, t, 1))
                decays((l, t, 1), 0)
                if t + 1 < NT:
                    values(l, t + 1)
                decays((l, t, 1), 1)
                free(run(oT[:], split3(FB.filled(act, ("oT", l, t)), FC), ACT.Copy), FB)
                if (l, t) == (0, 0):
                    ssm_rates()
                if t + 1 < NT:
                    turned_qk(l, t + 1)

            def ffn_features(l, t):
                src = FB.filled(act, ("nT", l, t))
                for c in range(HC):
                    at = l * HC + c
                    last = run(hT_write[:, c, t * P:(t + 1) * P], src[:, c * P:(c + 1) * P], ACT.Identity,
                               scale=cols["ln_g"][:, at:at + 1], bias=cols["ln_b"][:, at:at + 1])
                free(last, FB)

            def ffn_gates(l):
                for f in range(UC):
                    m = P if f < UC - 1 else LAST
                    at = (2 * l + 1) * UC + f
                    src = FB.filled(act, ("gate", l, f))
                    if f >= 2:
                        FB.emptied(act, ("up", l, f - 2))
                    free(run(gl[0:m, f % 2, :], src[0:m, :], ACT.Gelu, bias=cols["b1"][0:m, at:at + 1]), FB)

            act.wait_ge(wload, 16 * len(weight_loads))
            act.wait_ge(setup, 1)
            with act.Fori(0, B):
                for t in range(NT):
                    features(0, t)
                square(0, 0, 0)
                square(0, 0, 1)
                values(0, 0)
                ssm_inputs()
                turned_qk(0, 0)
                ssm_silus()
                for l in range(DEPTH):
                    for t in range(NT):
                        attention(l, t)
                    for t in range(NT - 1):
                        ffn_features(l, t)
                    if l == 0:
                        take_row("ffn")
                        decays("ffn")
                    ffn_features(l, NT - 1)
                    ffn_gates(l)
                    if l + 1 < DEPTH:
                        n = l + 1
                        features(n, 0)
                        square(n, 0, 0)
                        square(n, 0, 1)
                        values(n, 0)
                        for t in range(1, NT):
                            features(n, t)
                        take_row("layer")
                        decays("layer")
                        turned_qk(n, 0)
                end_of_turn(act, arrived, go["act"])

        @block.vector
        def _(dve):
            chain = Chain(dve, dve_chain)
            norms = [0]

            def tt(out, a, b, op):
                return nc.vector.tensor_tensor(out, a, b, op)

            def norm(src, dst, signal, tiles=range(NT)):
                cut = slice(tiles[0], tiles[-1] + 1)
                for t in tiles:
                    last = nc.vector.bn_stats(stat[:, t, :], src[:, t, :])
                chain(last)
                for t in tiles:
                    last = nc.vector.bn_aggr(mv[:, t, :], stat[:, t, :])
                chain(last)
                nc.vector.tensor_scalar(var[:, cut], mv[:, cut, 1], LN_EPS, None, ALU.add).then_inc(var_ready, 1)
                norms[0] += 1
                dve.wait_ge(rstd_ready, norms[0])
                for t in tiles:
                    nc.vector.tensor_scalar(dst[:, t, :], src[:, t, :], mv[:, t, 0:1], rstd[:, t:t + 1],
                                            ALU.subtract, ALU.mult).then_inc(signal, 1)

            def convolve():
                for k in range(CONV):
                    for f in range(IC):
                        if k == 0:
                            MB.emptied(dve, ("xb", f))
                            ins = nc.vector.tensor_scalar(y[:, f, :], xb[:, f, 0:L], conv_w[:, f, 0:1],
                                                          cols["conv_b"][:, f:f + 1], ALU.mult, ALU.add)
                        else:
                            dve.wait_ge(conv_ready, (k - 1) * IC + f + 1)
                            ins = nc.vector.scalar_tensor_tensor(
                                out=y[:, f, :], in0=xb[:, f, k:k + L], scalar=conv_w[:, f, k:k + 1],
                                in1=y[:, f, :], op0=ALU.mult, op1=ALU.add)
                        ins.then_inc(conv_ready, 1)

            def rate_inputs():
                for c in range(IC):
                    nc.vector.tensor_scalar(dt[:, c, :], MB.filled(dve, ("dt", c)), cols["dt_b"][:, c:c + 1],
                                            20.0, ALU.add, ALU.min).then_inc(MB.emptied_sem["dve"], 1)

            def clip_rates():
                for c in range(IC):
                    dve.wait_ge(sp_ready, c + 1)
                    nc.vector.tensor_scalar(dt[:, c, :], dt[:, c, :], 0.001, 0.1, ALU.max, ALU.min)\
                        .then_inc(dt_ready, 1)

            def split_rows():
                MB.emptied(dve, ("B",))
                tt(bcr[:, 0, :], bcr[:, 0, :], MB.filled(dve, ("mean",))[0:NS, :], ALU.mult)\
                    .then_inc(MB.emptied_sem["dve"], 1)
                MB.emptied(dve, ("mean",))
                rows = bcr[:, 0:2, :]
                chain(nc.vector.tensor_copy(bc3[0:NS], rows))
                chain(tt(left, rows, bc3[0:NS], ALU.subtract))
                chain(nc.vector.tensor_copy(rounded, left))
                nc.vector.tensor_copy(bc3[32:32 + NS], rounded)
                tt(bc3[64:64 + NS], left, rounded, ALU.subtract).then_inc(bc_split, 1)

            def scans(place, halves=(0, 1)):
                if place not in ROW_AT:
                    return
                for half in halves:
                    first = ROW_AT[place] * IC + 2 * half
                    pair = (first, first + 1)
                    for i in pair:
                        dve.wait_ge(decay_ready, i + 1)
                        dve.wait_ge(bx_ready, i + 1)
                        s = st[:, i % 4, :]
                        nc.vector.tensor_tensor_scan(s, decay[:, i % 4, :], s, 0.0, ALU.mult, ALU.add)\
                            .then_inc(scanned, 1)
                    for i in pair:
                        n, c = STEPS[i]
                        crow = MB.filled(dve, ("Crow", n))
                        dve.wait_ge(scanned, i + 1)
                        dst = y[:, c, :] if n == 0 else st[:, i % 4, :]
                        ins = tt(dst, st[:, i % 4, :], crow, ALU.mult)
                        ins.then_inc(MB.emptied_sem["dve"] if c == IC - 1 else hc_ready, 1)

            def rotate(l, t):
                g = l * NT + t
                for i, name in enumerate("qk"):
                    bank = FB.filled(dve, (name, l, t))
                    if g:
                        FB.filled(dve, (name + "T",) + ATT[g - 1])
                    heads = bank.rearrange("p (h d) -> p h d", h=NH)
                    swapped = bank.rearrange("p (h s d) -> p h s d", h=NH, s=2)[:, :, ::-1, :]
                    cos = rope[:, l, 2 * i, t, :].unsqueeze(1).to_broadcast([P, NH, DH])
                    sin = split3(rope[:, l, 2 * i + 1, t, :], 2).unsqueeze(1).to_broadcast([P, NH, 2, DH // 2])
                    rows = qk[:, i, :].rearrange("p (h d) -> p h d", h=NH)
                    dve.wait_ge(sq_ready, 2 * g + i + 1)
                    tt(rows, heads, cos, ALU.mult)
                    tt(turned.rearrange("p (h s d) -> p h s d", h=NH, s=2), swapped, sin, ALU.mult)\
                        .then_inc(FB.emptied_sem["dve"], 1)
                    nc.vector.reduce_sum(ssq[:, i, :], sq.rearrange("p (h d) -> p h d", h=NH), AX)\
                        .then_inc(ssq_ready, 1)
                    FB.emptied(dve, (name, l, t))
                    chain(tt(qk[:, i, :], qk[:, i, :], turned, ALU.add))

            def normalize(l, t):
                g = l * NT + t
                for i in range(2):
                    rows = qk[:, i, :].rearrange("p (h d) -> p h d", h=NH)
                    dve.wait_ge(rnorm_ready, 2 * g + i + 1)
                    tt(rows, rows, spread(rnorm[:, i, :], [P, NH, DH]), ALU.mult).then_inc(qk_ready, 1)

            def attention(l, t):
                g = l * NT + t
                lo = 0 if t else P
                for p in range(PAIRS):
                    bank = split3(FB.filled(dve, ("s", l, t, p)), 2)
                    if g:
                        FB.filled(dve, ("pT",) + ATT[g - 1] + (p,))
                    s = sm[:, p, :, lo:2 * P]
                    tt(s, bank[:, :, lo:2 * P], window[:, lo:2 * P].unsqueeze(1)
                       .to_broadcast([P, 2, 2 * P - lo]), ALU.add).then_inc(FB.emptied_sem["dve"], 1)
                    FB.emptied(dve, ("s", l, t, p))
                    nc.vector.tensor_reduce(nmax[:, p, :], s, AX, ALU.max, negate=True).then_inc(smax_ready, 1)
                if t + 1 < NT:
                    rotate(l, t + 1)
                scans((l, t, 0), (0,))
                if t + 1 < NT:
                    normalize(l, t + 1)
                scans((l, t, 0), (1,))
                if t == NT - 1:
                    ffn_norm(l, range(NT - 1))
                dve.wait_ge(p_ready, (g + 1) * PAIRS)
                chain(nc.vector.reciprocal(rinv[:], rsum[:, g % 2, :]))
                bank = FB.filled(dve, ("o", l, t))
                if g:
                    FB.filled(dve, ("oT",) + ATT[g - 1])
                tt(orow[:].rearrange("p (h d) -> p h d", h=NH), bank.rearrange("p (h d) -> p h d", h=NH),
                   spread(rinv[:], [P, NH, DH]), ALU.mult).then_inc(FB.emptied_sem["dve"], 1)
                scans((l, t, 1), (0,))
                if (l, t) == (0, 0):
                    rate_inputs()
                add_rows(("wo", l, t), t)
                scans((l, t, 1), (1,))
                if (l, t) == (0, 0):
                    clip_rates()
                    split_rows()

            def add_rows(key, t):
                tt(xf[:, t, :], xf[:, t, :], FB.filled(dve, key)[:, 0:H], ALU.add)\
                    .then_inc(FB.emptied_sem["dve"], 1)

            def ffn_norm(l, tiles):
                for t in tiles:
                    dve.wait_ge(shifted[l][t], 16 * 3)
                norm(xs, xs, n_ready, tiles)

            def hidden(l, f):
                m = P if f < UC - 1 else LAST
                at = 2 * l * UC + f
                bank = FB.filled(dve, ("up", l, f))
                FB.emptied(dve, ("gate", l, f))
                nc.vector.scalar_tensor_tensor(
                    out=u[0:m, f, :], in0=bank[0:m, :], scalar=cols["b1"][0:m, at:at + 1],
                    in1=gl[0:m, f % 2, :], op0=ALU.add, op1=ALU.mult).then_inc(FB.emptied_sem["dve"], 1)

            def add_ssm():
                for i in range(NT // 2):
                    pair = slice(2 * i, 2 * i + 2)
                    tt(xf[:, pair, :], xf[:, pair, :], split3(MB.filled(dve, ("ssm", i)), 2), ALU.add)\
                        .then_inc(MB.emptied_sem["dve"], 1)

            dve.memset(xb[:], 0.0)
            dve.memset(hT[:], 0.0)
            dve.memset(hid[32:64, (UC - 1) * L:UC * L], 1.0)
            dve.memset(zeros[:], 0.0)
            prepare = Chain(dve, setup_chain)
            prepare(dve.memset(bc3[:], 0.0))
            prepare(dve.memset(pick3[:], 0.0))
            dve.memset(ones[:], 1.0)
            dve.memset(one[:], 1.0)
            dve.memset(neghalf[:], -0.5)
            dve.memset(mean_w[:], 1.0 / INNER)
            dve.wait_ge(wload, 16 * len(weight_loads))
            for i in range(3):
                nc.vector.tensor_copy(pick3[32 * i:32 * i + NS, :], ident[0:NS, 0:NS])
            table = rope_table.rearrange("p (k t d) -> p k t d", k=4, t=NT)
            for l in range(DEPTH):
                for i in range(2):
                    s = scales[:, i, l, :]
                    flip = split3(s, 2)[:, ::-1, :]
                    tt(rope[:, l, 2 * i], table[:, 2 * i], s.unsqueeze(1).to_broadcast([P, NT, DH]), ALU.mult)
                    for t in range(NT):
                        ins = tt(split3(rope[:, l, 2 * i + 1, t], 2), split3(table[:, 2 * i + 1, t], 2), flip,
                                 ALU.mult)
            ins.then_inc(setup, 1)
            dve.wait_ge(setup, 1)
            with dve.Fori(0, B):
                chain.count = norms[0] = 0
                dve.wait_ge(x_loaded, 16)
                norm(xs, xf, xn_ready)
                dve.wait_ge(xn_ready, NT)
                norm(xf, xs, zn_ready)
                rotate(0, 0)
                normalize(0, 0)
                convolve()
                for l in range(DEPTH):
                    for t in range(NT):
                        attention(l, t)
                    ffn_norm(l, range(NT - 1, NT))
                    if l == 0:
                        scans("ffn", (0,))
                        hidden(l, 0)
                        scans("ffn", (1,))
                        for f in range(1, UC):
                            hidden(l, f)
                        add_rows(("down", l, 0), 0)
                        add_rows(("down", l, 1), 1)
                        add_rows(("down", l, 2), 2)
                        rotate(1, 0)
                        add_rows(("down", l, 3), 3)
                        normalize(1, 0)
                        scans("layer")
                    else:
                        add_ssm()
                        for f in range(UC):
                            hidden(l, f)
                            if f == 3:
                                dve.wait_ge(x_again, 16)
                                MB.emptied(dve, ("ssm", NT // 2 - 1))
                                chain(tt(xf[:], xf[:], xs[:], ALU.add))
                        for t in range(NT):
                            add_rows(("down", l, t), t)
                end_of_turn(dve, arrived, go["dve"])

        @block.gpsimd
        def _(pool):
            norms, tiles = [0], [0]

            def inverse_roots(first=0, last=NT):
                norms[0] += 1
                pool.wait_ge(var_ready, norms[0])
                nc.gpsimd.tensor_tensor(rstd[:, first:last], var[:, first:last], neghalf[:, first:last], ALU.pow)\
                    .then_inc(rstd_ready, 1)

            def inverse_norms(g):
                for i in range(2):
                    pool.wait_ge(ssq_ready, 2 * g + i + 1)
                    nc.gpsimd.tensor_scalar(ssq[:, i, :], ssq[:, i, :], 1e-24, None, ALU.max)\
                        .then_inc(pool_chain, 1)
                    pool.wait_ge(pool_chain, 2 * g + i + 1)
                    nc.gpsimd.tensor_tensor(rnorm[:, i, :], ssq[:, i, :], neghalf[:], ALU.pow)\
                        .then_inc(rnorm_ready, 1)

            def inputs(j):
                for i in (2 * j, 2 * j + 1):
                    n, c = STEPS[i]
                    MB.emptied(pool, ("Brow", n))
                    if i >= 4 + IC:
                        pool.wait_ge(y_added, i - 4 - IC + 1)
                    nc.gpsimd.tensor_tensor(st[:, i % 4, :], brow[:, n % 2, :], xa[:, c, :], ALU.mult)\
                        .then_inc(bx_ready, 1)

            def product_ready(i):
                n, c = STEPS[i]
                if c == IC - 1:
                    MB.emptied(pool, ("Crow", n))
                else:
                    pool.wait_ge(hc_ready, n * (IC - 1) + c + 1)

            def sums(j):
                for i in (2 * j, 2 * j + 1):
                    n, c = STEPS[i]
                    product_ready(i)
                    if n == 0:
                        continue
                    if n >= 2:
                        pool.wait_ge(y_added, i - 2 * IC + 1)
                    nc.gpsimd.tensor_tensor(y[:, c, :], y[:, c, :], st[:, i % 4, :], ALU.add).then_inc(y_added, 1)

            def row_inputs(place, half):
                if place in ROW_AT:
                    inputs(2 * ROW_AT[place] + half)

            def row_sums(place, half):
                if place in ROW_AT:
                    sums(2 * ROW_AT[place] + half)

            pool.wait_ge(setup, 1)
            with pool.Fori(0, B):
                norms[0] = 0
                inverse_roots()
                inverse_roots()
                inverse_norms(0)
                for l in range(DEPTH):
                    for t in range(NT):
                        row_inputs((l, t, 0), 0)
                        row_inputs((l, t, 0), 1)
                        if t + 1 < NT:
                            inverse_norms(l * NT + t + 1)
                        row_sums((l, t, 0), 0)
                        row_inputs((l, t, 1), 0)
                        row_sums((l, t, 0), 1)
                        if t == NT - 1:
                            inverse_roots(0, NT - 1)
                        row_inputs((l, t, 1), 1)
                        row_sums((l, t, 1), 0)
                        row_sums((l, t, 1), 1)
                    if l == 0:
                        inverse_roots(NT - 1, NT)
                        row_inputs("ffn", 0)
                        row_inputs("ffn", 1)
                        row_sums("ffn", 0)
                        row_sums("ffn", 1)
                        inverse_norms(NT)
                        row_inputs("layer", 0)
                        row_inputs("layer", 1)
                        row_sums("layer", 0)
                        row_sums("layer", 1)
                pool.wait_ge(y_added, (NS - 1) * IC)
                for f in range(IC):
                    MB.emptied(pool, ("z", f))
                    nc.gpsimd.tensor_tensor(y[:, f, :], y[:, f, :], xb[:, f, CONV - 1:], ALU.mult)\
                        .then_inc(gated_ready, 1)
                inverse_roots(NT - 1, NT)
                end_of_turn(pool, arrived, go["pool"])


QUAD = 4
HALF = KD // 2


def score_quad(j):
    return [2 * (QUAD * (j // 2) + i) + j % 2 for i in range(QUAD)]


def mixer_products():
    out = [(("xT", c), "act") for c in range(HC)] + [(("nT", c), "act") for c in range(HC)]
    out += [(("r",), "dve")] + [(("q", f), "act") for f in range(KC)]
    out += [(("beta",), "act"), (("hl",), "dve"), (("nq",), "dve")]
    out += [(("h", f), "act") for f in range(FFC)] + [(("hzT",), "act")]

    def keys_values(t):
        return [((name, t, i), "act") for name in "kv" for i in range(2)]

    def finish(t):
        return [(("oT", t, i), "act") for i in range(2)] + [(("y", t), "dve")]

    out += keys_values(0)
    for t in range(NT):
        out += [(("kT", t, i), "act") for i in range(2)]
        out += [(("s", t, j), "dve") for j in range(LH // QUAD)]
        out += [((name, t, i), "act") for name in "fg" for i in range(2)]
        out += keys_values(t + 1) if t + 1 < NT else []
        out += finish(t - 1) if t else []
        out += [(("o", t, i), "dve") for i in range(2)]
        out += [(("u", t, i), "dve") for i in range(2)] if t + 1 < NT else []
    return out + finish(NT - 1)


def stage_two(nc, w, mid, result, consts):
    with ExitStack() as ctx:
        def sb(name, shape, dt=F32):
            return ctx.enter_context(nc.sbuf_tensor("two_" + name, shape, dt))

        turn_sems = []

        def sem(name, per_turn=True):
            s = ctx.enter_context(nc.semaphore("two_" + name))
            if per_turn:
                turn_sems.append(s)
            return s

        ps = ctx.enter_context(nc.psum_tensor("two_ps", [P, 8, 512], F32))

        first = CONST_AT["after"][0]
        cst = sb("cst", [P, _at - first])
        ident_sb = sb("ident", [P, P])

        def const(name):
            a, n = CONST_AT[name]
            return cst[:, a - first:a - first + n]

        ident = ident_sb[:]
        wk, wv, wf, wg, wq = [sb("w" + n, [P, HC, KD]) for n in "kvfgq"]
        wb = sb("wb", [P, HC, LH])
        wo = sb("wo", [P, KC, H])
        w1t = sb("w1t", [P, HC, FF])
        w2t = sb("w2t", [P, FFC, H])
        router = sb("router", [P, HC, NB])
        ubasis = sb("ubasis", [P, H])
        uT = sb("uT", [P, HC, NB])
        vbasis = sb("vbasis", [P, H])
        gamma = sb("gamma", [P, H])
        bias3 = sb("bias3", [PART_ROWS, 2 * KD + NB], BF16)
        ones = sb("ones", [PART_ROWS, P], BF16)
        one = sb("one", [P, 1])
        neghalf = sb("neghalf", [P, NT * LH])
        col = sb("col", [P, 2 * HC + 1])
        rate = sb("rate", [P, LH + LH // 2])
        decay_s = sb("decay_s", [P, LH, P])
        decay_q = sb("decay_q", [P, LH // 2, P])
        decay_k = sb("decay_k", [P, LH])
        decay_all = sb("decay_all", [P, LH // 2])
        unit = sb("unit", [P, 4])

        xi = sb("xi", [P, NT, H])
        xn = sb("xn", [P, NT, H])
        zn = sb("zn", [P, NT, H])
        xT = sb("xT", [P, HC, L])
        squares = xn[:, 0, :]
        nT = sb("nT", [P, HC, L])
        qT = sb("qT", [P, KC, L])
        big = sb("big", [P, KC, L])
        rows = big[0:1].rearrange("p c t -> p (c t)")[:, 0:2 * KD + NB]
        rounded = xn[0:1].rearrange("p t h -> p (t h)").bitcast(BF16)[:, 0:HALF]
        beta = sb("beta", [P, NT, LH])
        qnorm = sb("qnorm", [P, NT, LH])
        r = sb("r", [P, NT, NB])
        rest = zn[:, :, 0:NB]
        alpha = zn[:, :, NB:2 * NB]
        top = sb("top", [P, NT, TOPK])
        mass = sb("mass", [P, 4, NT])
        hzT = nT[:, 0, :]
        k = sb("k", [P, 2, KD])
        v = sb("v", [P, 2, KD])
        vt = sb("vt", [P, KD])
        sqs = sb("sqs", [P, KD])
        kn = sb("kn", [P, LH])
        on = sb("on", [P, LH])
        kT = sb("kT", [P, KC, P])
        qd = sb("qd", [P, KC, P])
        sm = sb("sm", [P, LH, P])
        g = sb("g", [P, KD])
        gate = sb("gate", [P, KD])
        state = sb("state", [P, LH // 2, LD])
        o = sb("o", [P, KD])
        oT = sb("oT", [P, KC, P])
        stat = sb("stat", [P, NT, 6])
        mv = sb("mv", [P, NT, 2])
        var = sb("var", [P, NT])
        rstd = sb("rstd", [P, NT])

        wload = sem("wload", False)
        memset_done = sem("memset_done", False)
        prep = {e: sem("prep_" + e, False) for e in ("act", "dve", "pool", "pe")}
        setup_chain = sem("setup_chain", False)
        arrived = sem("arrived")
        go = {e: sem("go_" + e, False) for e in ("pe", "act", "dve", "pool")}
        BK = Banks(mixer_products(), [ps[:, i, :] for i in range(8)], sem("filled"),
                   {"act": sem("act_emptied"), "dve": sem("dve_emptied")})

        x_loaded = sem("x_loaded")
        stored = sem("stored")
        dve_chain = sem("dve_chain")
        pool_chain = sem("pool_chain")
        var_ready = sem("var_ready")
        rstd_ready = sem("rstd_ready")
        xn_ready = sem("xn_ready")
        zn_ready = sem("zn_ready")
        qsq_ready = sem("qsq_ready")
        qnorm_ready = sem("qnorm_ready")
        rc_ready = sem("rc_ready")
        er_ready = sem("er_ready")
        alpha_ready = sem("alpha_ready")
        mass_ready = sem("mass_ready")
        tanh_ready = sem("tanh_ready")
        hz_ready = sem("hz_ready")
        ksq_ready = sem("ksq_ready")
        ksum_ready = sem("ksum_ready")
        kn_ready = sem("kn_ready")
        v_ready = sem("v_ready")
        vt_ready = sem("vt_ready")
        qd_ready = sem("qd_ready")
        gq_ready = sem("gq_ready")
        osq_ready = sem("osq_ready")
        osum_ready = sem("osum_ready")
        on_ready = sem("on_ready")
        gated = sem("gated")
        o_ready = sem("o_ready")

        def wide(name):
            return w[name].rearrange("(c p) n -> p c n", p=P)

        weight_loads = [(cst[:], consts[:, first:_at]), (ident, consts[:, 0:P])]
        for dst, name in ((wk, "Wk"), (wv, "Wv"), (wf, "Wf"), (wg, "Wg"), (wq, "Wq"), (wb, "Wb"), (wo, "Wo")):
            weight_loads.append((dst[:], wide("L1_attn_" + name)))
        weight_loads += [(w1t[:], wide("W1_turned")), (w2t[:], wide("W2_turned")), (router[:], wide("router_turned")),
                         (ubasis[:], w["L1_ffn_raw_U"]), (vbasis[:], w["L1_ffn_raw_V"]),
                         (gamma[:], w["L1_ffn_gamma"].rearrange("a b h -> (a b h)").partition_broadcast(P)),
                         (rows[:, 0:KD], w["L1_attn_dt_bias"].unsqueeze(0)),
                         (rows[:, KD:2 * KD], w["L1_attn_bg"].unsqueeze(0)),
                         (rows[:, 2 * KD:], w["L1_ffn_router_b"].unsqueeze(0)),
                         (col[:, 0:HC], w["L1_ffn_ln_g"].rearrange("(c p) -> p c", p=P)),
                         (col[:, HC:2 * HC], w["L1_ffn_ln_b"].rearrange("(c p) -> p c", p=P)),
                         (rate[:, 0:LH], w["L1_attn_A_log"].partition_broadcast(P))]
        for half in range(2):
            part = slice(half * LD, (half + 1) * LD)
            weight_loads += [(col[part, 2 * HC:], w["L1_attn_norm_w"].unsqueeze(1)),
                             (rate[part, LH:], w["L1_attn_A_log"].rearrange("(j s) -> s j", s=2)[half]
                              .partition_broadcast(LD))]
        LOADED = 16 * len(weight_loads)
        mid_rows = mid.rearrange("b (t p) h -> b p t h", p=P)
        out_rows = result.rearrange("b (t p) h -> b p t h", p=P)
        block = ctx.enter_context(nc.Block())

        @block.sync
        def _(sp):
            with nc.allow_non_contiguous_dma(reason="per-feature vectors as columns, once"):
                for dst, src in weight_loads:
                    sp.dma_start(dst, src).then_inc(wload, 16)
            with sp.Fori(0, B) as b:
                sp.dma_start(xi[:], mid_rows[bass.ds(b, 1)].squeeze(0)).then_inc(x_loaded, 16)
                for t in range(NT):
                    BK.emptied(sp, ("y", t))
                    sp.dma_start(out_rows[bass.ds(b, 1)].squeeze(0)[:, t, :], xi[:, t, :]).then_inc(stored, 16)
                sp.wait_ge(stored, 16 * NT)
                sp.wait_ge(arrived, 4)
                for s in turn_sems:
                    sp.sem_clear(s)
                for e in go:
                    sp.sem_inc(go[e], 1)

        @block.tensor
        def _(pe):
            def mm(out, lhsT, rhs, first, last):
                return pe.matmul(out, lhsT, rhs, start=first, stop=last)

            def close(product):
                product.then_inc(BK.filled_sem, 1)

            def turn(key, source, n):
                bank = BK.claim(pe, key)
                for i in range(n):
                    last = pe.transpose(bank[:, i * P:(i + 1) * P], source(i), ident)
                close(last)

            def columns(name, weights, src, n):
                for f in range(n):
                    bank = BK.claim(pe, (name, f))
                    for c in range(HC):
                        last = mm(bank, weights[:, c, f * P:(f + 1) * P], src[:, c, :], c == 0, c == HC - 1)
                    close(last)

            def token_rows(key, t, weights, bias=None):
                bank = BK.claim(pe, key)
                for c in range(HC):
                    last = mm(bank, xT[:, c, t * P:(t + 1) * P], weights[:, c, :], c == 0,
                              c == HC - 1 and bias is None)
                if bias is not None:
                    last = mm(bank, ones[:], bias, False, True)
                close(last)

            def routing():
                BK.emptied(pe, ("nT", HC - 1))
                bank = BK.claim(pe, ("r",))
                for t in range(NT):
                    at = slice(t * P, (t + 1) * P)
                    for c in range(HC):
                        mm(bank[:, at], nT[:, c, at], router[:, c, :], c == 0, False)
                    last = mm(bank[:, at], ones[:], bias3[:, 2 * KD:], False, True)
                close(last)

            def small_products():
                bank = BK.claim(pe, ("beta",))
                for t in range(NT):
                    for c in range(HC):
                        last = mm(bank[:, t * LH:(t + 1) * LH], xT[:, c, t * P:(t + 1) * P], wb[:, c, :],
                                  c == 0, c == HC - 1)
                close(last)
                bank = BK.claim(pe, ("hl",))
                for t in range(NT):
                    at = slice(t * P, (t + 1) * P)
                    for c in range(HC):
                        last = mm(bank[:, at], xT[:, c, at], uT[:, c, :], c == 0, c == HC - 1)
                close(last)
                bank = BK.claim(pe, ("nq",))
                pe.wait_ge(qsq_ready, KC)
                for t in range(NT):
                    for j in range(KC):
                        at = t * LH + 2 * j
                        last = mm(bank[:, at:at + 2], big[:, j, t * P:(t + 1) * P], const("heads"), True, True)
                close(last)

            def keys_values(t):
                for name, weights in (("k", wk), ("v", wv)):
                    for i in range(2):
                        token_rows((name, t, i), t, weights[:, :, i * HALF:(i + 1) * HALF])

            def finish(t):
                pe.wait_ge(o_ready, t + 1)
                for i in range(2):
                    turn(("oT", t, i), lambda c: o[:, (4 * i + c) * P:(4 * i + c + 1) * P], 4)
                bank = BK.claim(pe, ("y", t))[:, 0:H]
                at = slice(t * P, (t + 1) * P)
                BK.emptied(pe, ("oT", t, 1))
                for f in range(FFC):
                    mm(bank, big[:, f, at], w2t[:, f, :], f == 0, False)
                for c in range(KC):
                    mm(bank, oT[:, c, :], wo[:, c, :], False, False)
                close(mm(bank, hzT[:, at], vbasis[:], False, True))

            pe.wait_ge(prep["dve"], 3)
            for c in range(HC):
                last = pe.transpose(ps[:, 0, c * P:(c + 1) * P], ubasis[:, c * P:(c + 1) * P], ident)
            last.then_inc(prep["pe"], 1)
            pe.wait_ge(prep["dve"], 4)
            pe.wait_ge(prep["pool"], 2)
            with pe.Fori(0, B):
                pe.wait_ge(xn_ready, NT)
                for c in range(HC):
                    turn(("xT", c), lambda t: xn[:, t, c * P:(c + 1) * P], NT)
                pe.wait_ge(zn_ready, NT)
                for c in range(HC):
                    turn(("nT", c), lambda t: zn[:, t, c * P:(c + 1) * P], NT)
                BK.emptied(pe, ("xT", HC - 1))
                routing()
                columns("q", wq, xT, KC)
                small_products()
                columns("h", w1t, xT, FFC)
                pe.wait_ge(hz_ready, 1)
                turn(("hzT",), lambda t: rest[:, t, :], NT)
                keys_values(0)
                BK.emptied(pe, ("hzT",))
                for t in range(NT):
                    at = slice(t * P, (t + 1) * P)
                    BK.emptied(pe, ("k", t, 1))
                    for i in range(2):
                        turn(("kT", t, i), lambda c: k[:, t % 2, (4 * i + c) * P:(4 * i + c + 1) * P], 4)
                    BK.emptied(pe, ("kT", t, 1))
                    for j in range(LH // QUAD):
                        bank = BK.claim(pe, ("s", t, j))
                        for i, h in enumerate(score_quad(j)):
                            part = slice(h % 2 * LD, (h % 2 + 1) * LD)
                            last = mm(bank[:, i * P:(i + 1) * P], kT[part, h // 2, :], qT[part, h // 2, at],
                                      True, True)
                        close(last)
                    for name, weights, b0 in (("f", wf, 0), ("g", wg, KD)):
                        for i in range(2):
                            token_rows((name, t, i), t, weights[:, :, i * HALF:(i + 1) * HALF],
                                       bias3[:, b0 + i * HALF:b0 + (i + 1) * HALF])
                    if t + 1 < NT:
                        keys_values(t + 1)
                    if t:
                        finish(t - 1)
                    pe.wait_ge(v_ready, t + 1)
                    BK.emptied(pe, ("s", t, LH // QUAD - 1))
                    if t:
                        pe.wait_ge(qd_ready, t)
                        BK.emptied(pe, ("u", t - 1, 1))
                    for i in range(2):
                        bank = BK.claim(pe, ("o", t, i))
                        part = slice(i * LD, (i + 1) * LD)
                        for j in range(LH // 2):
                            out, h = bank[:, j * LD:(j + 1) * LD], 2 * j + i
                            if t:
                                mm(out, qd[part, j, :], state[part, j, :], True, False)
                            last = mm(out, sm[:, h, :], v[:, t % 2, h * LD:(h + 1) * LD], t == 0, True)
                        close(last)
                    if t + 1 < NT:
                        pe.wait_ge(vt_ready, t + 1)
                        for i in range(2):
                            bank = BK.claim(pe, ("u", t, i))
                            for j in range(4):
                                pair = slice((4 * i + j) * P, (4 * i + j + 1) * P)
                                last = mm(bank[:, j * P:(j + 1) * P], k[:, t % 2, pair], vt[:, pair], True, True)
                            close(last)
                finish(NT - 1)
                end_of_turn(pe, arrived, go["pe"])

        @block.scalar
        def _(act):
            def run(out, src, func, **kw):
                return nc.scalar.activation(out, src, func, **kw)

            def take(dst, key, func, **kw):
                src = BK.filled(act, key)
                if len(dst.shape) == 3:
                    src = src[:, 0:dst.shape[1] * dst.shape[2]].rearrange("p (a b) -> p a b", a=dst.shape[1])
                run(dst, src, func, **kw).then_inc(BK.emptied_sem["act"], 1)

            def keys_values(t):
                if t >= 2:
                    BK.filled(act, ("u", t - 2, 1))
                for name, dst in (("k", k), ("v", v)):
                    for i in range(2):
                        take(dst[:, t % 2, i * HALF:(i + 1) * HALF], (name, t, i), ACT.Silu)

            def finish(t):
                if t:
                    BK.filled(act, ("y", t - 1))
                for i in range(2):
                    take(oT[:, 4 * i:4 * i + 4, :], ("oT", t, i), ACT.Copy)

            act.wait_ge(wload, LOADED)
            act.wait_ge(memset_done, 1)
            run(squares, ubasis[:], ACT.Square, accum_out=unit[:, 0:1]).then_inc(prep["act"], 1)
            act.wait_ge(prep["act"], 1)
            run(squares, vbasis[:], ACT.Square, accum_out=unit[:, 1:2]).then_inc(prep["act"], 1)
            run(rate[:], rate[:], ACT.Exp).then_inc(prep["act"], 1)
            act.wait_ge(prep["dve"], 1)
            for h in range(LH):
                run(decay_s[:, h, :], const("gap"), ACT.Exp, scale=rate[:, h:h + 1])
            for j in range(LH // 2):
                run(decay_q[:, j, :], const("steps"), ACT.Exp, scale=rate[:, LH + j:LH + j + 1])
            run(decay_k[:], rate[:, 0:LH], ACT.Exp, scale=const("tail"))
            run(decay_all[:], rate[:, LH:], ACT.Exp, scale=float(P)).then_inc(prep["act"], 1)
            act.wait_ge(prep["dve"], 4)
            act.wait_ge(prep["pool"], 2)
            with act.Fori(0, B):
                for c in range(HC):
                    take(xT[:, c, :], ("xT", c), ACT.Copy)
                for c in range(HC):
                    take(nT[:, c, :], ("nT", c), ACT.Identity, scale=col[:, c:c + 1], bias=col[:, HC + c:HC + c + 1])
                for f in range(KC):
                    take(qT[:, f, :], ("q", f), ACT.Silu)
                take(beta[:], ("beta",), ACT.Sigmoid)
                act.wait_ge(rc_ready, 1)
                run(alpha, r[:], ACT.Exp).then_inc(er_ready, 1)
                act.wait_ge(er_ready, 1)
                run(alpha, alpha, ACT.Ln, bias=one[:]).then_inc(alpha_ready, 1)
                act.wait_ge(mass_ready, 1)
                run(mass[:, 1, :], mass[:, 0, :], ACT.Tanh).then_inc(tanh_ready, 1)
                for f in range(FFC):
                    take(big[:, f, :], ("h", f), ACT.Gelu)
                take(hzT, ("hzT",), ACT.Copy)
                keys_values(0)
                for t in range(NT):
                    if t:
                        BK.filled(act, ("s", t - 1, LH // QUAD - 1))
                    for i in range(2):
                        take(kT[:, 4 * i:4 * i + 4, :], ("kT", t, i), ACT.Copy)
                    if t:
                        BK.emptied(act, ("o", t - 1, 1))
                    for i in range(2):
                        take(g[:, i * HALF:(i + 1) * HALF], ("f", t, i), ACT.Sigmoid)
                    if t:
                        act.wait_ge(gated, t)
                    for i in range(2):
                        take(gate[:, i * HALF:(i + 1) * HALF], ("g", t, i), ACT.Sigmoid)
                    if t + 1 < NT:
                        keys_values(t + 1)
                    if t:
                        finish(t - 1)
                finish(NT - 1)
                end_of_turn(act, arrived, go["act"])

        @block.vector
        def _(dve):
            chain = Chain(dve, dve_chain)
            norms = [0]

            def tt(out, a, b, op):
                return nc.vector.tensor_tensor(out, a, b, op)

            def by_head(ap):
                return ap.rearrange("p (h d) -> p h d", d=LD)

            def norm(src, dst, signal):
                for t in range(NT):
                    last = nc.vector.bn_stats(stat[:, t, :], src[:, t, :])
                chain(last)
                for t in range(NT):
                    last = nc.vector.bn_aggr(mv[:, t, :], stat[:, t, :])
                chain(last)
                nc.vector.tensor_scalar(var[:], mv[:, :, 1], LN_EPS, None, ALU.add).then_inc(var_ready, 1)
                norms[0] += 1
                dve.wait_ge(rstd_ready, norms[0])
                for t in range(NT):
                    nc.vector.tensor_scalar(dst[:, t, :], src[:, t, :], mv[:, t, 0:1], rstd[:, t:t + 1],
                                            ALU.subtract, ALU.mult).then_inc(signal, 1)

            def route():
                nc.vector.tensor_scalar(r[:], split3(BK.filled(dve, ("r",)), NT), -TAU, TAU, ALU.max, ALU.min)\
                    .then_inc(BK.emptied_sem["dve"], 1)
                BK.emptied(dve, ("r",))
                for t in range(NT):
                    last = nc.vector.max(top[:, t, :], r[:, t, :])
                last.then_inc(rc_ready, 1)
                dve.wait_ge(rc_ready, 1)
                for t in range(NT):
                    last = nc.vector.match_replace(rest[:, t, :], top[:, t, :], r[:, t, :], -1e30)
                chain(last)
                chain(tt(rest, r[:], rest, ALU.not_equal))
                dve.wait_ge(alpha_ready, 1)
                chain(tt(alpha, alpha, rest, ALU.mult))
                nc.vector.reduce_sum(mass[:, 0, :], alpha, AX).then_inc(mass_ready, 1)
                dve.wait_ge(mass_ready, 1)
                chain(nc.vector.tensor_scalar(mass[:, 2, :], mass[:, 0, :], UNIT_EPS, None, ALU.add))
                chain(nc.vector.reciprocal(mass[:, 3, :], mass[:, 2, :]))
                tt(rest, split3(BK.filled(dve, ("hl",)), NT), alpha, ALU.mult)\
                    .then_inc(BK.emptied_sem["dve"], 1)
                dve.wait_ge(tanh_ready, 1)
                chain(tt(mass[:, 3, :], mass[:, 3, :], mass[:, 1, :], ALU.mult))
                BK.emptied(dve, ("hl",))
                tt(rest, rest, spread(mass[:, 3, :], [P, NT, NB]), ALU.mult).then_inc(hz_ready, 1)

            def add_result(t):
                tt(xi[:, t, :], xi[:, t, :], BK.filled(dve, ("y", t))[:, 0:H], ALU.add)\
                    .then_inc(BK.emptied_sem["dve"], 1)

            def output_sums(t):
                dve.wait_ge(osq_ready, t + 1)
                nc.vector.reduce_sum(on[:], by_head(sqs[:]), AX).then_inc(osum_ready, 1)

            def output_norm(t):
                dve.wait_ge(gated, t + 1)
                dve.wait_ge(on_ready, t + 1)
                tt(by_head(o[:]), by_head(o[:]), spread(on[:], [P, LH, LD]), ALU.mult).then_inc(o_ready, 1)

            dve.memset(one[:], 1.0)
            dve.memset(ones[:], 1.0)
            prepare = Chain(dve, setup_chain)
            prepare(dve.memset(bias3[:], 0.0))
            dve.memset(neghalf[:], -0.5).then_inc(memset_done, 1)
            dve.wait_ge(wload, LOADED)
            dve.wait_ge(prep["act"], 3)
            nc.vector.tensor_scalar(rate[:], rate[:], -1.0, -1e30, ALU.mult, ALU.max).then_inc(prep["dve"], 1)
            nc.vector.tensor_scalar(unit[:, 2:4], unit[:, 0:2], UNIT_EPS * UNIT_EPS, None, ALU.max)\
                .then_inc(prep["dve"], 1)
            prepare(nc.vector.tensor_scalar(rows[:, 0:KD], rows[:, 0:KD], -1.0, None, ALU.mult))
            for at in range(0, 2 * KD + NB, HALF):
                cut = slice(at, min(at + HALF, 2 * KD + NB))
                piece = rounded[:, 0:cut.stop - cut.start]
                for i in range(3):
                    prepare(nc.vector.tensor_copy(piece, rows[:, cut]))
                    prepare(nc.vector.tensor_copy(bias3[32 * i:32 * i + 1, cut], piece))
                    prepare(tt(rows[:, cut], rows[:, cut], piece, ALU.subtract))
            nc.vector.tensor_scalar(wo[:], wo[:], col[:, 2 * HC:2 * HC + 1], None, ALU.mult)
            dve.wait_ge(prep["pool"], 1)
            nc.vector.scalar_tensor_tensor(out=vbasis[:], in0=vbasis[:], scalar=unit[:, 1:2], in1=gamma[:],
                                           op0=ALU.mult, op1=ALU.mult)
            nc.vector.tensor_scalar(ubasis[:], ubasis[:], unit[:, 0:1], None, ALU.mult).then_inc(prep["dve"], 1)
            dve.wait_ge(prep["pe"], 1)
            nc.vector.tensor_copy(uT[:], ps[:, 0, 0:HC * NB].rearrange("p (c n) -> p c n", c=HC))\
                .then_inc(prep["dve"], 1)
            dve.wait_ge(prep["dve"], 4)
            dve.wait_ge(prep["pool"], 2)
            with dve.Fori(0, B):
                chain.count = norms[0] = 0
                dve.wait_ge(x_loaded, 16)
                norm(xi, xn, xn_ready)
                dve.wait_ge(xn_ready, NT)
                norm(xn, zn, zn_ready)
                route()
                nc.vector.tensor_scalar(qnorm[:].rearrange("p t h -> p (t h)"), BK.filled(dve, ("nq",))[:, 0:NT * LH],
                                        1e-24, None, ALU.max).then_inc(BK.emptied_sem["dve"], 1)
                for t in range(NT):
                    if t:
                        output_sums(t - 1)
                    dve.wait_ge(ksq_ready, t + 1)
                    if t:
                        dve.wait_ge(vt_ready, t)
                    nc.vector.reduce_sum(kn[:], by_head(sqs[:]), AX).then_inc(ksum_ready, 1)
                    for j in range(LH // QUAD):
                        bank = split3(BK.filled(dve, ("s", t, j)), QUAD)
                        if t:
                            BK.filled(dve, ("o", t - 1, 1))
                        first, last = score_quad(j)[0], score_quad(j)[-1]
                        tt(sm[:, first:last + 1:2, :], bank, decay_s[:, first:last + 1:2, :], ALU.mult)\
                            .then_inc(BK.emptied_sem["dve"], 1)
                    if t:
                        output_norm(t - 1)
                    dve.wait_ge(kn_ready, t + 1)
                    BK.emptied(dve, ("v", t, 1))
                    rows_v = by_head(v[:, t % 2, :])
                    tt(rows_v, rows_v, spread(kn[:], [P, LH, LD]), ALU.mult).then_inc(v_ready, 1)
                    if t:
                        add_result(t - 1)
                        BK.filled(dve, ("oT", t - 1, 1))
                    dve.wait_ge(gq_ready, t + 1)
                    for i in range(2):
                        out = by_head(o[:])[:, i:LH:2, :]
                        tt(out, by_head(BK.filled(dve, ("o", t, i))), by_head(g[:])[:, i:LH:2, :], ALU.mult)\
                            .then_inc(BK.emptied_sem["dve"], 1)
                    if t + 1 < NT:
                        if t:
                            chain(tt(state[:], state[:], spread(decay_all[:], [P, LH // 2, LD]), ALU.mult))
                        for i in range(2):
                            bank = split3(BK.filled(dve, ("u", t, i)), 4)
                            for half in range(2):
                                part = slice(half * LD, (half + 1) * LD)
                                dst, src = state[part, 4 * i:4 * i + 4, :], bank[part, :, half * LD:(half + 1) * LD]
                                if t:
                                    ins = tt(dst, dst, src, ALU.add)
                                else:
                                    ins = nc.vector.tensor_copy(dst, src)
                            ins.then_inc(BK.emptied_sem["dve"], 1)
                output_sums(NT - 1)
                output_norm(NT - 1)
                add_result(NT - 1)
                end_of_turn(dve, arrived, go["dve"])

        @block.gpsimd
        def _(pool):
            steps = Chain(pool, pool_chain)
            norms = [0]

            def tt(out, a, b, op):
                return nc.gpsimd.tensor_tensor(out, a, b, op)

            def by_head(ap):
                return ap.rearrange("p (h d) -> p h d", d=LD)

            def inverse_roots():
                norms[0] += 1
                pool.wait_ge(var_ready, norms[0])
                tt(rstd[:], var[:], neghalf[:, 0:NT], ALU.pow).then_inc(rstd_ready, 1)

            def output_squares(t):
                BK.emptied(pool, ("o", t, 1))
                tt(sqs[:], o[:], o[:], ALU.mult).then_inc(osq_ready, 1)

            def output_gates(t):
                pool.wait_ge(osq_ready, t + 1)
                BK.emptied(pool, ("g", t, 1))
                tt(o[:], o[:], gate[:], ALU.mult).then_inc(gated, 1)
                pool.wait_ge(osum_ready, t + 1)
                steps(nc.gpsimd.tensor_scalar(on[:], on[:], 1.0 / LD, 1e-5, ALU.mult, ALU.add))
                tt(on[:], on[:], neghalf[:, 0:LH], ALU.pow).then_inc(on_ready, 1)

            pool.wait_ge(prep["dve"], 2)
            tt(unit[:, 0:2], unit[:, 2:4], neghalf[:, 0:2], ALU.pow).then_inc(prep["pool"], 1)
            pool.wait_ge(prep["act"], 4)
            tt(decay_s[:], decay_s[:], const("after").unsqueeze(1).to_broadcast([P, LH, P]), ALU.mult)\
                .then_inc(prep["pool"], 1)
            pool.wait_ge(prep["pool"], 2)
            with pool.Fori(0, B):
                steps.count = norms[0] = 0
                inverse_roots()
                inverse_roots()
                for f in range(KC):
                    BK.emptied(pool, ("q", f))
                    tt(big[:, f, :], qT[:, f, :], qT[:, f, :], ALU.mult).then_inc(qsq_ready, 1)
                BK.emptied(pool, ("nq",))
                flat = qnorm[:].rearrange("p t h -> p (t h)")
                tt(flat, flat, neghalf[:], ALU.pow).then_inc(qnorm_ready, 1)
                pool.wait_ge(qnorm_ready, 1)
                for t in range(NT):
                    if t:
                        output_squares(t - 1)
                        output_gates(t - 1)
                    BK.emptied(pool, ("k", t, 1))
                    tt(sqs[:], k[:, t % 2, :], k[:, t % 2, :], ALU.mult).then_inc(ksq_ready, 1)
                    if t:
                        BK.filled(pool, ("o", t - 1, 1))
                        tt(qd[:], qT[:, :, t * P:(t + 1) * P], decay_q[:], ALU.mult).then_inc(qd_ready, 1)
                    pool.wait_ge(ksum_ready, t + 1)
                    steps(nc.gpsimd.tensor_scalar(kn[:], kn[:], 1e-24, None, ALU.max))
                    steps(tt(kn[:], kn[:], neghalf[:, 0:LH], ALU.pow))
                    tt(kn[:], kn[:], beta[:, t, :], ALU.mult).then_inc(kn_ready, 1)
                    BK.emptied(pool, ("f", t, 1))
                    tt(by_head(g[:]), by_head(g[:]), spread(qnorm[:, t, :], [P, LH, LD]), ALU.mult)\
                        .then_inc(gq_ready, 1)
                    if t + 1 < NT:
                        pool.wait_ge(v_ready, t + 1)
                        if t:
                            BK.filled(pool, ("u", t - 1, 1))
                        tt(by_head(vt[:]), by_head(v[:, t % 2, :]), spread(decay_k[:], [P, LH, LD]), ALU.mult)\
                            .then_inc(vt_ready, 1)
                output_squares(NT - 1)
                output_gates(NT - 1)
                end_of_turn(pool, arrived, go["pool"])


def kernel(**inputs):
    import concourse.bacc as bacc
    from concourse.bass_utils import run_bass_kernel_spmd

    nc = bacc.Bacc("TRN2", target_bir_lowering=False, num_devices=1)
    arrays, aps = {}, {}

    def given(name, value):
        a = np.ascontiguousarray(value)
        arrays[f"in_{name}"] = a
        aps[name] = nc.dram_tensor(f"in_{name}", a.shape, mybir.dt.from_np(a.dtype), kind="ExternalInput").ap()

    turned = {"L1_ffn_W1": "W1_turned", "L1_ffn_W2": "W2_turned", "L1_ffn_router_W": "router_turned"}
    for name, value in inputs.items():
        if name in turned:
            given(turned[name], np.asarray(value).T)
        else:
            given(name, value)
    given("shape_constants", shape_constants())
    mid = nc.dram_tensor("mid", (B, L, H), F32, kind="Internal").ap()
    result = nc.dram_tensor("result", (B, L, H), F32, kind="ExternalOutput").ap()
    stage_one(nc, aps, mid, aps["shape_constants"])
    stage_two(nc, aps, mid, result, aps["shape_constants"])
    r = run_bass_kernel_spmd(nc, [arrays], core_ids=[0])
    return r.results[0]["result"]
```

```python
from contextlib import ExitStack

import numpy as np
import concourse.bass as bass
from concourse import mybir

F32 = mybir.dt.float32
BF16 = mybir.dt.bfloat16
ACT = mybir.ActivationFunctionType
ALU = mybir.AluOpType
AX = mybir.AxisListType.X

P = 128
B, L, H = 8, 512, 256
NT = L // P
HC = H // P
LN_EPS = 1e-5
PART_ROWS = 65

INNER, NS, CONV, DTR = 512, 16, 4, 16
IC = INNER // P
DEPTH, NH, DH, WIN = 2, 8, 64, 128
FI = NH * DH
FC = FI // P
HID = int(H * 4 * 2 / 3)
UC = -(-HID // P)
LAST = HID - (UC - 1) * P
QK_SCALE = 8.0
LH, LD = 16, 64
KD = LH * LD
KC = KD // P
NB, FF, TOPK, TAU, UNIT_EPS = 128, 1024, 8, 10.0, 1e-6
FFC = FF // P


def shape_constants():
    half = np.arange(0, DH, 2, dtype=np.float32)
    inv = (1.0 / 10000.0 ** (half / DH)).astype(np.float32)
    t = np.arange(L, dtype=np.float32)
    freqs = t[:, None] * inv[None, :]
    freqs = np.concatenate([freqs, freqs], -1)
    base = (half + np.float32(0.4 * DH)) / np.float32(1.4 * DH)
    power = (t - L // 2) / np.float32(WIN // 2)
    scale = base[None, :] ** power[:, None]
    scale = np.concatenate([scale, scale], -1)
    sign = np.where(np.arange(DH) < DH // 2, -1.0, 1.0).astype(np.float32)
    cos, sin = np.cos(freqs), np.sin(freqs) * sign
    rope = np.stack([cos * scale * QK_SCALE, sin * scale * QK_SCALE, cos / scale, sin / scale])
    rope = rope.reshape(4, NT, P, DH).transpose(2, 0, 1, 3)
    i = np.arange(P)
    far = -3.0e38
    window = np.stack([np.where(i[None, :] >= i[:, None], 0.0, far), np.where(i[None, :] <= i[:, None], 0.0, far)], 1)
    after = (i[None, :] > i[:, None]).astype(np.float32)
    gap = np.maximum(i[None, :] - 1 - i[:, None], 0)
    steps = np.broadcast_to(i[None, :], (P, P))
    tail = (P - 1 - i)[:, None]
    heads = (i[:, None] // LD == np.arange(2)[None, :])
    parts = [np.eye(P), rope, window, after, gap, steps, tail, heads]
    return np.concatenate([p.reshape(P, -1) for p in parts], 1).astype(np.float32)


CONST_AT = {}
_at = 0
for _name, _n in (("ident", P), ("rope", 4 * NT * DH), ("window", 2 * P), ("after", P), ("gap", P), ("steps", P),
                  ("tail", 1), ("heads", 2)):
    CONST_AT[_name] = (_at, _n)
    _at += _n


class Banks:

    def __init__(self, products, banks, filled, emptied):
        self.banks, self.filled_sem, self.emptied_sem = banks, filled, emptied
        self.place, self.by, self.nth, count = {}, [], [], {}
        for i, (key, engine) in enumerate(products):
            assert key not in self.place, key
            self.place[key] = i
            count[engine] = count.get(engine, 0) + 1
            self.by.append(engine)
            self.nth.append(count[engine])

    def bank(self, key):
        return self.banks[self.place[key] % len(self.banks)]

    def claim(self, pe, key):
        before = self.place[key] - len(self.banks)
        if before >= 0:
            pe.wait_ge(self.emptied_sem[self.by[before]], self.nth[before])
        return self.bank(key)

    def filled(self, eng, key):
        eng.wait_ge(self.filled_sem, self.place[key] + 1)
        return self.bank(key)

    def emptied(self, eng, key):
        i = self.place[key]
        eng.wait_ge(self.emptied_sem[self.by[i]], self.nth[i])


class Chain:

    def __init__(self, eng, sem):
        self.eng, self.sem, self.count = eng, sem, 0

    def __call__(self, instruction):
        self.count += 1
        instruction.then_inc(self.sem, 1)
        self.eng.wait_ge(self.sem, self.count)


def split3(ap, n):
    return ap.rearrange("p (a b) -> p a b", a=n)


def spread(column, shape):
    return column.unsqueeze(2).to_broadcast(shape)


def end_of_turn(eng, arrived, go):
    eng.drain().then_inc(arrived, 1)
    eng.wait_ge(go, 1)
    eng.sem_clear(go)


ATT = [(l, t) for l in range(DEPTH) for t in range(NT)]
PAIRS = FC
STEPS = [(n, c) for n in range(NS) for c in range(IC)]
FFN_ROWS = (3, 3)
FIRST_ROW = (0, NT - 1)
PLACES = [FIRST_ROW + (1,)] + [("ffn", 0, i) for i in range(FFN_ROWS[0])] + ["layer"] \
    + [(1, t, i) for t in range(NT) for i in range(2)] + [("ffn", 1, i) for i in range(FFN_ROWS[1])]
ROW_AT = {place: n for n, place in enumerate(PLACES)}
assert len(PLACES) == NS


def score_heads(p):
    return [4 * (p // 2) + 2 * i + p % 2 for i in range(2)]


def block_products():
    out = [(("hT", 0, t), "act") for t in range(NT)]
    out += [(("q", 0, 0), "dve"), (("k", 0, 0), "dve"), (("v", 0, 0), "act")]
    for l in range(DEPTH):
        out += [(("qT", l, 0), "act"), (("kT", l, 0), "act")]
        for t in range(NT):
            ahead = t + 1 < NT
            out += [(("s", l, t, p), "act") for p in range(PAIRS)]
            out += [(("q", l, t + 1), "dve"), (("k", l, t + 1), "dve"), (("v", l, t + 1), "act")] if ahead else []
            out += [(("pT", l, t, p), "act") for p in range(PAIRS)] + [(("oT", l, t), "act")]
            out += [(("qT", l, t + 1), "act"), (("kT", l, t + 1), "act")] if ahead else []
            out += [(("wo", l, t), "dve")]
        out += [(("nT", l, t), "act") for t in range(NT)]
        for f in range(UC):
            out += [(("gate", l, f), "act"), (("up", l, f), "dve")]
        if l + 1 < DEPTH:
            n = l + 1
            out += [(("down", l, 0), "dve"), (("down", l, 1), "dve"), (("hT", n, 0), "act"), (("down", l, 2), "dve"),
                    (("q", n, 0), "dve"), (("k", n, 0), "dve"), (("down", l, 3), "dve"), (("v", n, 0), "act"),
                    (("hT", n, 1), "act"), (("hT", n, 2), "act"), (("hT", n, 3), "act")]
        else:
            out += [(("down", l, t), "dve") for t in range(NT)]
    return out


def ssm_products():
    out = [(("zT", c), "act") for c in range(HC)]
    out += [(("xb", f), "act") for f in range(IC)] + [(("z", f), "act") for f in range(IC)]
    out += [(("BCR",), "act")]
    out += [(("dt", c), "dve") for c in range(IC)] + [(("mean",), "dve")]
    for n in range(NS):
        out += [(("Brow", n), "act"), (("Crow", n), "dve")]
    return out + [(("ssm", i), "dve") for i in range(NT // 2)]


def stage_one(nc, w, mid, consts):
    with ExitStack() as ctx:
        def sb(name, shape, dt=F32):
            return ctx.enter_context(nc.sbuf_tensor("one_" + name, shape, dt))

        turn_sems = []

        def sem(name, per_turn=True):
            s = ctx.enter_context(nc.semaphore("one_" + name))
            if per_turn:
                turn_sems.append(s)
            return s

        ps = ctx.enter_context(nc.psum_tensor("one_ps", [P, 8, 512], F32))

        ident = sb("ident", [P, P])[:]
        window = sb("window", [P, 2 * P], BF16)
        ident_bf = sb("ident_bf", [P, P], BF16)
        in_w = sb("in_w", [P, HC, 2 * INNER])
        out_w = sb("out_w", [P, IC, H])
        bcr_w = sb("bcr_w", [P, IC, 64 + DTR])
        dt_w = sb("dt_w", [DTR, INNER])
        out_b = sb("out_b", [1, H])
        ones = sb("ones", [1, P])
        wqkv = sb("wqkv", [P, DEPTH, HC, 3 * FI])
        wo = sb("wo", [P, DEPTH, FC, H])
        w1 = sb("w1", [P, DEPTH, HC, 2 * HID])
        w2 = sb("w2", [P, DEPTH, UC, H])
        col = sb("col", [P, 64])
        cols, at = {}, 0
        for name, n in (("norm_w", HC), ("norm_b", HC), ("in_b", 2 * IC), ("conv_b", IC), ("dt_b", IC),
                        ("ln_g", DEPTH * HC), ("ln_b", DEPTH * HC), ("b1", DEPTH * 2 * UC)):
            cols[name] = col[:, at:at + n]
            at += n
        conv_w = sb("conv_w", [P, IC, CONV])
        small_b = sb("small_b", [64 + DTR, 1])
        rope = sb("rope", [P, DEPTH, 4, NT, DH])
        mean_w = sb("mean_w", [P, NS])
        neghalf = sb("neghalf", [P, 8])
        one = sb("one", [P, 1])
        zeros = sb("zeros", [1, P])
        zero_row = zeros[0:1, :]

        xf = sb("xf", [P, NT, H])
        xs = sb("xs", [P, NT, H])
        hT = sb("hT", [P, HC * (L + 1)])
        hT_write = hT[:, :].rearrange("p (c t) -> p c t", c=HC)[:, :, 0:L]
        qk = sb("qk", [P, 2, FI])
        vv = sb("vv", [P, 3, FI])
        qT = sb("qT", [P, PAIRS, P])
        kT = sb("kT", [P, 2, PAIRS, P])
        sm = sb("sm", [P, PAIRS, 2, 2 * P])
        zs = sm[:, 0:2, :, :].rearrange("p i h k -> p (i h) k")
        scales = sm[:, 0, 0, 0:2 * DEPTH * DH].rearrange("p (i l d) -> p i l d", i=2, l=DEPTH)
        hid = sb("hid", [P, UC * L])
        pT = hid[:, 0:NH * 2 * P].rearrange("p (h k q) -> p h k q", h=NH, k=2)
        u = hid[:, :].rearrange("p (f t) -> p f t", f=UC)
        rope_table = hid[:, 0:4 * NT * DH]
        window_table = hid[:, 4 * NT * DH:4 * NT * DH + 2 * P]
        scratch = sb("scratch", [P, 2, L])
        sq, turned, gl = scratch[:, 0, :], scratch[:, 1, :], scratch
        oT = sb("oT", [P, FC, P])
        stat = sb("stat", [P, NT, 6])
        mv = sb("mv", [P, NT, 2])
        var = sb("var", [P, NT])
        rstd = sb("rstd", [P, NT])
        ssq = sb("ssq", [P, 2, NH])
        rnorm = sb("rnorm", [P, 2, NH])
        nmax = sb("nmax", [P, PAIRS, 2])
        rsum = sb("rsum", [P, PAIRS, 2])

        xb = sb("xb", [P, IC, L + CONV - 1])
        y = sb("y", [P, IC, L])
        xa = sb("xa", [P, IC, L])
        dt = sb("dt", [P, IC, L])
        bcr = sb("bcr", [NS, 3, L])
        rounded = bcr[:, 2, :].bitcast(BF16).rearrange("p (i t) -> p i t", i=2)
        left = scratch[0:NS]
        bc3 = sb("bc3", [64 + NS, 2, L], BF16)
        pick3 = sb("pick3", [64 + NS, NS], BF16)
        brow = sb("brow", [P, 2, L])
        decay = sb("decay", [P, 4, L])
        zT = decay[:, 0:HC, :]
        st = sb("st", [P, 4, L])

        wload = sem("wload", False)
        tables_loaded = sem("tables_loaded", False)
        setup = sem("setup", False)
        setup_chain = sem("setup_chain", False)
        arrived = sem("arrived")
        go = {e: sem("go_" + e, False) for e in ("pe", "act", "dve", "pool")}

        FB = Banks(block_products(), [ps[:, i, :] for i in range(5)], sem("blk_filled"),
                   {"act": sem("blk_act_emptied"), "dve": sem("blk_dve_emptied")})
        MB = Banks(ssm_products(), [ps[:, 5 + i, :] for i in range(3)], sem("ssm_filled"),
                   {"act": sem("ssm_act_emptied"), "dve": sem("ssm_dve_emptied")})

        next_loaded = sem("next_loaded")
        stored = sem("stored", False)
        xf_free = sem("xf_free")
        xf_ready = sem("xf_ready")
        shifted = [[sem(f"shifted_{l}_{t}") for t in range(NT)] for l in range(DEPTH)]
        x_again = sem("x_again")
        x_added = sem("x_added")
        dve_chain = sem("dve_chain")
        pool_chain = sem("pool_chain")
        var_ready = sem("var_ready")
        rstd_ready = sem("rstd_ready")
        xn_ready = sem("xn_ready")
        zn_ready = sem("zn_ready")
        opening = {name: sem("opening_" + name, False) for name in ("loaded", "var", "rstd", "xn", "zn")}
        sq_ready = sem("sq_ready")
        ssq_ready = sem("ssq_ready")
        rnorm_ready = sem("rnorm_ready")
        qk_ready = sem("qk_ready")
        smax_ready = sem("smax_ready")
        p_ready = sem("p_ready")
        n_ready = sem("n_ready")
        conv_ready = sem("conv_ready")
        xa_ready = sem("xa_ready")
        pre_ready = sem("pre_ready")
        e_ready = sem("e_ready")
        sp_ready = sem("sp_ready")
        dt_ready = sem("dt_ready")
        bc_split = sem("bc_split")
        decay_ready = sem("decay_ready")
        bx_ready = sem("bx_ready")
        scanned = sem("scanned")
        hc_ready = sem("hc_ready")
        y_added = sem("y_added")
        gated_ready = sem("gated_ready")

        def const(name):
            a, n = CONST_AT[name]
            return consts[:, a:a + n]

        table_loads = [
            (ident, const("ident")), (window_table, const("window")), (rope_table, const("rope")),
            (scales[:, 0], w["L0_ffn_q_scale"].partition_broadcast(P)),
            (scales[:, 1], w["L0_ffn_k_scale"].partition_broadcast(P)),
        ]
        weight_loads = [
            (in_w[:], w["L0_attn_in_w"].rearrange("(c p) n -> p c n", p=P)),
            (out_w[:], w["L0_attn_out_w"].rearrange("(c p) n -> p c n", p=P)),
            (bcr_w[:, :, 0:NS], w["L0_attn_bc_w"][:, 0:NS].rearrange("(c p) n -> p c n", p=P)),
            (bcr_w[:, :, 32:32 + NS], w["L0_attn_bc_w"][:, NS:2 * NS].rearrange("(c p) n -> p c n", p=P)),
            (bcr_w[:, :, 64:64 + DTR], w["L0_attn_dtr_w"].rearrange("(c p) n -> p c n", p=P)),
            (dt_w[:], w["L0_attn_dt_w"]), (out_b[:], w["L0_attn_out_b"].unsqueeze(0)),
            (conv_w[:], w["L0_attn_conv_w"].rearrange("(c p) k -> p c k", p=P)),
            (small_b[0:NS, :], w["L0_attn_bc_b"][0:NS].unsqueeze(1)),
            (small_b[32:32 + NS, :], w["L0_attn_bc_b"][NS:2 * NS].unsqueeze(1)),
            (small_b[64:64 + DTR, :], w["L0_attn_dtr_b"].unsqueeze(1)),
        ]
        for name in ("norm_w", "norm_b", "in_b", "conv_b", "dt_b"):
            weight_loads.append((cols[name], w["L0_attn_" + name].rearrange("(c p) -> p c", p=P)))
        for l in range(DEPTH):
            weight_loads += [
                (wqkv[:, l], w["L0_ffn_wqkv"][l].rearrange("(c p) n -> p c n", p=P)),
                (wo[:, l], w["L0_ffn_wo"][l].rearrange("(c p) n -> p c n", p=P)),
                (w1[:, l], w["L0_ffn_w1"][l].rearrange("(c p) n -> p c n", p=P)),
                (w2[:, l, 0:UC - 1], w["L0_ffn_w2"][l, 0:(UC - 1) * P].rearrange("(c p) n -> p c n", p=P)),
                (w2[0:LAST, l, UC - 1], w["L0_ffn_w2"][l, (UC - 1) * P:HID]),
                (w2[LAST:LAST + 1, l, UC - 1], w["L0_ffn_b2"][l:l + 1]),
                (cols["ln_g"][:, l * HC:(l + 1) * HC], w["L0_ffn_ln_g"][l].rearrange("(c p) -> p c", p=P)),
                (cols["ln_b"][:, l * HC:(l + 1) * HC], w["L0_ffn_ln_b"][l].rearrange("(c p) -> p c", p=P)),
            ]
            for part in range(2):
                at, b1 = (2 * l + part) * UC, w["L0_ffn_b1"][l, part * HID:(part + 1) * HID]
                weight_loads += [
                    (cols["b1"][:, at:at + UC - 1], b1[0:(UC - 1) * P].rearrange("(c p) -> p c", p=P)),
                    (cols["b1"][0:LAST, at + UC - 1:at + UC], b1[(UC - 1) * P:HID].unsqueeze(1)),
                ]

        x_rows = w["L0_attn_x"].rearrange("b (t p) h -> b p t h", p=P)
        mid_rows = mid.rearrange("b (t p) h -> b p t h", p=P)
        block = ctx.enter_context(nc.Block())

        @block.sync
        def _(sp):
            sp.dma_start(xs[:], x_rows[0]).then_inc(opening["loaded"], 16)
            for dst, src in table_loads:
                sp.dma_start(dst, src).then_inc(tables_loaded, 16)
            with nc.allow_non_contiguous_dma(reason="per-feature vectors as columns, once"):
                for dst, src in weight_loads:
                    sp.dma_start(dst, src).then_inc(wload, 16)
            sp.sem_inc(xf_free, 1)

            def turn(b, last=False):
                for l in range(DEPTH):
                    for t in range(NT):
                        FB.emptied(sp, ("wo", l, t))
                        sp.dma_start(xs[:, t, 0:P], xf[:, t, 0:P]).then_inc(shifted[l][t], 16)
                        sp.dma_start(xs[1:P, t, P:H], xf[0:P - 1, t, P:H]).then_inc(shifted[l][t], 16)
                        before = xf[P - 1:P, t - 1, P:H] if t else zero_row
                        sp.dma_start(xs[0:1, t, P:H], before).then_inc(shifted[l][t], 16)
                FB.filled(sp, ("nT", DEPTH - 1, NT - 1))
                sp.dma_start(xs[:], x_rows[bass.ds(b, 1)].squeeze(0)).then_inc(x_again, 16)
                sp.wait_ge(x_added, 1)
                if last:
                    sp.sem_inc(next_loaded, 16)
                else:
                    sp.dma_start(xs[:], x_rows[bass.ds(b + 1, 1)].squeeze(0)).then_inc(next_loaded, 16)
                for t in range(NT):
                    MB.emptied(sp, ("ssm", t // 2))
                    sp.dma_start(mid_rows[bass.ds(b, 1)].squeeze(0)[:, t, :], xf[:, t, :]).then_inc(stored, 16)
                sp.wait_ge(arrived, 4)
                for s in turn_sems:
                    sp.sem_clear(s)
                for e in go:
                    sp.sem_inc(go[e], 1)
                sp.wait_ge(stored, 16 * NT)
                sp.sem_clear(stored)
                sp.sem_inc(xf_free, 1)

            with sp.Fori(0, B - 1) as b:
                turn(b)
            turn(B - 1, last=True)

        @block.tensor
        def _(pe):
            def mm(out, lhsT, rhs, first, last):
                return pe.matmul(out, lhsT, rhs, start=first, stop=last)

            def close(product, banks):
                product.then_inc(banks.filled_sem, 1)

            def turn(banks, key, source, n):
                bank = banks.claim(pe, key)
                for i in range(n):
                    last = pe.transpose(bank[:, i * P:(i + 1) * P], source(i), ident)
                close(last, banks)

            def ssm_inputs():
                for c in range(HC):
                    turn(MB, ("zT", c), lambda t: zs[:, t, c * P:(c + 1) * P], NT)
                MB.emptied(pe, ("zT", HC - 1))
                ssm_project("xb", 0)

            def ssm_project(name, first_chunk, chunks=range(IC)):
                for f in chunks:
                    bank = MB.claim(pe, (name, f))
                    at = (first_chunk + f) * P
                    for c in range(HC):
                        last = mm(bank, in_w[:, c, at:at + P], zT[:, c, :], c == 0, c == HC - 1)
                    close(last, MB)

            def ssm_rows():
                pe.wait_ge(xa_ready, IC)
                bank = MB.claim(pe, ("BCR",))
                for c in range(IC):
                    last = mm(bank[0:64 + DTR, :], bcr_w[:, c, :], xa[:, c, :], c == 0, c == IC - 1)
                close(last, MB)

            def ssm_rates():
                MB.emptied(pe, ("BCR",))
                for c in range(IC):
                    bank = MB.claim(pe, ("dt", c))
                    close(mm(bank, dt_w[:, c * P:(c + 1) * P], bcr[:, 2, :], True, True), MB)

            def ssm_mean():
                bank = MB.claim(pe, ("mean",))
                pe.wait_ge(dt_ready, IC)
                for c in range(IC):
                    last = mm(bank[0:NS, :], mean_w[:], dt[:, c, :], c == 0, c == IC - 1)
                close(last, MB)

            def ssm_row(place):
                if place not in ROW_AT:
                    return
                n = ROW_AT[place]
                if n == 0:
                    pe.wait_ge(bc_split, 1)
                pick = pick3[:, n:n + 1].to_broadcast([64 + NS, P])
                for i, name in enumerate(("Brow", "Crow")):
                    bank = MB.claim(pe, (name, n))
                    close(mm(bank, pick, bc3[:, i, :], True, True), MB)

            def features(l, t):
                if l:
                    FB.emptied(pe, ("down", l - 1, t))
                rows = xf if l else xs
                turn(FB, ("hT", l, t), lambda c: rows[:, t, c * P:(c + 1) * P], HC)

            def project(l, t, names):
                FB.emptied(pe, ("hT", l, t))
                for name in names:
                    i = "qkv".index(name)
                    bank = FB.claim(pe, (name, l, t))
                    for c in range(HC):
                        last = mm(bank, hT[:, c * L + t * P:c * L + (t + 1) * P], wqkv[:, l, c, i * FI:(i + 1) * FI],
                                  c == 0, c == HC - 1)
                    close(last, FB)

            def turn_qk(l, t):
                g = l * NT + t
                for i, name in enumerate(("qT", "kT")):
                    pe.wait_ge(qk_ready, 2 * g + i + 1)
                    turn(FB, (name, l, t), lambda p: qk[:, i, p * P:(p + 1) * P], PAIRS)

            def scores(l, t):
                g = l * NT + t
                FB.emptied(pe, ("kT", l, t))
                if t == 0:
                    FB.emptied(pe, ("qT", l, t))
                for p in range(0, PAIRS, 2):
                    banks = [split3(FB.claim(pe, ("s", l, t, p + i)), 2) for i in range(2)]
                    lo = 0 if t else P
                    for bank in banks:
                        mm(bank[:, :, lo:], ident_bf[:],
                           window[:, lo:].unsqueeze(1).to_broadcast([P, 2, 2 * P - lo]), True, False)
                    for h in range(2):
                        for k in range(0 if t else 1, 2):
                            for i in range(2):
                                head = score_heads(p + i)[h]
                                rows = slice(i * DH, (i + 1) * DH)
                                last = mm(banks[i][:, h, k * P:(k + 1) * P], qT[rows, head // 2, :],
                                          kT[rows, (g + k - 1) % 2, head // 2, :], False, (h, k) == (1, 1))
                                if (h, k) == (1, 1):
                                    close(last, FB)

            def turn_p(l, t):
                g = l * NT + t
                for p in range(PAIRS):
                    bank = FB.claim(pe, ("pT", l, t, p)).rearrange("p (h k q) -> p h k q", h=2, k=2)
                    pe.wait_ge(p_ready, g * PAIRS + p + 1)
                    for h in range(2):
                        for k in range(0 if t else 1, 2):
                            last = pe.transpose(bank[:, h, k, :], sm[:, p, h, k * P:(k + 1) * P], ident)
                    close(last, FB)

            def attend(l, t):
                g = l * NT + t
                bank = FB.claim(pe, ("oT", l, t))
                FB.emptied(pe, ("v", l, t))
                FB.emptied(pe, ("pT", l, t, PAIRS - 1))
                for h in range(NH):
                    rows = slice(h % 2 * DH, (h % 2 + 1) * DH)
                    for k in range(0 if t else 1, 2):
                        last = mm(bank[rows, h // 2 * P:(h // 2 + 1) * P],
                                  vv[:, (g + k - 1) % 3, h * DH:(h + 1) * DH], pT[:, h, k, :],
                                  k == 0 or t == 0, k == 1)
                close(last, FB)

            def attend_out(l, t):
                bank = FB.claim(pe, ("wo", l, t))
                FB.emptied(pe, ("oT", l, t))
                for c in range(FC):
                    last = mm(bank[:, 0:H], oT[:, c, :], wo[:, l, c, :], c == 0, c == FC - 1)
                close(last, FB)

            def ffn_in(l, t):
                pe.wait_ge(n_ready, l * NT + t + 1)
                turn(FB, ("nT", l, t), lambda c: xs[:, t, c * P:(c + 1) * P], HC)

            def ffn_hidden(l, f):
                if f == 0:
                    FB.emptied(pe, ("nT", l, NT - 1))
                m = P if f < UC - 1 else LAST
                for name, at in (("gate", HID), ("up", 0)):
                    bank = FB.claim(pe, (name, l, f))
                    for c in range(HC):
                        last = mm(bank[0:m, :], w1[:, l, c, at + f * P:at + f * P + m], hT_write[:, c, :],
                                  c == 0, c == HC - 1)
                    close(last, FB)

            def ffn_down(l, t):
                FB.emptied(pe, ("up", l, UC - 1))
                bank = FB.claim(pe, ("down", l, t))
                for f in range(UC):
                    m = P if f < UC - 1 else LAST + 1
                    last = mm(bank[:, 0:H], u[0:m, f, t * P:(t + 1) * P], w2[0:m, l, f, :], f == 0, f == UC - 1)
                close(last, FB)

            def ssm_out():
                pe.wait_ge(gated_ready, IC)
                for i in range(NT // 2):
                    bank = MB.claim(pe, ("ssm", i))
                    for t in (2 * i, 2 * i + 1):
                        out = bank[:, (t % 2) * H:(t % 2 + 1) * H]
                        for c in range(IC):
                            mm(out, y[:, c, t * P:(t + 1) * P], out_w[:, c, :], c == 0, False)
                        last = mm(out, ones[:], out_b[:], False, True)
                    close(last, MB)

            pe.wait_ge(wload, 16 * len(weight_loads))
            pe.wait_ge(setup, 1)
            pe.wait_ge(opening["zn"], NT)
            with pe.Fori(0, B):
                for t in range(NT):
                    features(0, t)
                project(0, 0, "qkv")
                ssm_inputs()
                for l in range(DEPTH):
                    turn_qk(l, 0)
                    for t in range(NT):
                        scores(l, t)
                        ssm_row((l, t, 0))
                        if (l, t) == (0, 2):
                            ssm_project("z", IC, range(IC - 1, IC))
                            ssm_rows()
                        if t + 1 < NT:
                            project(l, t + 1, "qkv")
                        if (l, t) == (0, 1):
                            ssm_project("z", IC, range(IC - 1))
                        if (l, t) == (0, 3):
                            ssm_mean()
                        turn_p(l, t)
                        if (l, t) == (0, 2):
                            ssm_rates()
                        if (l, t) != FIRST_ROW:
                            ssm_row((l, t, 1))
                        attend(l, t)
                        if t + 1 < NT:
                            turn_qk(l, t + 1)
                        attend_out(l, t)
                        if (l, t) == FIRST_ROW:
                            ssm_row((l, t, 1))
                    for t in range(NT - 1):
                        ffn_in(l, t)
                    ffn_in(l, NT - 1)
                    for f in range(UC):
                        if f % 2 == 0:
                            ssm_row(("ffn", l, f // 2))
                        ffn_hidden(l, f)
                    if l + 1 < DEPTH:
                        n = l + 1
                        ffn_down(l, 0)
                        ffn_down(l, 1)
                        features(n, 0)
                        ffn_down(l, 2)
                        project(n, 0, "qk")
                        ffn_down(l, 3)
                        project(n, 0, "v")
                        for t in range(1, NT):
                            features(n, t)
                        ssm_row("layer")
                    else:
                        for t in range(NT):
                            ffn_down(l, t)
                        ssm_out()
                end_of_turn(pe, arrived, go["pe"])


        @block.scalar
        def _(act):
            def run(out, src, func, **kw):
                return nc.scalar.activation(out, src, func, **kw)

            def free(instruction, banks):
                instruction.then_inc(banks.emptied_sem["act"], 1)

            def ssm_inputs():
                for c in range(HC):
                    free(run(zT[:, c, :], MB.filled(act, ("zT", c)), ACT.Identity,
                             scale=cols["norm_w"][:, c:c + 1], bias=cols["norm_b"][:, c:c + 1]), MB)
                for f in range(IC):
                    free(run(xb[:, f, CONV - 1:], MB.filled(act, ("xb", f)), ACT.Identity,
                             bias=cols["in_b"][:, f:f + 1]), MB)

            def conv_silus():
                for f in range(IC):
                    act.wait_ge(conv_ready, (CONV - 1) * IC + f + 1)
                    run(xa[:, f, :], y[:, f, :], ACT.Silu).then_inc(xa_ready, 1)

            def gate_silus():
                for f in range(IC):
                    free(run(xb[:, f, CONV - 1:], MB.filled(act, ("z", f)), ACT.Silu,
                             bias=cols["in_b"][:, IC + f:IC + f + 1]), MB)

            def ssm_rows():
                bank = MB.filled(act, ("BCR",))
                for i in range(3):
                    last = run(bcr[:, i, :], bank[32 * i:32 * i + NS, :], ACT.Identity,
                               bias=small_b[32 * i:32 * i + NS, :])
                free(last, MB)

            def rate_exps():
                for c in range(IC):
                    MB.emptied(act, ("dt", c))
                    run(dt[:, c, :], dt[:, c, :], ACT.Exp).then_inc(e_ready, 1)

            def rate_logs():
                for c in range(IC):
                    act.wait_ge(e_ready, c + 1)
                    run(dt[:, c, :], dt[:, c, :], ACT.Ln, bias=one[:]).then_inc(sp_ready, 1)

            def take_row(place):
                if place not in ROW_AT:
                    return
                n = ROW_AT[place]
                src = MB.filled(act, ("Brow", n))
                if n >= 2:
                    act.wait_ge(bx_ready, IC * (n - 1))
                free(run(brow[:, n % 2, :], src, ACT.Copy), MB)

            def decays(place, half=None):
                if place not in ROW_AT:
                    return
                n = ROW_AT[place]
                for c in range(IC) if half is None else range(2 * half, 2 * half + 2):
                    i = n * IC + c
                    if i == 0:
                        act.wait_ge(dt_ready, IC)
                    if i >= 4:
                        act.wait_ge(scanned, i - 3)
                    run(decay[:, i % 4, :], dt[:, c, :], ACT.Exp, scale=-(n + 1.0)).then_inc(decay_ready, 1)

            def features(l, t):
                src = FB.filled(act, ("hT", l, t))[:, 0:HC * P]
                free(run(hT_write[:, :, t * P:(t + 1) * P], split3(src, HC), ACT.Copy), FB)

            def square(l, t, i):
                g = l * NT + t
                bank = FB.filled(act, ("qk"[i], l, t))
                if 2 * g + i >= 1:
                    act.wait_ge(ssq_ready, 2 * g + i)
                if t == 0 and l and i == 0:
                    FB.emptied(act, ("up", l - 1, UC - 1))
                run(sq, bank, ACT.Square).then_inc(sq_ready, 1)

            def values(l, t):
                free(run(vv[:, (l * NT + t) % 3, :], FB.filled(act, ("v", l, t)), ACT.Copy), FB)

            def turned_qk(l, t):
                for key, dst in ((("qT", l, t), qT[:]), (("kT", l, t), kT[:, (l * NT + t) % 2])):
                    free(run(dst, split3(FB.filled(act, key), PAIRS), ACT.Copy), FB)

            def attention(l, t):
                g = l * NT + t
                lo = 0 if t else P

                def exps(p):
                    act.wait_ge(smax_ready, g * PAIRS + p + 1)
                    bank = split3(FB.filled(act, ("s", l, t, p)), 2)
                    if g:
                        FB.filled(act, ("pT",) + ATT[g - 1] + (p,))
                    for h in range(2):
                        last = run(sm[:, p, h, lo:2 * P], bank[:, h, lo:], ACT.Exp, bias=nmax[:, p, h:h + 1],
                                   accum_out=rsum[:, p, h:h + 1])
                    free(last, FB)

                def take(p):
                    src = FB.filled(act, ("pT", l, t, p)).rearrange("p (h k q) -> p h k q", h=2, k=2)
                    k = 0 if t else 1
                    first, last = score_heads(p)
                    free(run(pT[:, first:last + 1:2, k:2, :], src[:, :, k:2, :], ACT.Copy), FB)

                decays((l, t, 0))
                for p in range(PAIRS):
                    exps(p)
                    if p == 1:
                        take_row((l, t, 0))
                if (l, t) == (0, 2):
                    ssm_rows()
                if t + 1 < NT:
                    square(l, t + 1, 0)
                    values(l, t + 1)
                take(0)
                take(1)
                if t + 1 < NT:
                    square(l, t + 1, 1)
                take(2)
                take(3)
                if (l, t) == (0, 2):
                    rate_exps()
                if (l, t) != FIRST_ROW:
                    take_row((l, t, 1))
                    decays((l, t, 1), 0)
                free(run(oT[:], split3(FB.filled(act, ("oT", l, t)), FC), ACT.Copy), FB)
                if (l, t) == FIRST_ROW:
                    take_row((l, t, 1))
                    decays((l, t, 1), 0)
                decays((l, t, 1), 1)
                if t + 1 < NT:
                    turned_qk(l, t + 1)
                if (l, t) == (0, 1):
                    conv_silus()
                    gate_silus()
                if (l, t) == (0, 2):
                    rate_logs()

            def ffn_features(l, t):
                src = FB.filled(act, ("nT", l, t))
                for c in range(HC):
                    at = l * HC + c
                    last = run(hT_write[:, c, t * P:(t + 1) * P], src[:, c * P:(c + 1) * P], ACT.Identity,
                               scale=cols["ln_g"][:, at:at + 1], bias=cols["ln_b"][:, at:at + 1])
                free(last, FB)

            def ffn_gates(l):
                for f in range(UC):
                    m = P if f < UC - 1 else LAST
                    at = (2 * l + 1) * UC + f
                    if f % 2 == 0:
                        take_row(("ffn", l, f // 2))
                        if f < 4:
                            decays(("ffn", l, f // 2))
                    src = FB.filled(act, ("gate", l, f))
                    if f >= 2:
                        FB.emptied(act, ("up", l, f - 2))
                    free(run(gl[0:m, f % 2, :], src[0:m, :], ACT.Gelu, bias=cols["b1"][0:m, at:at + 1]), FB)

            act.wait_ge(wload, 16 * len(weight_loads))
            act.wait_ge(setup, 1)
            with act.Fori(0, B):
                for t in range(NT):
                    features(0, t)
                square(0, 0, 0)
                square(0, 0, 1)
                values(0, 0)
                ssm_inputs()
                turned_qk(0, 0)
                for l in range(DEPTH):
                    for t in range(NT):
                        attention(l, t)
                    for t in range(NT - 1):
                        ffn_features(l, t)
                    ffn_features(l, NT - 1)
                    ffn_gates(l)
                    decays(("ffn", l, 2))
                    if l + 1 < DEPTH:
                        n = l + 1
                        features(n, 0)
                        square(n, 0, 0)
                        square(n, 0, 1)
                        values(n, 0)
                        for t in range(1, NT):
                            features(n, t)
                        take_row("layer")
                        decays("layer")
                        turned_qk(n, 0)
                end_of_turn(act, arrived, go["act"])

        @block.vector
        def _(dve):
            chain = Chain(dve, dve_chain)
            norms = [0]

            def tt(out, a, b, op):
                return nc.vector.tensor_tensor(out, a, b, op)

            def norm(src, dst, signal, tiles=range(NT), opened=None):
                cut = slice(tiles[0], tiles[-1] + 1)
                step = prepare if opened else chain
                for t in tiles:
                    last = nc.vector.bn_stats(stat[:, t, :], src[:, t, :])
                step(last)
                for t in tiles:
                    last = nc.vector.bn_aggr(mv[:, t, :], stat[:, t, :])
                step(last)
                nc.vector.tensor_scalar(var[:, cut], mv[:, cut, 1], LN_EPS, None, ALU.add)\
                    .then_inc(opening["var"] if opened else var_ready, 1)
                if opened:
                    dve.wait_ge(opening["rstd"], opened)
                else:
                    norms[0] += 1
                    dve.wait_ge(rstd_ready, norms[0])
                for t in tiles:
                    nc.vector.tensor_scalar(dst[:, t, :], src[:, t, :], mv[:, t, 0:1], rstd[:, t:t + 1],
                                            ALU.subtract, ALU.mult).then_inc(signal, 1)

            def convolve(*taps):
                for k in taps:
                    for f in range(IC):
                        if k == 0:
                            MB.emptied(dve, ("xb", f))
                            ins = nc.vector.tensor_scalar(y[:, f, :], xb[:, f, 0:L], conv_w[:, f, 0:1],
                                                          cols["conv_b"][:, f:f + 1], ALU.mult, ALU.add)
                        else:
                            dve.wait_ge(conv_ready, (k - 1) * IC + f + 1)
                            ins = nc.vector.scalar_tensor_tensor(
                                out=y[:, f, :], in0=xb[:, f, k:k + L], scalar=conv_w[:, f, k:k + 1],
                                in1=y[:, f, :], op0=ALU.mult, op1=ALU.add)
                        ins.then_inc(conv_ready, 1)

            def rate_inputs():
                for c in range(IC):
                    nc.vector.tensor_scalar(dt[:, c, :], MB.filled(dve, ("dt", c)), cols["dt_b"][:, c:c + 1],
                                            20.0, ALU.add, ALU.min).then_inc(MB.emptied_sem["dve"], 1)

            def clip_rates():
                for c in range(IC):
                    dve.wait_ge(sp_ready, c + 1)
                    nc.vector.tensor_scalar(dt[:, c, :], dt[:, c, :], 0.001, 0.1, ALU.max, ALU.min)\
                        .then_inc(dt_ready, 1)

            def split_rows():
                MB.emptied(dve, ("BCR",))
                tt(bcr[:, 0, :], bcr[:, 0, :], MB.filled(dve, ("mean",))[0:NS, :], ALU.mult)\
                    .then_inc(MB.emptied_sem["dve"], 1)
                MB.emptied(dve, ("mean",))
                rows = bcr[:, 0:2, :]
                chain(nc.vector.tensor_copy(bc3[0:NS], rows))
                chain(tt(left, rows, bc3[0:NS], ALU.subtract))
                chain(nc.vector.tensor_copy(rounded, left))
                nc.vector.tensor_copy(bc3[32:32 + NS], rounded)
                tt(bc3[64:64 + NS], left, rounded, ALU.subtract).then_inc(bc_split, 1)

            def scans(place, halves=(0, 1)):
                if place not in ROW_AT:
                    return
                for half in halves:
                    first = ROW_AT[place] * IC + 2 * half
                    pair = (first, first + 1)
                    for i in pair:
                        dve.wait_ge(decay_ready, i + 1)
                        dve.wait_ge(bx_ready, i + 1)
                        s = st[:, i % 4, :]
                        nc.vector.tensor_tensor_scan(s, decay[:, i % 4, :], s, 0.0, ALU.mult, ALU.add)\
                            .then_inc(scanned, 1)
                    for i in pair:
                        n, c = STEPS[i]
                        crow = MB.filled(dve, ("Crow", n))
                        dve.wait_ge(scanned, i + 1)
                        dst = y[:, c, :] if n == 0 else st[:, i % 4, :]
                        ins = tt(dst, st[:, i % 4, :], crow, ALU.mult)
                        ins.then_inc(MB.emptied_sem["dve"] if c == IC - 1 else hc_ready, 1)

            def rotate(l, t):
                g = l * NT + t
                for i, name in enumerate("qk"):
                    bank = FB.filled(dve, (name, l, t))
                    if g:
                        FB.filled(dve, (name + "T",) + ATT[g - 1])
                    heads = bank.rearrange("p (h d) -> p h d", h=NH)
                    swapped = bank.rearrange("p (h s d) -> p h s d", h=NH, s=2)[:, :, ::-1, :]
                    cos = rope[:, l, 2 * i, t, :].unsqueeze(1).to_broadcast([P, NH, DH])
                    sin = split3(rope[:, l, 2 * i + 1, t, :], 2).unsqueeze(1).to_broadcast([P, NH, 2, DH // 2])
                    rows = qk[:, i, :].rearrange("p (h d) -> p h d", h=NH)
                    dve.wait_ge(sq_ready, 2 * g + i + 1)
                    tt(rows, heads, cos, ALU.mult)
                    tt(turned.rearrange("p (h s d) -> p h s d", h=NH, s=2), swapped, sin, ALU.mult)\
                        .then_inc(FB.emptied_sem["dve"], 1)
                    nc.vector.reduce_sum(ssq[:, i, :], sq.rearrange("p (h d) -> p h d", h=NH), AX)\
                        .then_inc(ssq_ready, 1)
                    FB.emptied(dve, (name, l, t))
                    chain(tt(qk[:, i, :], qk[:, i, :], turned, ALU.add))

            def normalize(l, t):
                g = l * NT + t
                for i in range(2):
                    rows = qk[:, i, :].rearrange("p (h d) -> p h d", h=NH)
                    dve.wait_ge(rnorm_ready, 2 * g + i + 1)
                    tt(rows, rows, spread(rnorm[:, i, :], [P, NH, DH]), ALU.mult).then_inc(qk_ready, 1)

            def attention(l, t):
                g = l * NT + t
                lo = 0 if t else P
                for p in range(PAIRS):
                    bank = split3(FB.filled(dve, ("s", l, t, p)), 2)
                    nc.vector.tensor_reduce(nmax[:, p, :], bank[:, :, lo:], AX, ALU.max, negate=True)\
                        .then_inc(smax_ready, 1)
                if (l, t) == (0, 0):
                    convolve(0)
                if (l, t) == (0, 3):
                    clip_rates()
                for p in range(PAIRS):
                    FB.emptied(dve, ("s", l, t, p))
                    chain(nc.vector.reciprocal(rsum[:, p, :], rsum[:, p, :]))
                    s = sm[:, p, :, lo:2 * P]
                    tt(s, s, spread(rsum[:, p, :], [P, 2, 2 * P - lo]), ALU.mult).then_inc(p_ready, 1)
                if t + 1 < NT:
                    rotate(l, t + 1)
                if (l, t) == (0, 1):
                    convolve(3)
                if (l, t) == (0, 2):
                    rate_inputs()
                if (l, t) == (0, 0):
                    convolve(1)
                scans((l, t, 0), (0,))
                if t + 1 < NT:
                    normalize(l, t + 1)
                if (l, t) == (0, 0):
                    convolve(2)
                scans((l, t, 0), (1,))
                if t == NT - 1:
                    ffn_norm(l, range(NT - 1))
                    if (l, t) == FIRST_ROW:
                        split_rows()
                    add_rows(("wo", l, t), t)
                    ffn_norm(l, range(NT - 1, NT))
                scans((l, t, 1), (0,))
                if t < NT - 1:
                    add_rows(("wo", l, t), t)
                scans((l, t, 1), (1,))

            def add_rows(key, t):
                if key == ("wo", 0, 0):
                    dve.wait_ge(xf_ready, 1)
                tt(xf[:, t, :], xf[:, t, :], FB.filled(dve, key)[:, 0:H], ALU.add)\
                    .then_inc(FB.emptied_sem["dve"], 1)

            def ffn_norm(l, tiles):
                for t in tiles:
                    dve.wait_ge(shifted[l][t], 16 * 3)
                norm(xs, xs, n_ready, tiles)

            def hidden(l, f):
                m = P if f < UC - 1 else LAST
                at = 2 * l * UC + f
                bank = FB.filled(dve, ("up", l, f))
                FB.emptied(dve, ("gate", l, f))
                nc.vector.scalar_tensor_tensor(
                    out=u[0:m, f, :], in0=bank[0:m, :], scalar=cols["b1"][0:m, at:at + 1],
                    in1=gl[0:m, f % 2, :], op0=ALU.add, op1=ALU.mult).then_inc(FB.emptied_sem["dve"], 1)

            def add_ssm():
                for i in range(NT // 2):
                    pair = slice(2 * i, 2 * i + 2)
                    FB.emptied(dve, ("down", DEPTH - 1, 2 * i + 1))
                    tt(xf[:, pair, :], xf[:, pair, :], split3(MB.filled(dve, ("ssm", i)), 2), ALU.add)\
                        .then_inc(MB.emptied_sem["dve"], 1)

            dve.memset(xb[:], 0.0)
            dve.memset(hT[:], 0.0)
            dve.memset(hid[32:64, (UC - 1) * L:UC * L], 1.0)
            dve.memset(zeros[:], 0.0)
            for part in range(2):
                dve.memset(bcr_w[:, :, 32 * part + NS:32 * (part + 1)], 0.0)
            prepare = Chain(dve, setup_chain)
            prepare(dve.memset(bc3[:], 0.0))
            prepare(dve.memset(pick3[:], 0.0))
            dve.memset(ones[:], 1.0)
            dve.memset(one[:], 1.0)
            dve.memset(neghalf[:], -0.5)
            dve.memset(mean_w[:], 1.0 / INNER)
            dve.wait_ge(tables_loaded, 16 * len(table_loads))
            nc.vector.tensor_copy(window[:], window_table)
            nc.vector.tensor_copy(ident_bf[:], ident)
            for i in range(3):
                nc.vector.tensor_copy(pick3[32 * i:32 * i + NS, :], ident[0:NS, 0:NS])
            table = rope_table.rearrange("p (k t d) -> p k t d", k=4, t=NT)
            for l in range(DEPTH):
                for i in range(2):
                    s = scales[:, i, l, :]
                    flip = split3(s, 2)[:, ::-1, :]
                    tt(rope[:, l, 2 * i], table[:, 2 * i], s.unsqueeze(1).to_broadcast([P, NT, DH]), ALU.mult)
                    for t in range(NT):
                        ins = tt(split3(rope[:, l, 2 * i + 1, t], 2), split3(table[:, 2 * i + 1, t], 2), flip,
                                 ALU.mult)
            ins.then_inc(setup, 1)
            dve.wait_ge(setup, 1)
            dve.wait_ge(opening["loaded"], 16)
            norm(xs, xs, opening["xn"], opened=1)
            dve.wait_ge(opening["xn"], NT)
            norm(xs, zs, opening["zn"], opened=2)
            dve.wait_ge(wload, 16 * len(weight_loads))
            with dve.Fori(0, B):
                chain.count = norms[0] = 0
                rotate(0, 0)
                normalize(0, 0)
                for l in range(DEPTH):
                    for t in range(NT):
                        attention(l, t)
                    for f in range(UC):
                        hidden(l, f)
                        if f < 4:
                            scans(("ffn", l, f // 2), (f % 2,))
                        if l and f == 3:
                            dve.wait_ge(x_again, 16)
                            tt(xf[:], xf[:], xs[:], ALU.add).then_inc(x_added, 1)
                            dve.wait_ge(x_added, 1)
                    scans(("ffn", l, 2), (0,))
                    if l == 0:
                        add_rows(("down", l, 0), 0)
                        add_rows(("down", l, 1), 1)
                        scans(("ffn", l, 2), (1,))
                        add_rows(("down", l, 2), 2)
                        rotate(1, 0)
                        add_rows(("down", l, 3), 3)
                        normalize(1, 0)
                        scans("layer")
                    else:
                        scans(("ffn", l, 2), (1,))
                        for t in range(NT):
                            add_rows(("down", l, t), t)
                        dve.wait_ge(next_loaded, 16)
                        norm(xs, xs, xn_ready)
                        dve.wait_ge(xn_ready, NT)
                        norm(xs, zs, zn_ready)
                        add_ssm()
                end_of_turn(dve, arrived, go["dve"])

        @block.gpsimd
        def _(pool):
            norms, tiles = [0], [0]

            def inverse_roots(first=0, last=NT):
                norms[0] += 1
                pool.wait_ge(var_ready, norms[0])
                nc.gpsimd.tensor_tensor(rstd[:, first:last], var[:, first:last], neghalf[:, first:last], ALU.pow)\
                    .then_inc(rstd_ready, 1)

            def inverse_norms(g):
                for i in range(2):
                    pool.wait_ge(ssq_ready, 2 * g + i + 1)
                    nc.gpsimd.tensor_scalar(ssq[:, i, :], ssq[:, i, :], 1e-24, None, ALU.max)\
                        .then_inc(pool_chain, 1)
                    pool.wait_ge(pool_chain, 2 * g + i + 1)
                    nc.gpsimd.tensor_tensor(rnorm[:, i, :], ssq[:, i, :], neghalf[:], ALU.pow)\
                        .then_inc(rnorm_ready, 1)

            def inputs(j):
                for i in (2 * j, 2 * j + 1):
                    n, c = STEPS[i]
                    MB.emptied(pool, ("Brow", n))
                    if i >= 4 + IC:
                        pool.wait_ge(y_added, i - 4 - IC + 1)
                    nc.gpsimd.tensor_tensor(st[:, i % 4, :], brow[:, n % 2, :], xa[:, c, :], ALU.mult)\
                        .then_inc(bx_ready, 1)

            def product_ready(i):
                n, c = STEPS[i]
                if c == IC - 1:
                    MB.emptied(pool, ("Crow", n))
                else:
                    pool.wait_ge(hc_ready, n * (IC - 1) + c + 1)

            def sums(j):
                for i in (2 * j, 2 * j + 1):
                    n, c = STEPS[i]
                    product_ready(i)
                    if n == 0:
                        continue
                    if n >= 2:
                        pool.wait_ge(y_added, i - 2 * IC + 1)
                    nc.gpsimd.tensor_tensor(y[:, c, :], y[:, c, :], st[:, i % 4, :], ALU.add).then_inc(y_added, 1)

            def row_inputs(place, half):
                if place in ROW_AT:
                    inputs(2 * ROW_AT[place] + half)

            def row_sums(place, half):
                if place in ROW_AT:
                    sums(2 * ROW_AT[place] + half)

            pool.wait_ge(setup, 1)
            for i in range(2):
                pool.wait_ge(opening["var"], i + 1)
                nc.gpsimd.tensor_tensor(rstd[:], var[:], neghalf[:, 0:NT], ALU.pow).then_inc(opening["rstd"], 1)
            with pool.Fori(0, B):
                norms[0] = 0
                inverse_norms(0)
                pool.wait_ge(xf_free, 1)
                nc.gpsimd.tensor_copy(xf[:], xs[:]).then_inc(xf_ready, 1)
                for l in range(DEPTH):
                    for t in range(NT):
                        row_inputs((l, t, 0), 0)
                        row_inputs((l, t, 0), 1)
                        if t + 1 < NT:
                            inverse_norms(l * NT + t + 1)
                        row_sums((l, t, 0), 0)
                        if t == NT - 1:
                            inverse_roots(0, NT - 1)
                        if (l, t) == FIRST_ROW:
                            inverse_roots(NT - 1, NT)
                        row_inputs((l, t, 1), 0)
                        row_sums((l, t, 0), 1)
                        if t == NT - 1 and (l, t) != FIRST_ROW:
                            inverse_roots(NT - 1, NT)
                        row_inputs((l, t, 1), 1)
                        row_sums((l, t, 1), 0)
                        row_sums((l, t, 1), 1)
                    for i in range(FFN_ROWS[l]):
                        for half in range(2):
                            row_inputs(("ffn", l, i), half)
                        for half in range(2):
                            row_sums(("ffn", l, i), half)
                    if l == 0:
                        inverse_norms(NT)
                        for half in range(2):
                            row_inputs("layer", half)
                        for half in range(2):
                            row_sums("layer", half)
                pool.wait_ge(y_added, (NS - 1) * IC)
                for f in range(IC):
                    MB.emptied(pool, ("z", f))
                    nc.gpsimd.tensor_tensor(y[:, f, :], y[:, f, :], xb[:, f, CONV - 1:], ALU.mult)\
                        .then_inc(gated_ready, 1)
                for i in range(2):
                    inverse_roots()
                end_of_turn(pool, arrived, go["pool"])


QUAD = 4
HALF = KD // 2


def score_quad(j):
    return [2 * (QUAD * (j // 2) + i) + j % 2 for i in range(QUAD)]


def mixer_products():
    out = [(("xT", c), "act") for c in range(HC)] + [(("nT", c), "act") for c in range(HC)]
    out += [(("r",), "dve")] + [(("q", f), "act") for f in range(KC)]
    out += [(("beta",), "act"), (("hl",), "dve"), (("nq",), "dve")]
    out += [(("h", f), "act") for f in range(FFC)] + [(("hzT",), "act")]

    def keys_values(t):
        return [((name, t, i), "act") for name in "kv" for i in range(2)]

    def finish(t):
        return [(("oT", t, i), "act") for i in range(2)] + [(("y", t), "dve")]

    out += keys_values(0)
    for t in range(NT):
        out += [(("kT", t, i), "act") for i in range(2)]
        out += [(("s", t, j), "dve") for j in range(LH // QUAD)]
        out += [(("f", t, i), "act") for i in range(2)]
        out += keys_values(t + 1) if t + 1 < NT else []
        out += finish(t - 1) if t else []
        out += [(("o", t, i), "dve") for i in range(2)]
        out += [(("u", t, i), "dve") for i in range(2)] if t + 1 < NT else []
        out += [(("g", t, i), "act") for i in range(2)]
    return out + finish(NT - 1)


def stage_two(nc, w, mid, result, consts):
    with ExitStack() as ctx:
        def sb(name, shape, dt=F32):
            return ctx.enter_context(nc.sbuf_tensor("two_" + name, shape, dt))

        turn_sems = []

        def sem(name, per_turn=True):
            s = ctx.enter_context(nc.semaphore("two_" + name))
            if per_turn:
                turn_sems.append(s)
            return s

        ps = ctx.enter_context(nc.psum_tensor("two_ps", [P, 8, 512], F32))

        first = CONST_AT["after"][0]
        cst = sb("cst", [P, _at - first])
        ident_sb = sb("ident", [P, P])

        def const(name):
            a, n = CONST_AT[name]
            return cst[:, a - first:a - first + n]

        ident = ident_sb[:]
        wk, wv, wf, wg, wq = [sb("w" + n, [P, HC, KD]) for n in "kvfgq"]
        wb = sb("wb", [P, HC, LH])
        wo = sb("wo", [P, KC, H])
        w1t = sb("w1t", [P, HC, FF])
        w2t = sb("w2t", [P, FFC, H])
        router = sb("router", [P, HC, NB])
        ubasis = sb("ubasis", [P, H])
        uT = sb("uT", [P, HC, NB])
        vbasis = sb("vbasis", [P, H])
        gamma = sb("gamma", [P, H])
        bias3 = sb("bias3", [PART_ROWS, 2 * KD + NB], BF16)
        ones = sb("ones", [PART_ROWS, P], BF16)
        one = sb("one", [P, 1])
        neghalf = sb("neghalf", [P, NT * LH])
        col = sb("col", [P, 2 * HC + 1])
        rate = sb("rate", [P, LH + LH // 2])
        decay_s = sb("decay_s", [P, LH, P])
        decay_q = sb("decay_q", [P, LH // 2, P])
        decay_k = sb("decay_k", [P, LH])
        decay_all = sb("decay_all", [P, LH // 2])
        unit = sb("unit", [P, 4])

        xi = sb("xi", [P, NT, H])
        xn = sb("xn", [P, NT, H])
        zn = sb("zn", [P, NT, H])
        xT = sb("xT", [P, HC, L])
        nT = sb("nT", [P, HC, L])
        qT = sb("qT", [P, KC, L])
        big = sb("big", [P, KC, L])
        rows = big[0:1].rearrange("p c t -> p (c t)")[:, 0:2 * KD + NB]
        beta = sb("beta", [P, NT, LH])
        qnorm = sb("qnorm", [P, NT, LH])
        r = sb("r", [P, NT, NB])
        rest = zn[:, :, 0:NB]
        alpha = zn[:, :, NB:2 * NB]
        top = sb("top", [P, NT, TOPK])
        mass = sb("mass", [P, 4, NT])
        hzT = nT[:, 0, :]
        k = sb("k", [P, 2, KD])
        v = sb("v", [P, 2, KD])
        vt = sb("vt", [P, KD])
        sqs = sb("sqs", [P, KD])
        squares = sqs[:, 0:H]
        kn = sb("kn", [P, LH])
        on = sb("on", [P, LH])
        kT = sb("kT", [P, KC, P])
        qd = sb("qd", [P, KC, P])
        sm = sb("sm", [P, LH, P])
        g = sb("g", [P, KD])
        gate = sb("gate", [P, KD])
        state = sb("state", [P, LH // 2, LD])
        o = sb("o", [P, KD])
        rounded = o[0:1, :].bitcast(BF16)[:, 0:HALF]
        oT = sb("oT", [P, KC, P])
        stat = sb("stat", [P, NT, 6])
        mv = sb("mv", [P, NT, 2])
        var = sb("var", [P, NT])
        rstd = sb("rstd", [P, NT])

        wload = sem("wload", False)
        biases_loaded = sem("biases_loaded", False)
        memset_done = sem("memset_done", False)
        prep = {e: sem("prep_" + e, False) for e in ("act", "dve", "pool", "pe")}
        setup_chain = sem("setup_chain", False)
        arrived = sem("arrived")
        go = {e: sem("go_" + e, False) for e in ("pe", "act", "dve", "pool")}
        BK = Banks(mixer_products(), [ps[:, i, :] for i in range(8)], sem("filled"),
                   {"act": sem("act_emptied"), "dve": sem("dve_emptied")})

        x_loaded = sem("x_loaded")
        next_loaded = sem("next_loaded")
        stored = sem("stored", False)
        dve_chain = sem("dve_chain")
        pool_chain = sem("pool_chain")
        var_ready = sem("var_ready")
        rstd_ready = sem("rstd_ready")
        xn_ready = sem("xn_ready")
        zn_ready = sem("zn_ready")
        opening = {name: sem("opening_" + name, False) for name in ("loaded", "var", "rstd", "xn", "zn")}
        qsq_ready = sem("qsq_ready")
        qnorm_ready = sem("qnorm_ready")
        rc_ready = sem("rc_ready")
        er_ready = sem("er_ready")
        alpha_ready = sem("alpha_ready")
        mass_ready = sem("mass_ready")
        tanh_ready = sem("tanh_ready")
        hz_ready = sem("hz_ready")
        ksq_ready = sem("ksq_ready")
        ksum_ready = sem("ksum_ready")
        kn_ready = sem("kn_ready")
        v_ready = sem("v_ready")
        vt_ready = sem("vt_ready")
        qd_ready = sem("qd_ready")
        gq_ready = sem("gq_ready")
        osq_ready = sem("osq_ready")
        osum_ready = sem("osum_ready")
        on_ready = sem("on_ready")
        gated = sem("gated")
        o_ready = sem("o_ready")

        def wide(name):
            return w[name].rearrange("(c p) n -> p c n", p=P)

        weight_loads = [(cst[:], consts[:, first:_at]), (ident, consts[:, 0:P])]
        for dst, name in ((wk, "Wk"), (wv, "Wv"), (wf, "Wf"), (wg, "Wg"), (wq, "Wq"), (wb, "Wb"), (wo, "Wo")):
            weight_loads.append((dst[:], wide("L1_attn_" + name)))
        weight_loads += [(w1t[:], wide("W1_turned")), (w2t[:], wide("W2_turned")), (router[:], wide("router_turned")),
                         (ubasis[:], w["L1_ffn_raw_U"]), (vbasis[:], w["L1_ffn_raw_V"]),
                         (gamma[:], w["L1_ffn_gamma"].rearrange("a b h -> (a b h)").partition_broadcast(P)),
                         (col[:, 0:HC], w["L1_ffn_ln_g"].rearrange("(c p) -> p c", p=P)),
                         (col[:, HC:2 * HC], w["L1_ffn_ln_b"].rearrange("(c p) -> p c", p=P)),
                         (rate[:, 0:LH], w["L1_attn_A_log"].partition_broadcast(P))]
        for half in range(2):
            part = slice(half * LD, (half + 1) * LD)
            weight_loads += [(col[part, 2 * HC:], w["L1_attn_norm_w"].unsqueeze(1)),
                             (rate[part, LH:], w["L1_attn_A_log"].rearrange("(j s) -> s j", s=2)[half]
                              .partition_broadcast(LD))]
        bias_loads = [(rows[:, 0:KD], w["L1_attn_dt_bias"].unsqueeze(0)),
                      (rows[:, KD:2 * KD], w["L1_attn_bg"].unsqueeze(0)),
                      (rows[:, 2 * KD:], w["L1_ffn_router_b"].unsqueeze(0))]
        LOADED = 16 * len(weight_loads)
        mid_rows = mid.rearrange("b (t p) h -> b p t h", p=P)
        out_rows = result.rearrange("b (t p) h -> b p t h", p=P)
        block = ctx.enter_context(nc.Block())

        @block.sync
        def _(sp):
            for dst, src in bias_loads:
                sp.dma_start(dst, src).then_inc(biases_loaded, 16)
            sp.dma_start(xn[:], mid_rows[0]).then_inc(opening["loaded"], 16)
            with nc.allow_non_contiguous_dma(reason="per-feature vectors as columns, once"):
                for dst, src in weight_loads:
                    sp.dma_start(dst, src).then_inc(wload, 16)

            def turn(b, last=False):
                sp.dma_start(xi[:], mid_rows[bass.ds(b, 1)].squeeze(0)).then_inc(x_loaded, 16)
                BK.filled(sp, ("xT", HC - 1))
                if last:
                    sp.sem_inc(next_loaded, 16)
                else:
                    sp.dma_start(xn[:], mid_rows[bass.ds(b + 1, 1)].squeeze(0)).then_inc(next_loaded, 16)
                for t in range(NT):
                    BK.emptied(sp, ("y", t))
                    sp.dma_start(out_rows[bass.ds(b, 1)].squeeze(0)[:, t, :], xi[:, t, :]).then_inc(stored, 16)
                sp.wait_ge(arrived, 4)
                for s in turn_sems:
                    sp.sem_clear(s)
                for e in go:
                    sp.sem_inc(go[e], 1)
                sp.wait_ge(stored, 16 * NT)
                sp.sem_clear(stored)

            with sp.Fori(0, B - 1) as b:
                turn(b)
            turn(B - 1, last=True)

        @block.tensor
        def _(pe):
            def mm(out, lhsT, rhs, first, last):
                return pe.matmul(out, lhsT, rhs, start=first, stop=last)

            def close(product):
                product.then_inc(BK.filled_sem, 1)

            def turn(key, source, n):
                bank = BK.claim(pe, key)
                for i in range(n):
                    last = pe.transpose(bank[:, i * P:(i + 1) * P], source(i), ident)
                close(last)

            def columns(name, weights, src, n):
                for f in range(n):
                    bank = BK.claim(pe, (name, f))
                    for c in range(HC):
                        last = mm(bank, weights[:, c, f * P:(f + 1) * P], src[:, c, :], c == 0, c == HC - 1)
                    close(last)

            def token_rows(key, t, weights, bias=None):
                bank = BK.claim(pe, key)
                for c in range(HC):
                    last = mm(bank, xT[:, c, t * P:(t + 1) * P], weights[:, c, :], c == 0,
                              c == HC - 1 and bias is None)
                if bias is not None:
                    last = mm(bank, ones[:], bias, False, True)
                close(last)

            def routing():
                BK.emptied(pe, ("nT", HC - 1))
                bank = BK.claim(pe, ("r",))
                for t in range(NT):
                    at = slice(t * P, (t + 1) * P)
                    for c in range(HC):
                        mm(bank[:, at], nT[:, c, at], router[:, c, :], c == 0, False)
                    last = mm(bank[:, at], ones[:], bias3[:, 2 * KD:], False, True)
                close(last)

            def small_products():
                bank = BK.claim(pe, ("beta",))
                for t in range(NT):
                    for c in range(HC):
                        last = mm(bank[:, t * LH:(t + 1) * LH], xT[:, c, t * P:(t + 1) * P], wb[:, c, :],
                                  c == 0, c == HC - 1)
                close(last)
                bank = BK.claim(pe, ("hl",))
                for t in range(NT):
                    at = slice(t * P, (t + 1) * P)
                    for c in range(HC):
                        last = mm(bank[:, at], xT[:, c, at], uT[:, c, :], c == 0, c == HC - 1)
                close(last)
                bank = BK.claim(pe, ("nq",))
                pe.wait_ge(qsq_ready, KC)
                for t in range(NT):
                    for j in range(KC):
                        at = t * LH + 2 * j
                        last = mm(bank[:, at:at + 2], big[:, j, t * P:(t + 1) * P], const("heads"), True, True)
                close(last)

            def keys_values(t):
                for name, weights in (("k", wk), ("v", wv)):
                    for i in range(2):
                        token_rows((name, t, i), t, weights[:, :, i * HALF:(i + 1) * HALF])

            def gates(name, weights, first_bias, t):
                for i in range(2):
                    token_rows((name, t, i), t, weights[:, :, i * HALF:(i + 1) * HALF],
                               bias3[:, first_bias + i * HALF:first_bias + (i + 1) * HALF])

            def finish(t):
                at = slice(t * P, (t + 1) * P)
                bank = BK.claim(pe, ("y", t))[:, 0:H]
                for f in range(FFC):
                    mm(bank, big[:, f, at], w2t[:, f, :], f == 0, False)
                pe.wait_ge(o_ready, t + 1)
                for i in range(2):
                    turn(("oT", t, i), lambda c: o[:, (4 * i + c) * P:(4 * i + c + 1) * P], 4)
                BK.emptied(pe, ("oT", t, 1))
                for c in range(KC):
                    mm(bank, oT[:, c, :], wo[:, c, :], False, False)
                close(mm(bank, hzT[:, at], vbasis[:], False, True))

            pe.wait_ge(prep["dve"], 3)
            for c in range(HC):
                last = pe.transpose(ps[:, 0, c * P:(c + 1) * P], ubasis[:, c * P:(c + 1) * P], ident)
            last.then_inc(prep["pe"], 1)
            pe.wait_ge(prep["dve"], 4)
            pe.wait_ge(prep["pool"], 2)
            pe.wait_ge(opening["zn"], NT)
            with pe.Fori(0, B):
                for c in range(HC):
                    turn(("xT", c), lambda t: xn[:, t, c * P:(c + 1) * P], NT)
                for c in range(HC):
                    turn(("nT", c), lambda t: zn[:, t, c * P:(c + 1) * P], NT)
                BK.emptied(pe, ("xT", HC - 1))
                routing()
                columns("q", wq, xT, KC)
                small_products()
                columns("h", w1t, xT, FFC)
                pe.wait_ge(hz_ready, 1)
                turn(("hzT",), lambda t: rest[:, t, :], NT)
                keys_values(0)
                BK.emptied(pe, ("hzT",))
                for t in range(NT):
                    at = slice(t * P, (t + 1) * P)
                    BK.emptied(pe, ("k", t, 1))
                    for i in range(2):
                        turn(("kT", t, i), lambda c: k[:, t % 2, (4 * i + c) * P:(4 * i + c + 1) * P], 4)
                    BK.emptied(pe, ("kT", t, 1))
                    for j in range(LH // QUAD):
                        bank = BK.claim(pe, ("s", t, j))
                        for i, h in enumerate(score_quad(j)):
                            part = slice(h % 2 * LD, (h % 2 + 1) * LD)
                            last = mm(bank[:, i * P:(i + 1) * P], kT[part, h // 2, :], qT[part, h // 2, at],
                                      True, True)
                        close(last)
                    gates("f", wf, 0, t)
                    if t + 1 < NT:
                        keys_values(t + 1)
                    if t:
                        finish(t - 1)
                    pe.wait_ge(v_ready, t + 1)
                    BK.emptied(pe, ("s", t, LH // QUAD - 1))
                    if t:
                        pe.wait_ge(qd_ready, t)
                        BK.emptied(pe, ("u", t - 1, 1))
                    for i in range(2):
                        bank = BK.claim(pe, ("o", t, i))
                        part = slice(i * LD, (i + 1) * LD)
                        for j in range(LH // 2):
                            out, h = bank[:, j * LD:(j + 1) * LD], 2 * j + i
                            if t:
                                mm(out, qd[part, j, :], state[part, j, :], True, False)
                            last = mm(out, sm[:, h, :], v[:, t % 2, h * LD:(h + 1) * LD], t == 0, True)
                        close(last)
                    if t + 1 < NT:
                        pe.wait_ge(vt_ready, t + 1)
                        for i in range(2):
                            bank = BK.claim(pe, ("u", t, i))
                            for j in range(4):
                                pair = slice((4 * i + j) * P, (4 * i + j + 1) * P)
                                last = mm(bank[:, j * P:(j + 1) * P], k[:, t % 2, pair], vt[:, pair], True, True)
                            close(last)
                    gates("g", wg, KD, t)
                finish(NT - 1)
                end_of_turn(pe, arrived, go["pe"])

        @block.scalar
        def _(act):
            def run(out, src, func, **kw):
                return nc.scalar.activation(out, src, func, **kw)

            def take(dst, key, func, **kw):
                src = BK.filled(act, key)
                if len(dst.shape) == 3:
                    src = src[:, 0:dst.shape[1] * dst.shape[2]].rearrange("p (a b) -> p a b", a=dst.shape[1])
                run(dst, src, func, **kw).then_inc(BK.emptied_sem["act"], 1)

            def keys_values(t):
                if t >= 2:
                    BK.filled(act, ("u", t - 2, 1))
                for name, dst in (("k", k), ("v", v)):
                    for i in range(2):
                        take(dst[:, t % 2, i * HALF:(i + 1) * HALF], (name, t, i), ACT.Silu)

            def finish(t):
                if t:
                    BK.filled(act, ("y", t - 1))
                for i in range(2):
                    take(oT[:, 4 * i:4 * i + 4, :], ("oT", t, i), ACT.Copy)

            act.wait_ge(wload, LOADED)
            act.wait_ge(memset_done, 1)
            run(squares, ubasis[:], ACT.Square, accum_out=unit[:, 0:1]).then_inc(prep["act"], 1)
            act.wait_ge(prep["act"], 1)
            run(squares, vbasis[:], ACT.Square, accum_out=unit[:, 1:2]).then_inc(prep["act"], 1)
            run(rate[:], rate[:], ACT.Exp).then_inc(prep["act"], 1)
            act.wait_ge(prep["dve"], 1)
            for h in range(LH):
                run(decay_s[:, h, :], const("gap"), ACT.Exp, scale=rate[:, h:h + 1])
            for j in range(LH // 2):
                run(decay_q[:, j, :], const("steps"), ACT.Exp, scale=rate[:, LH + j:LH + j + 1])
            run(decay_k[:], rate[:, 0:LH], ACT.Exp, scale=const("tail"))
            run(decay_all[:], rate[:, LH:], ACT.Exp, scale=float(P)).then_inc(prep["act"], 1)
            act.wait_ge(prep["dve"], 4)
            act.wait_ge(prep["pool"], 2)
            with act.Fori(0, B):
                for c in range(HC):
                    take(xT[:, c, :], ("xT", c), ACT.Copy)
                for c in range(HC):
                    take(nT[:, c, :], ("nT", c), ACT.Identity, scale=col[:, c:c + 1], bias=col[:, HC + c:HC + c + 1])
                for f in range(KC):
                    take(qT[:, f, :], ("q", f), ACT.Silu)
                take(beta[:], ("beta",), ACT.Sigmoid)
                act.wait_ge(rc_ready, 1)
                run(alpha, r[:], ACT.Exp).then_inc(er_ready, 1)
                act.wait_ge(er_ready, 1)
                run(alpha, alpha, ACT.Ln, bias=one[:]).then_inc(alpha_ready, 1)
                act.wait_ge(mass_ready, 1)
                run(mass[:, 1, :], mass[:, 0, :], ACT.Tanh).then_inc(tanh_ready, 1)
                for f in range(FFC):
                    take(big[:, f, :], ("h", f), ACT.Gelu)
                take(hzT, ("hzT",), ACT.Copy)
                keys_values(0)
                for t in range(NT):
                    if t:
                        BK.filled(act, ("s", t - 1, LH // QUAD - 1))
                    for i in range(2):
                        take(kT[:, 4 * i:4 * i + 4, :], ("kT", t, i), ACT.Copy)
                    if t:
                        BK.emptied(act, ("o", t - 1, 1))
                    for i in range(2):
                        take(g[:, i * HALF:(i + 1) * HALF], ("f", t, i), ACT.Sigmoid)
                    if t + 1 < NT:
                        keys_values(t + 1)
                    if t:
                        finish(t - 1)
                    if t:
                        act.wait_ge(gated, t)
                    for i in range(2):
                        take(gate[:, i * HALF:(i + 1) * HALF], ("g", t, i), ACT.Sigmoid)
                finish(NT - 1)
                end_of_turn(act, arrived, go["act"])

        @block.vector
        def _(dve):
            chain = Chain(dve, dve_chain)

            def tt(out, a, b, op):
                return nc.vector.tensor_tensor(out, a, b, op)

            def by_head(ap):
                return ap.rearrange("p (h d) -> p h d", d=LD)

            def norm(src, dst, chain, var_ready, rstd_ready, count, signal):
                for t in range(NT):
                    last = nc.vector.bn_stats(stat[:, t, :], src[:, t, :])
                chain(last)
                for t in range(NT):
                    last = nc.vector.bn_aggr(mv[:, t, :], stat[:, t, :])
                chain(last)
                nc.vector.tensor_scalar(var[:], mv[:, :, 1], LN_EPS, None, ALU.add).then_inc(var_ready, 1)
                dve.wait_ge(rstd_ready, count)
                for t in range(NT):
                    nc.vector.tensor_scalar(dst[:, t, :], src[:, t, :], mv[:, t, 0:1], rstd[:, t:t + 1],
                                            ALU.subtract, ALU.mult).then_inc(signal, 1)

            def route():
                nc.vector.tensor_scalar(r[:], split3(BK.filled(dve, ("r",)), NT), -TAU, TAU, ALU.max, ALU.min)\
                    .then_inc(BK.emptied_sem["dve"], 1)
                BK.emptied(dve, ("r",))
                for t in range(NT):
                    last = nc.vector.max(top[:, t, :], r[:, t, :])
                last.then_inc(rc_ready, 1)
                dve.wait_ge(rc_ready, 1)
                for t in range(NT):
                    last = nc.vector.match_replace(rest[:, t, :], top[:, t, :], r[:, t, :], -1e30)
                chain(last)
                chain(tt(rest, r[:], rest, ALU.not_equal))
                dve.wait_ge(alpha_ready, 1)
                chain(tt(alpha, alpha, rest, ALU.mult))
                nc.vector.reduce_sum(mass[:, 0, :], alpha, AX).then_inc(mass_ready, 1)
                dve.wait_ge(mass_ready, 1)
                chain(nc.vector.tensor_scalar(mass[:, 2, :], mass[:, 0, :], UNIT_EPS, None, ALU.add))
                chain(nc.vector.reciprocal(mass[:, 3, :], mass[:, 2, :]))
                tt(rest, split3(BK.filled(dve, ("hl",)), NT), alpha, ALU.mult)\
                    .then_inc(BK.emptied_sem["dve"], 1)
                dve.wait_ge(tanh_ready, 1)
                chain(tt(mass[:, 3, :], mass[:, 3, :], mass[:, 1, :], ALU.mult))
                BK.emptied(dve, ("hl",))
                tt(rest, rest, spread(mass[:, 3, :], [P, NT, NB]), ALU.mult).then_inc(hz_ready, 1)

            def add_result(t):
                if t == 0:
                    dve.wait_ge(x_loaded, 16)
                tt(xi[:, t, :], xi[:, t, :], BK.filled(dve, ("y", t))[:, 0:H], ALU.add)\
                    .then_inc(BK.emptied_sem["dve"], 1)

            def output_sums(t):
                dve.wait_ge(osq_ready, t + 1)
                nc.vector.reduce_sum(on[:], by_head(sqs[:]), AX).then_inc(osum_ready, 1)

            def output_norm(t):
                dve.wait_ge(gated, t + 1)
                dve.wait_ge(on_ready, t + 1)
                tt(by_head(o[:]), by_head(o[:]), spread(on[:], [P, LH, LD]), ALU.mult).then_inc(o_ready, 1)

            dve.memset(one[:], 1.0)
            dve.memset(ones[:], 1.0)
            prepare = Chain(dve, setup_chain)
            prepare(dve.memset(bias3[:], 0.0))
            dve.memset(neghalf[:], -0.5).then_inc(memset_done, 1)
            dve.wait_ge(biases_loaded, 16 * len(bias_loads))
            prepare(nc.vector.tensor_scalar(rows[:, 0:KD], rows[:, 0:KD], -1.0, None, ALU.mult))
            for at in range(0, 2 * KD + NB, HALF):
                cut = slice(at, min(at + HALF, 2 * KD + NB))
                piece = rounded[:, 0:cut.stop - cut.start]
                for i in range(3):
                    prepare(nc.vector.tensor_copy(piece, rows[:, cut]))
                    prepare(nc.vector.tensor_copy(bias3[32 * i:32 * i + 1, cut], piece))
                    prepare(tt(rows[:, cut], rows[:, cut], piece, ALU.subtract))
            dve.wait_ge(opening["loaded"], 16)
            norm(xn, xn, prepare, opening["var"], opening["rstd"], 1, opening["xn"])
            dve.wait_ge(opening["xn"], NT)
            norm(xn, zn, prepare, opening["var"], opening["rstd"], 2, opening["zn"])
            dve.wait_ge(wload, LOADED)
            dve.wait_ge(prep["act"], 3)
            nc.vector.tensor_scalar(rate[:], rate[:], -1.0, -1e30, ALU.mult, ALU.max).then_inc(prep["dve"], 1)
            nc.vector.tensor_scalar(unit[:, 2:4], unit[:, 0:2], UNIT_EPS * UNIT_EPS, None, ALU.max)\
                .then_inc(prep["dve"], 1)
            nc.vector.tensor_scalar(wo[:], wo[:], col[:, 2 * HC:2 * HC + 1], None, ALU.mult)
            dve.wait_ge(prep["pool"], 1)
            nc.vector.scalar_tensor_tensor(out=vbasis[:], in0=vbasis[:], scalar=unit[:, 1:2], in1=gamma[:],
                                           op0=ALU.mult, op1=ALU.mult)
            nc.vector.tensor_scalar(ubasis[:], ubasis[:], unit[:, 0:1], None, ALU.mult).then_inc(prep["dve"], 1)
            dve.wait_ge(prep["pe"], 1)
            nc.vector.tensor_copy(uT[:], ps[:, 0, 0:HC * NB].rearrange("p (c n) -> p c n", c=HC))\
                .then_inc(prep["dve"], 1)
            dve.wait_ge(prep["dve"], 4)
            dve.wait_ge(prep["pool"], 2)
            with dve.Fori(0, B):
                chain.count = 0
                route()
                nc.vector.tensor_scalar(qnorm[:].rearrange("p t h -> p (t h)"), BK.filled(dve, ("nq",))[:, 0:NT * LH],
                                        1e-24, None, ALU.max).then_inc(BK.emptied_sem["dve"], 1)
                for t in range(NT):
                    if t:
                        output_sums(t - 1)
                    dve.wait_ge(ksq_ready, t + 1)
                    if t:
                        dve.wait_ge(vt_ready, t)
                    nc.vector.reduce_sum(kn[:], by_head(sqs[:]), AX).then_inc(ksum_ready, 1)
                    for j in range(LH // QUAD):
                        bank = split3(BK.filled(dve, ("s", t, j)), QUAD)
                        if t:
                            BK.filled(dve, ("o", t - 1, 1))
                        first, last = score_quad(j)[0], score_quad(j)[-1]
                        tt(sm[:, first:last + 1:2, :], bank, decay_s[:, first:last + 1:2, :], ALU.mult)\
                            .then_inc(BK.emptied_sem["dve"], 1)
                    if t:
                        output_norm(t - 1)
                    dve.wait_ge(kn_ready, t + 1)
                    BK.emptied(dve, ("v", t, 1))
                    rows_v = by_head(v[:, t % 2, :])
                    tt(rows_v, rows_v, spread(kn[:], [P, LH, LD]), ALU.mult).then_inc(v_ready, 1)
                    if t:
                        add_result(t - 1)
                        BK.filled(dve, ("oT", t - 1, 1))
                    dve.wait_ge(gq_ready, t + 1)
                    for i in range(2):
                        out = by_head(o[:])[:, i:LH:2, :]
                        tt(out, by_head(BK.filled(dve, ("o", t, i))), by_head(g[:])[:, i:LH:2, :], ALU.mult)\
                            .then_inc(BK.emptied_sem["dve"], 1)
                    if t + 1 < NT:
                        if t:
                            chain(tt(state[:], state[:], spread(decay_all[:], [P, LH // 2, LD]), ALU.mult))
                        for i in range(2):
                            bank = split3(BK.filled(dve, ("u", t, i)), 4)
                            for half in range(2):
                                part = slice(half * LD, (half + 1) * LD)
                                dst, src = state[part, 4 * i:4 * i + 4, :], bank[part, :, half * LD:(half + 1) * LD]
                                if t:
                                    ins = tt(dst, dst, src, ALU.add)
                                else:
                                    ins = nc.vector.tensor_copy(dst, src)
                            ins.then_inc(BK.emptied_sem["dve"], 1)
                output_sums(NT - 1)
                output_norm(NT - 1)
                dve.wait_ge(next_loaded, 16)
                norm(xn, xn, chain, var_ready, rstd_ready, 1, xn_ready)
                dve.wait_ge(xn_ready, NT)
                norm(xn, zn, chain, var_ready, rstd_ready, 2, zn_ready)
                add_result(NT - 1)
                end_of_turn(dve, arrived, go["dve"])

        @block.gpsimd
        def _(pool):
            steps = Chain(pool, pool_chain)

            def tt(out, a, b, op):
                return nc.gpsimd.tensor_tensor(out, a, b, op)

            def by_head(ap):
                return ap.rearrange("p (h d) -> p h d", d=LD)

            def inverse_roots(var_ready, rstd_ready, count):
                pool.wait_ge(var_ready, count)
                tt(rstd[:], var[:], neghalf[:, 0:NT], ALU.pow).then_inc(rstd_ready, 1)

            def output_squares(t):
                BK.emptied(pool, ("o", t, 1))
                tt(sqs[:], o[:], o[:], ALU.mult).then_inc(osq_ready, 1)

            def output_gates(t):
                pool.wait_ge(osq_ready, t + 1)
                BK.emptied(pool, ("g", t, 1))
                tt(o[:], o[:], gate[:], ALU.mult).then_inc(gated, 1)
                pool.wait_ge(osum_ready, t + 1)
                steps(nc.gpsimd.tensor_scalar(on[:], on[:], 1.0 / LD, 1e-5, ALU.mult, ALU.add))
                tt(on[:], on[:], neghalf[:, 0:LH], ALU.pow).then_inc(on_ready, 1)

            inverse_roots(opening["var"], opening["rstd"], 1)
            inverse_roots(opening["var"], opening["rstd"], 2)
            pool.wait_ge(prep["dve"], 2)
            tt(unit[:, 0:2], unit[:, 2:4], neghalf[:, 0:2], ALU.pow).then_inc(prep["pool"], 1)
            pool.wait_ge(prep["act"], 4)
            tt(decay_s[:], decay_s[:], const("after").unsqueeze(1).to_broadcast([P, LH, P]), ALU.mult)\
                .then_inc(prep["pool"], 1)
            pool.wait_ge(prep["pool"], 2)
            with pool.Fori(0, B):
                steps.count = 0
                for f in range(KC):
                    BK.emptied(pool, ("q", f))
                    tt(big[:, f, :], qT[:, f, :], qT[:, f, :], ALU.mult).then_inc(qsq_ready, 1)
                BK.emptied(pool, ("nq",))
                flat = qnorm[:].rearrange("p t h -> p (t h)")
                tt(flat, flat, neghalf[:], ALU.pow).then_inc(qnorm_ready, 1)
                pool.wait_ge(qnorm_ready, 1)
                for t in range(NT):
                    if t:
                        output_squares(t - 1)
                        output_gates(t - 1)
                    BK.emptied(pool, ("k", t, 1))
                    tt(sqs[:], k[:, t % 2, :], k[:, t % 2, :], ALU.mult).then_inc(ksq_ready, 1)
                    if t:
                        BK.filled(pool, ("o", t - 1, 1))
                        tt(qd[:], qT[:, :, t * P:(t + 1) * P], decay_q[:], ALU.mult).then_inc(qd_ready, 1)
                    pool.wait_ge(ksum_ready, t + 1)
                    steps(nc.gpsimd.tensor_scalar(kn[:], kn[:], 1e-24, None, ALU.max))
                    steps(tt(kn[:], kn[:], neghalf[:, 0:LH], ALU.pow))
                    tt(kn[:], kn[:], beta[:, t, :], ALU.mult).then_inc(kn_ready, 1)
                    BK.emptied(pool, ("f", t, 1))
                    tt(by_head(g[:]), by_head(g[:]), spread(qnorm[:, t, :], [P, LH, LD]), ALU.mult)\
                        .then_inc(gq_ready, 1)
                    if t + 1 < NT:
                        pool.wait_ge(v_ready, t + 1)
                        if t:
                            BK.filled(pool, ("u", t - 1, 1))
                        tt(by_head(vt[:]), by_head(v[:, t % 2, :]), spread(decay_k[:], [P, LH, LD]), ALU.mult)\
                            .then_inc(vt_ready, 1)
                output_squares(NT - 1)
                output_gates(NT - 1)
                inverse_roots(var_ready, rstd_ready, 1)
                inverse_roots(var_ready, rstd_ready, 2)
                end_of_turn(pool, arrived, go["pool"])


def kernel(**inputs):
    import concourse.bacc as bacc
    from concourse.bass_utils import run_bass_kernel_spmd

    nc = bacc.Bacc("TRN2", target_bir_lowering=False, num_devices=1)
    arrays, aps = {}, {}

    def given(name, value):
        a = np.ascontiguousarray(value)
        arrays[f"in_{name}"] = a
        aps[name] = nc.dram_tensor(f"in_{name}", a.shape, mybir.dt.from_np(a.dtype), kind="ExternalInput").ap()

    turned = {"L1_ffn_W1": "W1_turned", "L1_ffn_W2": "W2_turned", "L1_ffn_router_W": "router_turned"}
    for name, value in inputs.items():
        if name in turned:
            given(turned[name], np.asarray(value).T)
        else:
            given(name, value)
    given("shape_constants", shape_constants())
    mid = nc.dram_tensor("mid", (B, L, H), F32, kind="Internal").ap()
    result = nc.dram_tensor("result", (B, L, H), F32, kind="ExternalOutput").ap()
    stage_one(nc, aps, mid, aps["shape_constants"])
    stage_two(nc, aps, mid, result, aps["shape_constants"])
    r = run_bass_kernel_spmd(nc, [arrays], core_ids=[0])
    return r.results[0]["result"]
```
